# Optimizing a Trainium2 kernel written in Bass

```python
import numpy as np
import jax
import jax.numpy as jnp

def _softmax(x, axis=-1):
    return jax.nn.softmax(x, axis=axis)

def _gelu(x):
    return jax.nn.gelu(x, approximate=True)

def _silu(x):
    return jax.nn.silu(x)

def _sigmoid(x):
    return jax.nn.sigmoid(x)

def _layernorm(x, axis=-1, eps=1e-05):
    m = jnp.mean(x, axis=axis, keepdims=True)
    v = jnp.var(x, axis=axis, keepdims=True)
    return (x - m) / jnp.sqrt(v + eps)

def _scatter_add(tgt, idx, src, axis=0):
    return tgt.at[idx].add(src)

def _segment_sum(src, seg, n):
    return jax.ops.segment_sum(src, seg, n)
kernel_name = 'mk_decoder_postln_d2_seqx_r8_043811'

def setup_inputs(seed: int=0):
    np.random.seed(seed)
    _w = jnp.asarray

    def _rec_inputs():
        import jax
        import jax.numpy as jnp
        _rk = jax.random.key(seed)
        x = 0.0001212 + 1 * jax.random.normal(jax.random.fold_in(_rk, 1), (8, 128, 512), jnp.float32)
        _lenS = 128 - jax.random.randint(jax.random.fold_in(_rk, 7), (8,), 0, max(1, 128 // 4) + 1, jnp.int32)
        _lenS2 = 128 - jax.random.randint(jax.random.fold_in(_rk, 8), (8,), 0, max(1, 128 // 4) + 1, jnp.int32)
        _ctx_4096P = jax.random.normal(jax.random.fold_in(_rk, 11), (8, 16, 512), jnp.float32)
        _ctx_4096c = jax.random.dirichlet(jax.random.fold_in(_rk, 511), 0.3 * jnp.ones((16,), jnp.float32), (8, 128))
        _ctx_4096t = jnp.einsum('bsk,bkd->bsd', _ctx_4096c, _ctx_4096P)
        _ctx_4096t = _ctx_4096t * jax.lax.rsqrt(jnp.mean(jnp.square(_ctx_4096t)) + 1e-12) * 0.953939
        ctx_4096 = -0.000125008 + 0.999885 * (_ctx_4096t + 0.3 * jax.random.normal(jax.random.fold_in(_rk, 611), (8, 128, 512), jnp.float32))
        return (x, ctx_4096)
    x, ctx_4096 = _rec_inputs()

    def _L0_attn_setup():
        import jax, jax.numpy as jnp
        import numpy as np
        B, N, D = (8, 128, 512)
        H = 8
        HEAD_DIM = D // H
        E = HEAD_DIM // H
        key = jax.random.key(seed)
        ks = jax.random.split(key, 7)
        s = 0.02
        return {'x': jax.random.normal(ks[0], (B, N, D), dtype=jnp.float32), 'Wqk_w': jax.random.normal(ks[1], (2 * HEAD_DIM, D), dtype=jnp.float32) * s, 'Wqk_b': jnp.zeros((2 * HEAD_DIM,), dtype=jnp.float32), 'Wv_w': jax.random.normal(ks[2], (HEAD_DIM, D), dtype=jnp.float32) * s, 'Wv_b': jnp.zeros((HEAD_DIM,), dtype=jnp.float32), 'Wo_w': jax.random.normal(ks[3], (D, HEAD_DIM), dtype=jnp.float32) * s, 'Wo_b': jnp.zeros((D,), dtype=jnp.float32)}
    _L0_attn_all = _L0_attn_setup()
    _L0_attn_in = {k: v for k, v in _L0_attn_all.items() if k in ('Wqk_w', 'Wqk_b', 'Wv_w', 'Wv_b', 'Wo_w', 'Wo_b')}
    del _L0_attn_all

    def _L0_xattn_setup():
        import jax, jax.numpy as jnp
        import numpy as np
        N, C, S = (16, 64, 512)
        rng = jax.random.key(seed)
        k1, k2, k3 = jax.random.split(rng, 3)
        return {'key': jax.random.normal(k1, (N, C, S), dtype=jnp.float32), 'value': jax.random.normal(k2, (N, C, S), dtype=jnp.float32), 'query': jax.random.normal(k3, (N, C, S), dtype=jnp.float32)}
    _L0_xattn_all = _L0_xattn_setup()
    _L0_xattn_in = {k: v for k, v in _L0_xattn_all.items() if k in ()}
    del _L0_xattn_all

    def _L0_ffn_setup():
        import jax, jax.numpy as jnp
        import numpy as np
        RANKS = (8, 16, 32, 64)
        TOPK = 1
        SCALING = 1.0 / 4
        key = jax.random.key(seed)
        ks = jax.random.split(key, 7)
        D_IN, D_OUT, MAX_R, N_RANKS = (512, 512, 64, len(RANKS))
        B_, S_ = (4, 256)
        return {'hidden_states': jax.random.normal(ks[0], (B_, S_, D_IN), jnp.float32), 'W': jax.random.normal(ks[1], (D_OUT, D_IN), jnp.float32) * 0.02, 'b': jax.random.normal(ks[2], (D_OUT,), jnp.float32) * 0.02, 'A': jax.random.normal(ks[3], (MAX_R, D_IN), jnp.float32) * 0.02, 'B': jnp.zeros((D_OUT, MAX_R), jnp.float32) + jax.random.normal(ks[4], (D_OUT, MAX_R), jnp.float32) * 0.02, 'gate_w': jax.random.normal(ks[5], (N_RANKS, D_IN), jnp.float32) * 0.02, 'gate_b': jax.random.normal(ks[6], (N_RANKS,), jnp.float32) * 0.02}
    _L0_ffn_all = _L0_ffn_setup()
    _L0_ffn_in = {k: v for k, v in _L0_ffn_all.items() if k in ('W', 'b', 'A', 'B', 'gate_w', 'gate_b')}
    del _L0_ffn_all

    def _L1_attn_setup():
        import jax, jax.numpy as jnp
        import numpy as np
        NF4 = jnp.array([-1.0, -0.6961928009986877, -0.5250730514526367, -0.39491748809814453, -0.28444138169288635, -0.18477343022823334, -0.09105003625154495, 0.0, 0.07958029955625534, 0.16093020141124725, 0.24611230194568634, 0.33791524171829224, 0.44070982933044434, 0.5626170039176941, 0.7229568362236023, 1.0], dtype=jnp.float32)
        BLOCK = 64

        def _dequant(codes, scales):
            w = NF4[codes]
            O, I = w.shape
            w = w.reshape(O, I // BLOCK, BLOCK) * scales[:, :, None]
            return w.reshape(O, I)

        def _lin_lora(x, W, A, B):
            base = jnp.einsum('bsh,oh->bso', x, W)
            lora = jnp.einsum('bsr,or->bso', jnp.einsum('bsh,rh->bsr', x, A), B)
            return base + lora
        H, I, R, BT, S = (512, 1792, 16, 2, 256)
        key = jax.random.key(seed)
        ks = jax.random.split(key, 12)
        x = jax.random.normal(ks[0], (BT, S, H), jnp.float32)
        codes_attn = jax.random.randint(ks[1], (4, H, H), 0, 16, jnp.int32)
        scales_attn = jax.random.uniform(ks[2], (4, H, H // BLOCK), jnp.float32) * 0.02
        codes_gu = jax.random.randint(ks[3], (2, I, H), 0, 16, jnp.int32)
        scales_gu = jax.random.uniform(ks[4], (2, I, H // BLOCK), jnp.float32) * 0.02
        codes_down = jax.random.randint(ks[5], (H, I), 0, 16, jnp.int32)
        scales_down = jax.random.uniform(ks[6], (H, I // BLOCK), jnp.float32) * 0.02
        lora_A_h = jax.random.normal(ks[7], (6, R, H), jnp.float32) * 0.02
        lora_A_down = jax.random.normal(ks[8], (R, I), jnp.float32) * 0.02
        lora_B_attn = jax.random.normal(ks[9], (4, H, R), jnp.float32) * 0.02
        lora_B_gu = jax.random.normal(ks[10], (2, I, R), jnp.float32) * 0.02
        lora_B_down = jax.random.normal(ks[11], (H, R), jnp.float32) * 0.02
        return dict(x=x, codes_attn=codes_attn, scales_attn=scales_attn, codes_gu=codes_gu, scales_gu=scales_gu, codes_down=codes_down, scales_down=scales_down, lora_A_h=lora_A_h, lora_A_down=lora_A_down, lora_B_attn=lora_B_attn, lora_B_gu=lora_B_gu, lora_B_down=lora_B_down)
    _L1_attn_all = _L1_attn_setup()
    _L1_attn_in = {k: v for k, v in _L1_attn_all.items() if k in ('codes_attn', 'scales_attn', 'codes_gu', 'scales_gu', 'codes_down', 'scales_down', 'lora_A_h', 'lora_A_down', 'lora_B_attn', 'lora_B_gu', 'lora_B_down')}
    del _L1_attn_all

    def _L1_xattn_setup():
        import jax, jax.numpy as jnp
        import numpy as np
        TEXT_DIM = 512
        FEATURE_DIM = 512

        def _xavier_uniform(key, shape):
            fan_in, fan_out = (shape[1], shape[0])
            limit = float(np.sqrt(6.0 / (fan_in + fan_out)))
            return jax.random.uniform(key, shape, jnp.float32, -limit, limit)
        key = jax.random.key(seed)
        k1, k2, k3, k4 = jax.random.split(key, 4)
        text = jax.random.normal(k1, (8, 256, TEXT_DIM), jnp.float32)
        features = jax.random.normal(k2, (8, 72, FEATURE_DIM), jnp.float32)
        Wq = _xavier_uniform(k3, (FEATURE_DIM, TEXT_DIM))
        bq = jnp.zeros((FEATURE_DIM,), jnp.float32)
        Wk = _xavier_uniform(k4, (FEATURE_DIM, FEATURE_DIM))
        bk = jnp.zeros((FEATURE_DIM,), jnp.float32)
        return {'text': text, 'features': features, 'Wq': Wq, 'bq': bq, 'Wk': Wk, 'bk': bk}
    _L1_xattn_all = _L1_xattn_setup()
    _L1_xattn_in = {k: v for k, v in _L1_xattn_all.items() if k in ('Wq', 'bq', 'Wk', 'bk')}
    del _L1_xattn_all

    def _L1_ffn_setup():
        import jax, jax.numpy as jnp
        import numpy as np
        H, FF = (512, 1792)
        B, S = (4, 256)
        key = jax.random.key(seed)
        ks = jax.random.split(key, 7)
        x = jax.random.normal(ks[0], (B, S, H), dtype=jnp.float32)
        gate_t = jax.random.randint(ks[1], (FF, H), -1, 2, dtype=jnp.int32)
        up_t = jax.random.randint(ks[2], (FF, H), -1, 2, dtype=jnp.int32)
        down_t = jax.random.randint(ks[3], (H, FF), -1, 2, dtype=jnp.int32)
        gate_s = jax.random.uniform(ks[4], (FF,), jnp.float32, 0.01, 0.1)
        up_s = jax.random.uniform(ks[5], (FF,), jnp.float32, 0.01, 0.1)
        down_s = jax.random.uniform(ks[6], (H,), jnp.float32, 0.01, 0.1)
        return {'x': x, 'gate_t': gate_t, 'up_t': up_t, 'down_t': down_t, 'gate_s': gate_s, 'up_s': up_s, 'down_s': down_s}
    _L1_ffn_all = _L1_ffn_setup()
    _L1_ffn_in = {k: v for k, v in _L1_ffn_all.items() if k in ('gate_t', 'up_t', 'down_t', 'gate_s', 'up_s', 'down_s')}
    del _L1_ffn_all
    return {'x': x, 'ctx_4096': ctx_4096, 'L0_attn_Wqk_w': _L0_attn_in['Wqk_w'], 'L0_attn_Wqk_b': _L0_attn_in['Wqk_b'], 'L0_attn_Wv_w': _L0_attn_in['Wv_w'], 'L0_attn_Wv_b': _L0_attn_in['Wv_b'], 'L0_attn_Wo_w': _L0_attn_in['Wo_w'], 'L0_attn_Wo_b': _L0_attn_in['Wo_b'], 'L0_ffn_W': _L0_ffn_in['W'], 'L0_ffn_b': _L0_ffn_in['b'], 'L0_ffn_A': _L0_ffn_in['A'], 'L0_ffn_B': _L0_ffn_in['B'], 'L0_ffn_gate_w': _L0_ffn_in['gate_w'], 'L0_ffn_gate_b': _L0_ffn_in['gate_b'], 'L1_attn_codes_attn': _L1_attn_in['codes_attn'], 'L1_attn_scales_attn': _L1_attn_in['scales_attn'], 'L1_attn_codes_gu': _L1_attn_in['codes_gu'], 'L1_attn_scales_gu': _L1_attn_in['scales_gu'], 'L1_attn_codes_down': _L1_attn_in['codes_down'], 'L1_attn_scales_down': _L1_attn_in['scales_down'], 'L1_attn_lora_A_h': _L1_attn_in['lora_A_h'], 'L1_attn_lora_A_down': _L1_attn_in['lora_A_down'], 'L1_attn_lora_B_attn': _L1_attn_in['lora_B_attn'], 'L1_attn_lora_B_gu': _L1_attn_in['lora_B_gu'], 'L1_attn_lora_B_down': _L1_attn_in['lora_B_down'], 'L1_xattn_Wq': _L1_xattn_in['Wq'], 'L1_xattn_bq': _L1_xattn_in['bq'], 'L1_xattn_Wk': _L1_xattn_in['Wk'], 'L1_xattn_bk': _L1_xattn_in['bk'], 'L1_ffn_gate_t': _L1_ffn_in['gate_t'], 'L1_ffn_up_t': _L1_ffn_in['up_t'], 'L1_ffn_down_t': _L1_ffn_in['down_t'], 'L1_ffn_gate_s': _L1_ffn_in['gate_s'], 'L1_ffn_up_s': _L1_ffn_in['up_s'], 'L1_ffn_down_s': _L1_ffn_in['down_s']}

def reference(x, ctx_4096, L0_attn_Wqk_w, L0_attn_Wqk_b, L0_attn_Wv_w, L0_attn_Wv_b, L0_attn_Wo_w, L0_attn_Wo_b, L0_ffn_W, L0_ffn_b, L0_ffn_A, L0_ffn_B, L0_ffn_gate_w, L0_ffn_gate_b, L1_attn_codes_attn, L1_attn_scales_attn, L1_attn_codes_gu, L1_attn_scales_gu, L1_attn_codes_down, L1_attn_scales_down, L1_attn_lora_A_h, L1_attn_lora_A_down, L1_attn_lora_B_attn, L1_attn_lora_B_gu, L1_attn_lora_B_down, L1_xattn_Wq, L1_xattn_bq, L1_xattn_Wk, L1_xattn_bk, L1_ffn_gate_t, L1_ffn_up_t, L1_ffn_down_t, L1_ffn_gate_s, L1_ffn_up_s, L1_ffn_down_s):
    import jax
    import jax.numpy as jnp

    def _L0_attn_ref(x, Wqk_w, Wqk_b, Wv_w, Wv_b, Wo_w, Wo_b):
        import jax, jax.numpy as jnp
        import numpy as np
        B, N, D = (8, 128, 512)
        H = 8
        HEAD_DIM = D // H
        E = HEAD_DIM // H
        b, n, _ = x.shape
        qk = (x @ Wqk_w.T + Wqk_b).reshape(b, n, H, E, 2)
        q = jnp.transpose(qk[..., 0], (0, 2, 1, 3))
        k = jnp.transpose(qk[..., 1], (0, 2, 1, 3))
        v = (x @ Wv_w.T + Wv_b).reshape(b, n, H, E)
        v = jnp.transpose(v, (0, 2, 1, 3))
        scores = jnp.einsum('bhqd,bhkd->bhqk', q, k)
        attn = jax.nn.softmax(scores, axis=-1) / jnp.asarray(HEAD_DIM ** 0.5, x.dtype)
        out = jnp.einsum('bhsl,bhlv->bhsv', attn, v)
        out = jnp.transpose(out, (0, 2, 1, 3)).reshape(b, n, H * E)
        return out @ Wo_w.T + Wo_b

    def _L0_xattn_ref(key, value, query):
        import jax, jax.numpy as jnp
        import numpy as np
        N, C, S = (16, 64, 512)
        KC = key.shape[1]
        sim = jnp.einsum('ncs,nds->ncd', key, query) * KC ** (-0.5)
        sim = jax.nn.softmax(sim, axis=1)
        context = jnp.einsum('ncd,nds->ncs', sim, value)
        return context

    def _L0_ffn_ref(hidden_states, W, b, A, B, gate_w, gate_b):
        import jax, jax.numpy as jnp
        import numpy as np
        RANKS = (8, 16, 32, 64)
        TOPK = 1
        SCALING = 1.0 / 4
        bsz, seq, d_in = hidden_states.shape
        out = jnp.einsum('bsd,od->bso', hidden_states, W) + b
        x = hidden_states.reshape(-1, d_in)
        scores = x @ gate_w.T + gate_b
        probs = jax.nn.softmax(scores, axis=-1)
        routing_weights, selected = jax.lax.top_k(probs, TOPK)
        routing_weights = routing_weights / jnp.sum(routing_weights, axis=-1, keepdims=True)
        lora_outputs = jnp.stack([x @ A[:r, :].T @ B[:, :r].T for r in RANKS], axis=1)
        sel = jnp.take_along_axis(lora_outputs, selected[:, :, None], axis=1)
        final = jnp.sum(sel * routing_weights[:, :, None], axis=1)
        return out + final.reshape(bsz, seq, -1)

    def _L1_attn_ref(x, codes_attn, scales_attn, codes_gu, scales_gu, codes_down, scales_down, lora_A_h, lora_A_down, lora_B_attn, lora_B_gu, lora_B_down):
        import jax, jax.numpy as jnp
        import numpy as np
        NF4 = jnp.array([-1.0, -0.6961928009986877, -0.5250730514526367, -0.39491748809814453, -0.28444138169288635, -0.18477343022823334, -0.09105003625154495, 0.0, 0.07958029955625534, 0.16093020141124725, 0.24611230194568634, 0.33791524171829224, 0.44070982933044434, 0.5626170039176941, 0.7229568362236023, 1.0], dtype=jnp.float32)
        BLOCK = 64

        def _dequant(codes, scales):
            w = NF4[codes]
            O, I = w.shape
            w = w.reshape(O, I // BLOCK, BLOCK) * scales[:, :, None]
            return w.reshape(O, I)

        def _lin_lora(x, W, A, B):
            base = jnp.einsum('bsh,oh->bso', x, W)
            lora = jnp.einsum('bsr,or->bso', jnp.einsum('bsh,rh->bsr', x, A), B)
            return base + lora
        q = _lin_lora(x, _dequant(codes_attn[0], scales_attn[0]), lora_A_h[0], lora_B_attn[0])
        k = _lin_lora(x, _dequant(codes_attn[1], scales_attn[1]), lora_A_h[1], lora_B_attn[1])
        v = _lin_lora(x, _dequant(codes_attn[2], scales_attn[2]), lora_A_h[2], lora_B_attn[2])
        attn = (q + k + v) / 3.0
        o = _lin_lora(attn, _dequant(codes_attn[3], scales_attn[3]), lora_A_h[3], lora_B_attn[3])
        x1 = x + o
        g = _lin_lora(x1, _dequant(codes_gu[0], scales_gu[0]), lora_A_h[4], lora_B_gu[0])
        u = _lin_lora(x1, _dequant(codes_gu[1], scales_gu[1]), lora_A_h[5], lora_B_gu[1])
        h = jax.nn.silu(g) * u
        d = _lin_lora(h, _dequant(codes_down, scales_down), lora_A_down, lora_B_down)
        return x1 + d

    def _L1_xattn_ref(text, features, Wq, bq, Wk, bk):
        import jax, jax.numpy as jnp
        import numpy as np
        TEXT_DIM = 512
        FEATURE_DIM = 512

        def _xavier_uniform(key, shape):
            fan_in, fan_out = (shape[1], shape[0])
            limit = float(np.sqrt(6.0 / (fan_in + fan_out)))
            return jax.random.uniform(key, shape, jnp.float32, -limit, limit)
        Q = jnp.einsum('btx,dx->btd', text, Wq) + bq
        K = jnp.einsum('bpx,dx->bpd', features, Wk) + bk
        scale = 1.0 / jnp.sqrt(jnp.asarray(K.shape[-1], K.dtype))
        scores = jnp.einsum('btd,bpd->btp', Q, K) * scale
        attn = jax.nn.softmax(scores, axis=-1)
        attended = jnp.einsum('btp,bpd->btd', attn, features)
        return attended

    def _L1_ffn_ref(x, gate_t, up_t, down_t, gate_s, up_s, down_s):
        import jax, jax.numpy as jnp
        import numpy as np
        H, FF = (512, 1792)
        B, S = (4, 256)
        Bb, Ss, Hh = x.shape
        x_flat = x.reshape(Bb * Ss, Hh)
        gate_w = gate_t.astype(jnp.float32) * gate_s[:, None]
        up_w = up_t.astype(jnp.float32) * up_s[:, None]
        down_w = down_t.astype(jnp.float32) * down_s[:, None]
        gate_out = x_flat @ gate_w.T
        up_out = x_flat @ up_w.T
        hidden = jax.nn.silu(gate_out) * up_out
        out_flat = hidden @ down_w.T
        return out_flat.reshape(Bb, Ss, -1)
    x = _layernorm(x + _L0_attn_ref(x, L0_attn_Wqk_w, L0_attn_Wqk_b, L0_attn_Wv_w, L0_attn_Wv_b, L0_attn_Wo_w, L0_attn_Wo_b), axis=-1)
    x = _layernorm(x + _L0_xattn_ref(ctx_4096, ctx_4096, x), axis=-1)
    x = _layernorm(x + _L0_ffn_ref(x, L0_ffn_W, L0_ffn_b, L0_ffn_A, L0_ffn_B, L0_ffn_gate_w, L0_ffn_gate_b), axis=-1)
    x = _layernorm(x + _L1_attn_ref(x, L1_attn_codes_attn, L1_attn_scales_attn, L1_attn_codes_gu, L1_attn_scales_gu, L1_attn_codes_down, L1_attn_scales_down, L1_attn_lora_A_h, L1_attn_lora_A_down, L1_attn_lora_B_attn, L1_attn_lora_B_gu, L1_attn_lora_B_down), axis=-1)
    x = _layernorm(x + _L1_xattn_ref(x, ctx_4096, L1_xattn_Wq, L1_xattn_bq, L1_xattn_Wk, L1_xattn_bk), axis=-1)
    x = _layernorm(x + _L1_ffn_ref(x, L1_ffn_gate_t, L1_ffn_up_t, L1_ffn_down_t, L1_ffn_gate_s, L1_ffn_up_s, L1_ffn_down_s), axis=-1)
    return x

_drawn_inputs = setup_inputs


def setup_inputs(seed=0):
    import zlib

    import numpy as np

    out = dict(_drawn_inputs(seed))
    spreads = {'L0_attn_Wqk_b': (0.0, 0.8),
     'L0_attn_Wv_b': (0.0, 0.8),
     'L0_attn_Wo_b': (0.0, 0.1),
     'L1_xattn_bq': (0.0, 0.335),
     'L1_xattn_bk': (0.0, 0.8)}
    factors = {'L0_attn_Wqk_w': 8.0,
     'L0_attn_Wv_w': 8.0,
     'L0_attn_Wo_w': 8.0,
     'L0_ffn_b': 2.944,
     'L0_ffn_gate_b': 8.0,
     'L1_attn_scales_attn': 8.0,
     'L1_attn_scales_gu': 8.0,
     'L1_attn_scales_down': 8.0,
     'L1_attn_lora_A_h': 8.0,
     'L1_attn_lora_A_down': 8.0,
     'L1_attn_lora_B_attn': 8.0,
     'L1_attn_lora_B_gu': 8.0,
     'L1_attn_lora_B_down': 8.0}
    for name, (base, spread) in spreads.items():
        noise = np.random.default_rng([zlib.crc32(name.encode()), seed]).standard_normal(out[name].shape)
        drawn = base * np.exp(spread * noise) if base else spread * noise
        out[name] = jnp.asarray(drawn.astype(out[name].dtype))
    for name, factor in factors.items():
        out[name] = (out[name] * factor).astype(out[name].dtype)
    return out
```

```python
from contextlib import ExitStack

import numpy as np
import concourse.bass as bass
from concourse import mybir

F32 = mybir.dt.float32
I32 = mybir.dt.int32
ALU = mybir.AluOpType
ACT = mybir.ActivationFunctionType
AX = mybir.AxisListType

P = 128
NT = 8
T = NT * P
D = 512
KD = D // P
FF = 1792
NF = FF // P
HEADS, HD = 8, 8
NQ = 4
QR = P // NQ
RANKS = (8, 16, 32, 64)
RMAX = RANKS[-1]
NR = len(RANKS)
R1 = 16
BLOCK = 64
NB = D // BLOCK
CH = 1024
TG = T // 512
LN_EPS = 1e-5

NF4 = np.array([-1.0, -0.6961928009986877, -0.5250730514526367, -0.39491748809814453,
                -0.28444138169288635, -0.18477343022823334, -0.09105003625154495, 0.0,
                0.07958029955625534, 0.16093020141124725, 0.24611230194568634, 0.33791524171829224,
                0.44070982933044434, 0.5626170039176941, 0.7229568362236023, 1.0], np.float32)


def _lines():
    def near(v, n):
        out, up, down = [v], v, v
        for _ in range(n):
            up, down = np.nextafter(up, np.float32(np.inf)), np.nextafter(down, np.float32(-np.inf))
            out += [up, down]
        return out

    lines = []
    for pair in range(len(NF4) // 2):
        lo, hi = 2 * pair, 2 * pair + 1
        y = {lo: float(NF4[lo]), hi: float(NF4[hi])}
        slope = np.float32(y[hi] - y[lo])
        offset = np.float32(y[lo] - lo * float(slope))
        best = None
        for a in near(slope, 12):
            for b in near(offset, 6):
                worst = 0.0
                for c in (lo, hi):
                    fused = np.float32(float(a) * c + float(b))
                    twice = np.float32(np.float32(a * np.float32(c)) + b)
                    worst = max([worst] + [abs(float(v) - y[c]) / max(abs(y[c]), 0.05) for v in (fused, twice)])
                if best is None or worst < best[0]:
                    best = (worst, float(a), float(b))
        lines.append(best[1:])
    return lines


LINES = _lines()
NEG, POS = (0, 1, 2, 3), (4, 5, 6, 7)
DQ = 7

C_QKV, C_O, C_GU, C_DN = 0, 6, 8, 8 + NF
C_END = C_DN + NF


def decoder_kernel(nc, i, out):
    ctx = ExitStack()
    with ctx:
        def sb(name, shape, dt=F32):
            return ctx.enter_context(nc.sbuf_tensor(name, shape, dt))

        def sem(name):
            return ctx.enter_context(nc.semaphore(name))

        x = sb("x", [P, NT, D])
        xT = sb("xT", [P, KD, T])
        line = sb("line", [P, 8, CH])
        codes = sb("codes", [P, 2, CH], I32)
        scales = sb("scales", [P, 2, CH])
        w = sb("w", [P, 2, CH])
        b_gu = sb("b_gu", [R1, 2, 2, P])
        ff_s = sb("ff_s", [P, 2, 2])
        h_use = sb("h_use", [P, 2, T])
        sil = sb("sil", [P, TG, 512])
        arena = sb("arena", [P, NF * T])
        fold = sb("fold", [P, NF, D])
        rbuf = sb("rbuf", [P, 2, D])
        ident = sb("ident", [P, P])
        st = sb("st", [P, 2, 6])
        mv = sb("mv", [P, 2, 2])
        rstd = sb("rstd", [P, 2, 2])
        minus_half = sb("minus_half", [P, 1])
        small = sb("small", [P, 2, 32])
        gate_v = sb("gate_v", [P, 2, 16])
        lm = sb("lm", [P, 2, RMAX])
        lmT = sb("lmT", [RMAX + 1, 2, P])
        prob = sb("prob", [P, 2, P])
        probT = sb("probT", [P, 2, P])
        s_qkv = sb("s_qkv", [P, 3 * KD * NB])
        qk_b = sb("qk_b", [P, 4])
        v_b = sb("v_b", [P, HEADS * HD])
        g_b = sb("g_b", [P, NR])
        q_b = sb("q_b", [P, KD])
        k_b = sb("k_b", [P, KD])
        a_g = sb("a_g", [R1, D])
        a_u = sb("a_u", [R1, D])
        bT_d = sb("bT_d", [R1, D])
        ds = sb("ds", [P, D])

        hT = arena[:, :].rearrange("p (f t) -> p f t", f=NF)
        at = [0]

        def early(n):
            at[0] += n
            return arena[:, at[0] - n:at[0]]

        wsum = early(KD * D).rearrange("p (j c) -> p j c", j=KD)
        woT = early(KD * D).rearrange("p (j c) -> p j c", j=KD)
        mT = early(KD * D).rearrange("p (j c) -> p j c", j=KD)
        wqkT = early(KD * 4 * P).rearrange("p (j c) -> p j c", j=KD)
        wvT = early(KD * 64).rearrange("p (j c) -> p j c", j=KD)
        wo0 = early(D)
        w0T = early(KD * D).rearrange("p (j c) -> p j c", j=KD)
        agT = early(KD * (RMAX + NR)).rearrange("p (j c) -> p j c", j=KD)
        bT0 = early(D)
        ctx_r = early(2 * D).rearrange("p (s c) -> p s c", s=2)
        ctxT_r = early(2 * D).rearrange("p (s j c) -> p s j c", s=2, j=KD)
        assert at[0] <= NF * T
        at[0] = 0
        ctx1 = early(NT * D).rearrange("p (b c) -> p b c", b=NT)
        ctxT1 = early(KD * T).rearrange("p (j t) -> p j t", j=KD)
        wqT1 = early(KD * D).rearrange("p (j c) -> p j c", j=KD)
        wkT1 = early(KD * D).rearrange("p (j c) -> p j c", j=KD)
        lines_flat = line[:, :, :].rearrange("p l c -> p (l c)")
        qT1 = lines_flat[:, 0:KD * T].rearrange("p (j t) -> p j t", j=KD)
        kT1 = lines_flat[:, KD * T:2 * KD * T].rearrange("p (j t) -> p j t", j=KD)
        fold_flat = fold[:, :, :].rearrange("p f c -> p (f c)")
        at[0] = 0

        def heads(n):
            at[0] += n
            return fold_flat[:, at[0] - n:at[0]]

        qk = heads(2 * 4 * P).rearrange("p (s c t) -> p s c t", s=2, c=4)
        q_aug = heads(2 * P).rearrange("p (a t) -> p a t", a=2)
        mz = heads(2 * P).rearrange("p (a c) -> p a c", a=2)
        pT = heads(2 * CH).rearrange("p (s j a t) -> p s j a t", s=2, j=NQ, a=2)
        v1 = heads(2 * HEADS * (HD + 1)).rearrange("p (s h e) -> p s h e", s=2, h=HEADS)
        att = heads(2 * 64).rearrange("p (s c) -> p s c", s=2)
        attT = heads(2 * P).rearrange("p (s t) -> p s t", s=2)
        aT_3 = heads(D)
        bT_3 = heads(D)
        aT_o = heads(D)
        bT_o = heads(D)
        assert at[0] <= NF * D
        a_d = h_use[:, :, :].rearrange("p s t -> p (s t)")[0:R1, 0:FF]

        bank = [ctx.enter_context(nc.psum_tensor(f"bank{n}", [P, 512], F32)) for n in range(2)]
        heads_ps = ctx.enter_context(nc.psum_tensor("bank2345", [P, 4, 512], F32))
        bank += [heads_ps[:, n, :] for n in range(4)]
        bank += [ctx.enter_context(nc.psum_tensor(f"bank{n}", [P, 512], F32)) for n in (6, 7)]
        gu_fold = heads_ps[:, 2:4, :].rearrange("p b c -> p (b c)")

        in_x = [sem(f"in_x{n}") for n in range(4)]
        in_qk, in_v, in_bias, in_xn, in_wo0 = sem("in_qk"), sem("in_v"), sem("in_bias"), sem("in_xn"), sem("in_wo0")
        in_ffn0, in_lora = sem("in_ffn0"), sem("in_lora")
        in_ctx = [sem(f"in_ctx{n}") for n in range(2)]
        in_codes = [sem(f"in_codes{n}") for n in range(2)]
        in_dn = [sem(f"in_dn{n}") for n in range(2)]
        in_gu = [sem(f"in_gu{n}") for n in range(2)]
        in_ctx1, in_w1, in_ds = sem("in_xctx"), sem("in_w1"), sem("in_ds")
        in_tgu = [sem(f"in_tgu{n}") for n in range(2)]
        in_tdn = [sem(f"in_tdn{n}") for n in range(2)]
        consts = sem("consts")
        ident0 = sem("ident0")
        ident_ready = sem("ident_ready")
        dve_step = sem("dve_step")
        pool_step = sem("pool_step")
        neg_ready, pos_ready, joined, scaled = sem("neg_ready"), sem("pos_ready"), sem("joined"), sem("scaled")
        summed = sem("summed")
        w_ready, w_used = sem("w_ready"), sem("w_used")
        folded, fold_ready, fold_kept = sem("folded"), sem("fold_ready"), sem("fold_kept")
        ln_stats, ln_rstd, ln_sum, ln_done = sem("ln_stats"), sem("ln_rstd"), sem("ln_sum"), sem("ln_done")
        xt_ps, xt_ready = sem("xt_ps"), sem("xt_ready")
        qkv_ps, qk_ready, v_ready = sem("qkv_ps"), sem("qk_ready"), sem("v_ready")
        s_ps, max_ready, max_ps, aug_ready, sT_ps, p_ready = (sem(n) for n in ("s_ps", "max_ready", "max_ps", "aug_ready", "sT_ps", "p_ready"))
        pv_ps, att_ready, attT_ps, attT_ready, o_ps = (sem(n) for n in ("pv_ps", "att_ready", "attT_ps", "attT_ready", "o_ps"))
        sim_ps, sim_max, sim_exp, sim_p, cx_ps = (sem(n) for n in ("sim_ps", "sim_max", "sim_exp", "sim_p", "cx_ps"))
        ag_ps, lm_ready, lm_ps, lmT_ready, f0_ps = (sem(n) for n in ("ag_ps", "lm_ready", "lm_ps", "lmT_ready", "f0_ps"))
        af_ps, af_added, m_ps, m_ready, x1_ps, x1_ready = (sem(n) for n in ("af_ps", "af_added", "m_ps", "m_ready", "x1_ps", "x1_ready"))
        gate_ps, up_ps, sil_ready, h_ready = (sem(n) for n in ("gate_ps", "up_ps", "sil_ready", "h_ready"))
        hu_ready, hu_used, d_ps = sem("hu_ready"), sem("hu_used"), sem("d_ps")
        pj_ps, pj_ready = sem("pj_ps"), sem("pj_ready")
        x_ps, x_max, x_exp, xpT_ps, xpT_ready, xo_ps = (sem(n) for n in ("x_ps", "x_max", "x_exp", "xpT_ps", "xpT_ready", "xo_ps"))
        t_cast, t_gate_ps, t_up_ps, t_sil, t_h, t_gu_used = (sem(n) for n in ("t_cast", "t_gate_ps", "t_up_ps", "t_sil", "t_h", "t_gu_used"))
        t_dcast, t_hu, t_used, t_d_ps = (sem(n) for n in ("t_dcast", "t_hu", "t_used", "t_d_ps"))
        out_done = sem("out_done")
        pool_seen, sp_seen = sem("pool_seen"), sem("sp_seen")

        block = ctx.enter_context(nc.Block())

        def codes_landed(eng, c, i):
            if isinstance(c, int) and c < C_O:
                eng.wait_ge(in_codes[c % 2], 16 * (c // 2 + 1))
            elif isinstance(c, int) and c < C_GU:
                eng.wait_ge(in_codes[c % 2], 16 * (C_O // 2) + 48)

        @block.sync
        def _(sp):
            sp.dma_start(wqkT, i["wqkT"]).then_inc(in_qk, 16)
            for n in range(4):
                sp.dma_start(xT[:, :, 2 * n * P:2 * (n + 1) * P], i["xT"][:, :, 2 * n * P:2 * (n + 1) * P]).then_inc(in_x[n], 16)
                if n == 0:
                    sp.dma_start(wvT, i["wvT"]).then_inc(in_v, 16)
                    sp.dma_start(qk_b[:, :], i["qk_b"]).then_inc(in_bias, 16)
                    sp.dma_start(v_b[:, :], i["v_b"].partition_broadcast(P)).then_inc(in_bias, 16)
                    sp.dma_start(g_b[:, :], i["g_b"].partition_broadcast(P)).then_inc(in_bias, 16)
                    sp.dma_start(s_qkv[:, :], i["s_qkv"]).then_inc(in_bias, 16)
                    sp.dma_start(q_b[:, :], i["q_b"]).then_inc(in_bias, 16)
                    sp.dma_start(k_b[:, :], i["k_b"]).then_inc(in_bias, 16)
                    for c in range(2):
                        sp.dma_start(codes[:, c, :], i["c_qkv"][c]).then_inc(in_codes[c], 16)
            sp.dma_start(x[:, :, :], i["x"]).then_inc(in_xn, 16)
            sp.dma_start(wo0[0:65, :], i["wo0"]).then_inc(in_wo0, 16)
            for n in range(2):
                sp.dma_start(ctx_r[:, n, :], i["ctx"][:, n, :]).then_inc(in_ctx[n], 16)
                sp.dma_start(ctxT_r[:, n, :, :], i["ctxT"][:, :, n * P:(n + 1) * P]).then_inc(in_ctx[n], 16)
            sp.dma_start(w0T, i["w0T"]).then_inc(in_ffn0, 16)
            sp.dma_start(agT, i["agT"]).then_inc(in_ffn0, 16)
            sp.dma_start(bT0[0:RMAX + 1, :], i["bT0"]).then_inc(in_ffn0, 16)
            for dst, name in ((aT_3[0:3 * R1, :], "a_3"), (bT_3[0:3 * R1, :], "bT_3"), (aT_o[0:R1, :], "a_o"), (bT_o[0:R1, :], "bT_o"),
                              (a_g[:, :], "a_g"), (a_u[:, :], "a_u"), (bT_d[:, :], "bT_d"), (a_d, "a_d")):
                sp.dma_start(dst, i[name]).then_inc(in_lora, 16)
            sp.dma_start(ds[:, :], i["ds"].partition_broadcast(P)).then_inc(in_ds, 16)

            def slot_free(c):
                sp.wait_ge(neg_ready, 4 * (c - 1))
                sp.wait_ge(pos_ready, 4 * (c - 1))
                sp.wait_ge(scaled, c - 1)
                if not isinstance(c, int):
                    sp.sem_inc(sp_seen, 1)

            for c in range(2, C_GU):
                slot_free(c)
                if c < C_O:
                    sp.dma_start(codes[:, c % 2, :], i["c_qkv"][c]).then_inc(in_codes[c % 2], 16)
                else:
                    sp.dma_start(codes[:, c % 2, :], i["c_o"][c - C_O]).then_inc(in_codes[c % 2], 16)
                    for half in range(2):
                        sp.dma_start(scales[half * BLOCK:(half + 1) * BLOCK, c % 2, :],
                                     i["s_o"][c - C_O, half:half + 1, :].partition_broadcast(BLOCK)).then_inc(in_codes[c % 2], 16)

            for b in range(2, NT):
                sp.wait_ge(cx_ps, b - 1)
                sp.dma_start(ctx_r[:, b % 2, :], i["ctx"][:, b, :]).then_inc(in_ctx[b % 2], 16)
                sp.dma_start(ctxT_r[:, b % 2, :, :], i["ctxT"][:, :, b * P:(b + 1) * P]).then_inc(in_ctx[b % 2], 16)

            with sp.Fori(0, NF // 2) as n:
                for s in range(2):
                    j = 2 * n + s
                    slot_free(C_GU + j)
                    sp.wait_ge(folded, j + 1)
                    sp.sem_inc(sp_seen, 1)
                    sp.dma_start(codes[:, s, :], i["c_gu"][bass.ds(j, 1), :, :].rearrange("o p c -> (o p) c")).then_inc(in_gu[s], 16)
                    for half in range(2):
                        sp.dma_start(scales[half * BLOCK:(half + 1) * BLOCK, s, :],
                                     i["s_gu"][bass.ds(j, 1), half, :].partition_broadcast(BLOCK).rearrange("p o c -> p (o c)")).then_inc(in_gu[s], 16)
                    sp.dma_start(b_gu[:, s, :, :], i["bT_gu"][bass.ds(j, 1), :, :, :].rearrange("o r g c -> (o r) g c")).then_inc(in_gu[s], 16)
            with sp.Fori(0, NF // 2) as n:
                for s in range(2):
                    j = 2 * n + s
                    slot_free(C_DN + j)
                    sp.dma_start(codes[:, s, 0:D], i["c_dn"][bass.ds(j, 1), :, :].rearrange("o p c -> (o p) c")).then_inc(in_dn[s], 16)
                    for half in range(2):
                        sp.dma_start(scales[half * BLOCK:(half + 1) * BLOCK, s, 0:D],
                                     i["s_dn"][bass.ds(j, 1), half, :].partition_broadcast(BLOCK).rearrange("p o c -> p (o c)")).then_inc(in_dn[s], 16)

            sp.wait_ge(d_ps, 1)
            sp.wait_ge(hu_ready, NF)
            sp.dma_start(ctxT1, i["ctxT"]).then_inc(in_ctx1, 16)
            sp.dma_start(wkT1, i["wkT1"]).then_inc(in_w1, 16)
            sp.dma_start(wqT1, i["wqT1"]).then_inc(in_w1, 16)
            sp.dma_start(ctx1, i["ctx"]).then_inc(in_ctx1, 16)

            sp.wait_ge(neg_ready, 4 * C_END)
            sp.wait_ge(pos_ready, 4 * C_END)
            with sp.Fori(0, NF // 2) as n:
                for s in range(2):
                    j = 2 * n + s
                    sp.wait_ge(t_h, 2 * j + 2)
                    sp.sem_inc(sp_seen, 1)
                    sp.wait_ge(t_cast, j + 1)
                    sp.sem_inc(sp_seen, 1)
                    sp.dma_start(codes[:, s, :], i["t_gu"][bass.ds(j, 1), :, :].rearrange("o p c -> (o p) c")).then_inc(in_tgu[s], 16)
                    sp.dma_start(ff_s[:, s, :], i["ts_gu"][bass.ds(j, 1), :, :].rearrange("o p c -> (o p) c")).then_inc(in_tgu[s], 16)
            sp.wait_ge(t_cast, NF + 2)
            with sp.Fori(0, NF // 2) as n:
                for s in range(2):
                    j = 2 * n + s
                    sp.wait_ge(t_dcast, j + 1)
                    sp.sem_inc(sp_seen, 1)
                    sp.dma_start(codes[:, s, 0:D], i["t_dn"][bass.ds(j, 1), :, :].rearrange("o p c -> (o p) c")).then_inc(in_tdn[s], 16)

            for b in range(NT):
                sp.wait_ge(ln_done, 5 * NT + b + 1)
                sp.dma_start(out[b, :, :], x[:, b, :]).then_inc(out_done, 16)
            sp.wait_ge(out_done, 16 * NT)

        @block.tensor
        def _(pe):
            def transpose_tile(b, src, dst):
                for k in range(KD):
                    last = pe.transpose(dst[:, k * P:(k + 1) * P], src[:, k * P:(k + 1) * P], ident[:, :])
                last.then_inc(xt_ps, 1)

            def qkv(b):
                if b == 0:
                    pe.wait_ge(in_qk, 16)
                    pe.wait_ge(in_v, 16)
                if b % 2 == 0:
                    pe.wait_ge(in_x[b // 2], 16)
                if b >= 1:
                    pe.wait_ge(qk_ready, b)
                    pe.wait_ge(v_ready, b)
                if b >= 2:
                    pe.wait_ge(att_ready, b - 1)
                t = slice(b * P, (b + 1) * P)
                for c in range(4):
                    for k in range(KD):
                        pe.matmul(bank[0][:, c * P:(c + 1) * P], wqkT[:, k, c * P:(c + 1) * P], xT[:, k, t],
                                  start=(k == 0), stop=(k == KD - 1))
                for k in range(KD):
                    last = pe.matmul(bank[1][:, 0:64], xT[:, k, t], wvT[:, k, :], start=(k == 0), stop=(k == KD - 1))
                last.then_inc(qkv_ps, 1)

            def scores(b):
                pe.wait_ge(qk_ready, b + 1)
                if b >= 1:
                    pe.wait_ge(p_ready, b)
                for a in range(2):
                    for j in range(NQ):
                        q = slice(QR * j, QR * (j + 1))
                        last = pe.matmul(bank[2 + j][:, a * P:(a + 1) * P], qk[q, b % 2, a, :], qk[q, b % 2, 2 + a, :],
                                         start=True, stop=True)
                last.then_inc(s_ps, 1)

            def max_rows(b):
                pe.wait_ge(max_ready, b + 1)
                if b >= 2:
                    pe.wait_ge(ln_sum, b - 1)
                for a in range(2):
                    last = pe.transpose(bank[7][:, a * P:(a + 1) * P], mz[:, a, :], ident[:, :])
                last.then_inc(max_ps, 1)

            def scores_T(b):
                pe.wait_ge(aug_ready, b + 1)
                for a in range(2):
                    for j in range(NQ):
                        q = slice(QR * j, QR * (j + 1))
                        last = pe.matmul(bank[2 + j][:, a * P:(a + 1) * P], qk[q, b % 2, 2 + a, :], q_aug[q, a, :],
                                         start=True, stop=True)
                last.then_inc(sT_ps, 1)

            def heads_out(b):
                pe.wait_ge(p_ready, b + 1)
                pe.wait_ge(v_ready, min(b + 2, NT))
                for h in range(HEADS):
                    last = pe.matmul(bank[1][:, h * (HD + 1):(h + 1) * (HD + 1)], pT[:, b % 2, h % NQ, h // NQ, :],
                                     v1[:, b % 2, h, :], start=True, stop=True)
                last.then_inc(pv_ps, 1)

            def heads_T(b):
                pe.wait_ge(att_ready, b + 1)
                if b >= 1:
                    pe.wait_ge(xt_ready, b)
                pe.transpose(bank[6][0:64, 0:P], att[:, b % 2, :], ident[:, :]).then_inc(attT_ps, 1)

            def o_proj(b):
                pe.wait_ge(attT_ready, b + 1)
                if b == 0:
                    pe.wait_ge(in_wo0, 16)
                pe.matmul(bank[7][:, :], attT[0:65, b % 2, :], wo0[0:65, :], start=True, stop=True).then_inc(o_ps, 1)

            def x_T(layer, b, n=6):
                pe.wait_ge(ln_done, layer * NT + b + 1)
                if n == 6 and layer:
                    pe.wait_ge(xt_ready, layer * NT + b)
                transpose_tile(b, x[:, b, :], bank[n])

            pe.wait_ge(ident_ready, 1)
            qkv(0)
            for t in range(NT + 2):
                if t < NT:
                    scores(t)
                if t >= 2:
                    pe.wait_ge(attT_ready, t - 1)
                    x_T(0, t - 2)
                if t + 1 < NT:
                    qkv(t + 1)
                if t < NT:
                    max_rows(t)
                if 1 <= t <= NT:
                    heads_T(t - 1)
                if t < NT:
                    scores_T(t)
                if 1 <= t <= NT:
                    o_proj(t - 1)
                if t < NT:
                    heads_out(t)

            def sims(b):
                pe.wait_ge(xt_ready, b + 1)
                pe.wait_ge(in_ctx[b % 2], 32 * (b // 2 + 1))
                if b >= 2:
                    pe.wait_ge(sim_exp, b - 1)
                for k in range(KD):
                    last = pe.matmul(bank[2 + b % 2][:, 0:P], xT[:, k, b * P:(b + 1) * P], ctxT_r[:, b % 2, k, :],
                                     start=(k == 0), stop=(k == KD - 1))
                last.then_inc(sim_ps, 1)

            def context(b):
                pe.wait_ge(sim_p, b + 1)
                if b >= 2:
                    pe.wait_ge(ln_sum, NT + b - 1)
                pe.matmul(bank[4 + b % 2][:, :], prob[:, b % 2, :], ctx_r[:, b % 2, :], start=True, stop=True).then_inc(cx_ps, 1)

            for t in range(NT + 2):
                if t < NT:
                    sims(t)
                if t >= 2:
                    x_T(1, t - 2)
                if 1 <= t <= NT:
                    context(t - 1)

            def ranks(b):
                pe.wait_ge(xt_ready, NT + b + 1)
                if b == 0:
                    pe.wait_ge(in_ffn0, 48)
                if b >= 2:
                    pe.wait_ge(lm_ready, b - 1)
                for k in range(KD):
                    last = pe.matmul(bank[b % 2][:, 0:RMAX + NR], xT[:, k, b * P:(b + 1) * P], agT[:, k, :],
                                     start=(k == 0), stop=(k == KD - 1))
                last.then_inc(ag_ps, 1)
                if b >= 2:
                    pe.wait_ge(ln_sum, 2 * NT + b - 1)
                for k in range(KD):
                    pe.matmul(bank[2 + b % 2][:, :], xT[:, k, b * P:(b + 1) * P], w0T[:, k, :], start=(k == 0), stop=False)

            def lora_T(b):
                pe.wait_ge(lm_ready, b + 1)
                if b >= 1:
                    pe.wait_ge(lmT_ready, b)
                pe.transpose(bank[7][0:RMAX, 0:P], lm[:, b % 2, :], ident[:, :]).then_inc(lm_ps, 1)

            def lora_out(b):
                pe.wait_ge(lmT_ready, b + 1)
                pe.matmul(bank[2 + b % 2][:, :], lmT[:, b % 2, :], bT0[0:RMAX + 1, :], start=False, stop=True).then_inc(f0_ps, 1)

            for t in range(NT + 2):
                if t < NT:
                    ranks(t)
                if t >= 2:
                    x_T(2, t - 2)
                if 1 <= t <= NT:
                    lora_T(t - 1)
                    lora_out(t - 1)

            pe.wait_ge(in_lora, 16 * 8)
            for n in range(2 * KD):
                j = n % KD
                if n >= 2:
                    pe.wait_ge(af_added, n - 1)
                lhs, rhs = (bT_3[0:3 * R1, j * P:(j + 1) * P], aT_3[0:3 * R1, :]) if n < KD else (aT_o[0:R1, j * P:(j + 1) * P], bT_o[0:R1, :])
                pe.matmul(bank[n % 2][:, :], lhs, rhs, start=True, stop=True).then_inc(af_ps, 1)
            pe.wait_ge(af_added, 2 * KD)
            pe.wait_ge(ln_sum, 3 * NT)
            for c in range(KD):
                for j in range(KD):
                    last = pe.matmul(bank[2 + c][:, :], wsum[:, j, c * P:(c + 1) * P], woT[:, j, :], start=(j == 0), stop=(j == KD - 1))
                last.then_inc(m_ps, 1)
            pe.wait_ge(m_ready, KD)
            for t in range(NT + 1):
                if t < NT:
                    pe.wait_ge(xt_ready, 2 * NT + t + 1)
                    if t >= 2:
                        pe.wait_ge(x1_ready, t - 1)
                    for k in range(KD):
                        last = pe.matmul(bank[t % 2][:, :], xT[:, k, t * P:(t + 1) * P], mT[:, k, :], start=(k == 0), stop=(k == KD - 1))
                    last.then_inc(x1_ps, 1)
                if t >= 1:
                    pe.wait_ge(x1_ready, t)
                    pe.wait_ge(xt_ready, 3 * NT + t - 1)
                    transpose_tile(t - 1, rbuf[:, (t - 1) % 2, :], bank[6])

            for j in range(NF):
                if j >= 2:
                    pe.wait_ge(fold_kept, j - 1)
                pe.matmul(bank[4 + j % 2][:, :], a_d[:, j * P:(j + 1) * P], bT_d[:, :], start=True, stop=True).then_inc(fold_ready, 1)

            def gu_lora(s, n):
                pe.wait_ge(in_gu[s], 64 * (n + 1))
                for k in range(KD):
                    for g, a in ((0, a_g), (1, a_u)):
                        c = (2 * k + g) * P
                        last = pe.matmul(gu_fold[:, c:c + P], a[:, k * P:(k + 1) * P], b_gu[:, s, g, :], start=True, stop=True)
                last.then_inc(folded, 1)

            def gu_tile(s, j):
                pe.wait_ge(w_ready, j + 1)
                for tg in range(TG):
                    pe.wait_ge(h_ready, 2 * j + tg + 1)
                    for g, done in ((0, gate_ps), (1, up_ps)):
                        for k in range(KD):
                            c = (2 * k + g) * P
                            last = pe.matmul(bank[2 * g + tg][:, :], w[:, s, c:c + P], xT[:, k, tg * 512:(tg + 1) * 512],
                                             start=(k == 0), stop=(k == KD - 1))
                        last.then_inc(done, 1)

            pe.wait_ge(xt_ready, 4 * NT)
            pe.wait_ge(fold_kept, NF)
            gu_lora(0, 0)
            with pe.Fori(0, NF // 2 - 1) as n:
                pe.wait_ge(w_ready, 2 * n + 1)
                gu_lora(1, n)
                gu_tile(0, 2 * n)
                pe.wait_ge(w_ready, 2 * n + 2)
                gu_lora(0, n + 1)
                gu_tile(1, 2 * n + 1)
            pe.wait_ge(w_ready, NF - 1)
            gu_lora(1, NF // 2 - 1)
            gu_tile(0, NF - 2)
            gu_tile(1, NF - 1)

            def down_tile(s, j, w_sem, w_n, h_sem, h_n, used, first, last_one, done):
                pe.wait_ge(w_sem, w_n)
                pe.wait_ge(h_sem, h_n)
                for b in range(NT):
                    last = pe.matmul(bank[b][:, :], h_use[:, s, b * P:(b + 1) * P], w[:, s, 0:D], start=first, stop=last_one)
                last.then_inc(used, 1)
                if last_one:
                    return last

            pe.wait_ge(h_ready, 2 * NF + 2)
            down_tile(0, 0, w_ready, NF + 1, hu_ready, 1, hu_used, True, False, None)
            down_tile(1, 1, w_ready, NF + 2, hu_ready, 2, hu_used, False, False, None)
            with pe.Fori(1, NF // 2 - 1) as n:
                for s in range(2):
                    down_tile(s, None, w_ready, NF + 2 * n + s + 1, hu_ready, 2 * n + s + 1, hu_used, False, False, None)
            down_tile(0, NF - 2, w_ready, 2 * NF - 1, hu_ready, NF - 1, hu_used, False, False, None)
            down_tile(1, NF - 1, w_ready, 2 * NF, hu_ready, NF, d_ps, False, True, None)
            for b in range(NT):
                x_T(3, b, n=b)

            def project(wT, src, n):
                for c in range(KD):
                    for tg in range(TG):
                        m = n + c * TG + tg
                        if m >= 4:
                            pe.wait_ge(pj_ready, m - 3)
                        for k in range(KD):
                            last = pe.matmul(bank[m % 4][:, :], wT[:, k, c * P:(c + 1) * P], src[:, k, tg * 512:(tg + 1) * 512],
                                             start=(k == 0), stop=(k == KD - 1))
                        last.then_inc(pj_ps, 1)

            pe.wait_ge(xt_ready, 5 * NT)
            pe.wait_ge(in_ctx1, 32)
            pe.wait_ge(in_w1, 32)
            project(wkT1, ctxT1, 0)
            project(wqT1, xT, KD * TG)
            pe.wait_ge(pj_ready, 2 * KD * TG)

            def x_scores(b):
                if b >= 2:
                    pe.wait_ge(x_exp, b - 1)
                for k in range(KD):
                    last = pe.matmul(bank[4 + b % 2][:, 0:P], qT1[:, k, b * P:(b + 1) * P], kT1[:, k, b * P:(b + 1) * P],
                                     start=(k == 0), stop=(k == KD - 1))
                last.then_inc(x_ps, 1)

            def x_probT(b):
                pe.wait_ge(x_exp, b + 1)
                if b >= 2:
                    pe.wait_ge(xpT_ready, b - 1)
                pe.transpose(bank[2 + b % 2][:, 0:P], prob[:, b % 2, :], ident[:, :]).then_inc(xpT_ps, 1)

            def x_out(b):
                pe.wait_ge(xpT_ready, b + 1)
                if b >= 2:
                    pe.wait_ge(ln_sum, 4 * NT + b - 1)
                pe.matmul(bank[b % 2][:, :], probT[:, b % 2, :], ctx1[:, b, :], start=True, stop=True).then_inc(xo_ps, 1)

            for t in range(NT + 2):
                if t < NT:
                    x_scores(t)
                if t >= 2:
                    x_T(4, t - 2)
                if 1 <= t <= NT:
                    x_probT(t - 1)
                    x_out(t - 1)

            def t_gu_tile(s, j):
                pe.wait_ge(t_cast, j + 3)
                for tg in range(TG):
                    pe.wait_ge(t_h, 2 * j + tg + 3)
                    for g, done in ((0, t_gate_ps), (1, t_up_ps)):
                        for k in range(KD):
                            c = (2 * k + g) * P
                            last = pe.matmul(bank[2 * g + tg][:, :], w[:, s, c:c + P], xT[:, k, tg * 512:(tg + 1) * 512],
                                             start=(k == 0), stop=(k == KD - 1))
                        last.then_inc(done, 1)

            pe.wait_ge(xt_ready, 6 * NT)
            with pe.Fori(0, NF // 2) as n:
                for s in range(2):
                    t_gu_tile(s, 2 * n + s)
            pe.wait_ge(t_h, 2 * NF + 4)
            down_tile(0, 0, t_dcast, 3, t_hu, 1, t_used, True, False, None)
            down_tile(1, 1, t_dcast, 4, t_hu, 2, t_used, False, False, None)
            with pe.Fori(1, NF // 2 - 1) as n:
                for s in range(2):
                    down_tile(s, None, t_dcast, 2 * n + s + 3, t_hu, 2 * n + s + 1, t_used, False, False, None)
            down_tile(0, NF - 2, t_dcast, NF + 1, t_hu, NF - 1, t_used, False, False, None)
            down_tile(1, NF - 1, t_dcast, NF + 2, t_hu, NF, t_d_ps, False, True, None)

        @block.scalar
        def _(act):
            def neg_lines(c, slot, n, e=CH):
                for line_n, freed in ((1, 1), (2, 3), (3, 5), (0, 7)):
                    if not (isinstance(c, int) and c == 0):
                        act.wait_ge(joined, DQ * (c - 1) + freed)
                    a, b = LINES[line_n]
                    nc.scalar.activation(line[:, line_n, 0:e], codes[:, slot, 0:e], ACT.Copy, bias=b, scale=a).then_inc(neg_ready, 1)

            def early_lines(c):
                codes_landed(act, c, None)
                neg_lines(c, c % 2, None)

            def gu_lines(s, n):
                act.wait_ge(in_gu[s], 64 * (n + 1))
                neg_lines(C_GU + 2 * n + s, s, n)

            def dn_lines(s, n):
                act.wait_ge(in_dn[s], 48 * (n + 1))
                neg_lines(C_DN + 2 * n + s, s, n, D)

            def x_T_out(m, n=6):
                act.wait_ge(xt_ps, m + 1)
                b = m % NT
                nc.scalar.activation(xT[:, :, b * P:(b + 1) * P], bank[n][:, :].rearrange("p (k t) -> p k t", k=KD),
                                     ACT.Copy).then_inc(xt_ready, 1)

            early_lines(0)
            for t in range(NT + 2):
                if t >= 2:
                    x_T_out(t - 2)
                if 1 <= t <= NT:
                    act.wait_ge(attT_ps, t)
                    if t == 1:
                        act.wait_ge(consts, 1)
                    if t >= 3:
                        act.wait_ge(o_ps, t - 2)
                    nc.scalar.activation(attT[0:64, (t - 1) % 2, :], bank[6][0:64, 0:P], ACT.Copy).then_inc(attT_ready, 1)
                if t < NT:
                    act.wait_ge(sT_ps, t + 1)
                    if t >= 2:
                        act.wait_ge(pv_ps, t - 1)
                    nc.scalar.activation(pT[:, t % 2, :, :, :].rearrange("p j a t -> p j (a t)"), heads_ps[:, :, 0:2 * P],
                                         ACT.Exp).then_inc(p_ready, 1)
                    if t + 1 < C_GU:
                        early_lines(t + 1)

            for t in range(NT + 2):
                if t < NT:
                    act.wait_ge(sim_max, t + 1)
                    nc.scalar.activation(prob[:, t % 2, :], bank[2 + t % 2][:, 0:P], ACT.Exp, bias=small[:, t % 2, 0:1],
                                         scale=float(P) ** -0.5, accum_out=small[:, t % 2, 1:2]).then_inc(sim_exp, 1)
                if t >= 2:
                    x_T_out(NT + t - 2)

            for t in range(NT + 2):
                if 1 <= t <= NT:
                    act.wait_ge(lm_ps, t)
                    if t >= 3:
                        act.wait_ge(f0_ps, t - 2)
                    nc.scalar.activation(lmT[0:RMAX, (t - 1) % 2, :], bank[7][0:RMAX, 0:P], ACT.Copy).then_inc(lmT_ready, 1)
                if t >= 2:
                    x_T_out(2 * NT + t - 2)

            for c in range(KD):
                act.wait_ge(m_ps, c + 1)
                nc.scalar.activation(mT[:, c, :], bank[2 + c][:, :], ACT.Copy, scale=1.0 / 3.0).then_inc(m_ready, 1)
            gu_lines(0, 0)
            for b in range(NT):
                x_T_out(3 * NT + b)
            act.wait_ge(af_ps, 2 * KD)
            for j in range(NF):
                act.wait_ge(fold_ready, j + 1)
                nc.scalar.activation(fold[:, j, :], bank[4 + j % 2][:, :], ACT.Copy).then_inc(fold_kept, 1)

            def silu(j):
                for tg in range(TG):
                    act.wait_ge(gate_ps, 2 * j + tg + 1)
                    act.wait_ge(h_ready, 2 * j + tg + 1)
                    nc.scalar.activation(sil[:, tg, :], bank[tg][:, :], ACT.Silu).then_inc(sil_ready, 1)

            with act.Fori(0, NF // 2 - 1) as n:
                gu_lines(1, n)
                silu(2 * n)
                gu_lines(0, n + 1)
                silu(2 * n + 1)
            gu_lines(1, NF // 2 - 1)
            silu(NF - 2)
            dn_lines(0, 0)
            silu(NF - 1)

            def h_copy(s, j, n_free):
                if n_free is not None:
                    act.wait_ge(hu_used, n_free)
                nc.scalar.activation(h_use[:, s, :], hT[:, bass.ds(j, 1), :].rearrange("p o t -> p (o t)"), ACT.Copy).then_inc(hu_ready, 1)

            dn_lines(1, 0)
            act.wait_ge(h_ready, 2 * NF + 2)
            act.wait_ge(fold_ready, NF)
            h_copy(0, 0, None)
            h_copy(1, 1, None)
            with act.Fori(1, NF // 2) as n:
                for s in range(2):
                    dn_lines(s, n)
                    h_copy(s, 2 * n + s, 2 * n + s - 1)
            for b in range(NT):
                x_T_out(4 * NT + b, n=b)

            for m in range(2 * KD * TG):
                act.wait_ge(pj_ps, m + 1)
                if m == 0:
                    act.wait_ge(joined, DQ * C_END)
                c, tg = (m % (KD * TG)) // TG, m % TG
                dst, bias = (kT1, k_b) if m < KD * TG else (qT1, q_b)
                nc.scalar.activation(dst[:, c, tg * 512:(tg + 1) * 512], bank[m % 4][:, :], ACT.Identity,
                                     bias=bias[:, c:c + 1]).then_inc(pj_ready, 1)
            for t in range(NT + 2):
                if t < NT:
                    act.wait_ge(x_max, t + 1)
                    if t >= 2:
                        act.wait_ge(xpT_ps, t - 1)
                    nc.scalar.activation(prob[:, t % 2, :], bank[4 + t % 2][:, 0:P], ACT.Exp, bias=small[:, t % 2, 0:1],
                                         scale=float(D) ** -0.5, accum_out=small[:, t % 2, 1:2]).then_inc(x_exp, 1)
                if t >= 2:
                    x_T_out(5 * NT + t - 2)
                if 1 <= t <= NT:
                    act.wait_ge(xpT_ps, t)
                    if t >= 3:
                        act.wait_ge(xo_ps, t - 2)
                    nc.scalar.activation(probT[:, (t - 1) % 2, :], bank[2 + (t - 1) % 2][:, 0:P], ACT.Copy).then_inc(xpT_ready, 1)

            def t_gu_cast(s, n, free):
                act.wait_ge(in_tgu[s], 32 * (n + 1))
                if free is not None:
                    act.wait_ge(t_up_ps, free)
                nc.scalar.activation(w[:, s, :], codes[:, s, :], ACT.Copy).then_inc(t_cast, 1)

            def t_silu(s, j):
                for tg in range(TG):
                    act.wait_ge(t_gate_ps, 2 * j + tg + 1)
                    act.wait_ge(t_h, 2 * j + tg + 3)
                    nc.scalar.activation(sil[:, tg, :], bank[tg][:, :], ACT.Silu, scale=ff_s[:, s, 0:1]).then_inc(t_sil, 1)

            act.wait_ge(hu_used, NF - 1)
            act.wait_ge(d_ps, 1)
            t_gu_cast(0, 0, None)
            t_gu_cast(1, 0, None)
            with act.Fori(0, NF // 2 - 1) as n:
                t_silu(0, 2 * n)
                t_gu_cast(0, n + 1, 4 * n + 2)
                t_silu(1, 2 * n + 1)
                t_gu_cast(1, n + 1, 4 * n + 4)
            t_silu(0, NF - 2)
            t_silu(1, NF - 1)

            def t_dn(s, j, n, free):
                act.wait_ge(in_tdn[s], 16 * (n + 1))
                if free is not None:
                    act.wait_ge(t_used, free)
                nc.scalar.activation(w[:, s, 0:D], codes[:, s, 0:D], ACT.Copy).then_inc(t_dcast, 1)
                nc.scalar.activation(h_use[:, s, :], hT[:, bass.ds(j, 1), :].rearrange("p o t -> p (o t)"), ACT.Copy).then_inc(t_hu, 1)

            act.wait_ge(t_up_ps, 2 * NF)
            act.wait_ge(t_h, 2 * NF + 4)
            t_dn(0, 0, 0, None)
            t_dn(1, 1, 0, None)
            with act.Fori(1, NF // 2) as n:
                for s in range(2):
                    t_dn(s, 2 * n + s, n, 2 * n + s - 1)

        @block.gpsimd
        def _(pool):
            steps = [0]

            def link(ins):
                steps[0] += 1
                ins.then_inc(pool_step, 1)
                pool.wait_ge(pool_step, steps[0])

            link(nc.gpsimd.memset(ident[:, :], 0.0))
            nc.gpsimd.affine_select(out=ident[:, :], in_=ident[:, :], compare_op=ALU.not_equal, fill=1.0, base=0,
                                    pattern=[[-1, P]], channel_multiplier=1).then_inc(ident_ready, 1)
            link(nc.gpsimd.memset(minus_half[:, :], -0.5))

            def pos_lines(c, slot, e=CH):
                for line_n, freed in ((5, 2), (6, 4), (7, 6), (4, 7)):
                    if not (isinstance(c, int) and c == 0):
                        pool.wait_ge(joined, DQ * (c - 1) + freed)
                    if not isinstance(c, int):
                        pool.sem_inc(pool_seen, 1)
                    a, b = LINES[line_n]
                    nc.gpsimd.tensor_scalar(line[:, line_n, 0:e], codes[:, slot, 0:e], a, b, ALU.mult, ALU.add).then_inc(pos_ready, 1)

            def early_lines(c):
                codes_landed(pool, c, None)
                pos_lines(c, c % 2)

            def gu_lines(s, n):
                pool.wait_ge(in_gu[s], 64 * (n + 1))
                pos_lines(C_GU + 2 * n + s, s)

            def dn_lines(s, n):
                pool.wait_ge(in_dn[s], 48 * (n + 1))
                pos_lines(C_DN + 2 * n + s, s, D)

            def scale(c, s, e=CH):
                pool.wait_ge(joined, DQ * (c + 1))
                nc.gpsimd.tensor_tensor(w[:, s, 0:e], w[:, s, 0:e], scales[:, s, 0:e], ALU.mult).then_inc(scaled, 1)

            def scale_attention(c):
                s = c % 2
                pool.wait_ge(joined, DQ * (c + 1))
                if c < C_O:
                    m, half = c // 2, c % 2
                    dst = wsum[:, 2 * half:2 * half + 2, :].rearrange("p j c -> p (j c)") if m == 0 else w[:, s, :]
                    nb = 2 * NB
                    sc = s_qkv[:, (2 * m + half) * nb:(2 * m + half + 1) * nb]
                    if c == 0:
                        pool.wait_ge(in_bias, 16 * 6)
                    nc.gpsimd.tensor_tensor(dst.rearrange("p (b c) -> p b c", b=nb), w[:, s, :].rearrange("p (b c) -> p b c", b=nb),
                                            sc.unsqueeze(2).to_broadcast([P, nb, BLOCK]), ALU.mult).then_inc(scaled, 1)
                else:
                    half = c - C_O
                    nc.gpsimd.tensor_tensor(woT[:, 2 * half:2 * half + 2, :].rearrange("p j c -> p (j c)"), w[:, s, :],
                                            scales[:, s, :], ALU.mult).then_inc(scaled, 1)

            def rstd_of(m):
                pool.wait_ge(ln_stats, m + 1)
                link(nc.gpsimd.tensor_scalar(rstd[:, m % 2, 0:1], mv[:, m % 2, 1:2], LN_EPS, None, ALU.add))
                nc.gpsimd.tensor_tensor(rstd[:, m % 2, 1:2], rstd[:, m % 2, 0:1], minus_half[:, :], ALU.pow).then_inc(ln_rstd, 1)

            early_lines(0)
            for t in range(NT + 1):
                if t >= 1:
                    rstd_of(t - 1)
                if t + 1 < C_GU:
                    early_lines(t + 1)
                if t < C_GU:
                    scale_attention(t)
            for m in range(NT, 3 * NT):
                rstd_of(m)
            gu_lines(0, 0)
            with pool.Fori(0, NF // 2 - 1) as n:
                gu_lines(1, n)
                scale(C_GU + 2 * n, 0)
                gu_lines(0, n + 1)
                scale(C_GU + 2 * n + 1, 1)
            gu_lines(1, NF // 2 - 1)
            scale(C_DN - 2, 0)
            dn_lines(0, 0)
            scale(C_DN - 1, 1)
            with pool.Fori(0, NF // 2 - 1) as n:
                dn_lines(1, n)
                scale(C_DN + 2 * n, 0, D)
                dn_lines(0, n + 1)
                scale(C_DN + 2 * n + 1, 1, D)
            dn_lines(1, NF // 2 - 1)
            scale(C_END - 2, 0, D)
            scale(C_END - 1, 1, D)
            for m in range(3 * NT, 6 * NT):
                rstd_of(m)

        @block.vector
        def _(dve):
            steps = [0]

            def link(ins):
                steps[0] += 1
                ins.then_inc(dve_step, 1)
                dve.wait_ge(dve_step, steps[0])

            def join(c, s, e=CH):
                def L(n):
                    return line[:, n, 0:e]

                base = DQ * c
                neg, pos = 4 * c, 4 * c
                dve.wait_ge(neg_ready, neg + 4)
                nc.vector.tensor_tensor(L(0), L(0), L(1), ALU.min).then_inc(joined, 1)
                dve.wait_ge(pos_ready, pos + 4)
                nc.vector.tensor_tensor(L(4), L(4), L(5), ALU.max).then_inc(joined, 1)
                dve.wait_ge(joined, base + 1)
                nc.vector.tensor_tensor(L(0), L(0), L(2), ALU.min).then_inc(joined, 1)
                dve.wait_ge(joined, base + 2)
                nc.vector.tensor_tensor(L(4), L(4), L(6), ALU.max).then_inc(joined, 1)
                dve.wait_ge(joined, base + 3)
                nc.vector.scalar_tensor_tensor(L(0), L(0), 0.0, L(3), ALU.min, ALU.min).then_inc(joined, 1)
                dve.wait_ge(joined, base + 4)
                nc.vector.tensor_tensor(L(4), L(4), L(7), ALU.max).then_inc(joined, 1)
                dve.wait_ge(joined, base + 6)
                nc.vector.scalar_tensor_tensor(w[:, s, 0:e], L(4), 0.0, L(0), ALU.max, ALU.add).then_inc(joined, 1)

            def add_attention(c):
                if 2 <= c < C_O:
                    dve.wait_ge(scaled, c + 1)
                    half = c % 2
                    dst = wsum[:, 2 * half:2 * half + 2, :].rearrange("p j c -> p (j c)")
                    link(nc.vector.tensor_tensor(dst, dst, w[:, c % 2, :], ALU.add))

            def ln_head(m, add):
                b, s = m % NT, m % 2
                if m >= 2:
                    dve.wait_ge(ln_done, m - 1)
                add(rbuf[:, s, :], x[:, b, :])
                dve.wait_ge(ln_sum, m + 1)
                link(nc.vector.bn_stats(st[:, s, :], rbuf[:, s, :]))
                nc.vector.bn_aggr(mv[:, s, :], st[:, s, :]).then_inc(ln_stats, 1)

            def ln_tail(m):
                b, s = m % NT, m % 2
                dve.wait_ge(ln_rstd, m + 1)
                nc.vector.tensor_scalar(x[:, b, :], rbuf[:, s, :], mv[:, s, 0:1], rstd[:, s, 1:2],
                                        ALU.subtract, ALU.mult).then_inc(ln_done, 1)

            def plus(n):
                return lambda r, xb: nc.vector.tensor_tensor(r, xb, bank[n][:, :], ALU.add).then_inc(ln_sum, 1)

            nc.vector.memset(attT[64:65, :, :], 1.0)
            nc.vector.memset(lmT[64:65, :, :], 1.0)
            nc.vector.memset(mz[:, :, :], 0.0)
            nc.vector.memset(v1[:, :, :, HD:HD + 1], 1.0).then_inc(consts, 1)
            nc.vector.sem_inc(h_ready, 2)
            nc.vector.sem_inc(t_h, 4)
            nc.vector.sem_inc(t_cast, 2)
            nc.vector.sem_inc(t_dcast, 2)
            nc.vector.sem_inc(folded, 2)
            dve.wait_ge(consts, 1)

            def qkv_out(b):
                dve.wait_ge(qkv_ps, b + 1)
                if b >= 2:
                    dve.wait_ge(sT_ps, b - 1)
                    dve.wait_ge(pv_ps, b - 1)
                if b == 0:
                    dve.wait_ge(in_bias, 16 * 6)
                nc.vector.tensor_tensor(qk[:, b % 2, :, :], bank[0][:, :].rearrange("p (c t) -> p c t", c=4),
                                        qk_b[:, :].unsqueeze(2).to_broadcast([P, 4, P]), ALU.add).then_inc(qk_ready, 1)
                nc.vector.tensor_tensor(v1[:, b % 2, :, 0:HD], bank[1][:, 0:64].rearrange("p (h e) -> p h e", h=HEADS),
                                        v_b[:, :].rearrange("p (h e) -> p h e", h=HEADS), ALU.add).then_inc(v_ready, 1)

            def row_max(b):
                dve.wait_ge(s_ps, b + 1)
                s = b % 2
                link(nc.vector.tensor_reduce(small[:, s, 0:8].rearrange("p (j a) -> p j a", j=NQ),
                                             heads_ps[:, :, 0:2 * P].rearrange("p j (a k) -> p j a k", a=2), AX.X, ALU.max))
                if b >= 1:
                    dve.wait_ge(max_ps, b)
                nc.vector.tensor_scalar(mz[:, :, :].rearrange("p a (j r) -> p a j r", j=NQ)[:, :, :, HD],
                                        small[:, s, 0:8].rearrange("p (j a) -> p a j", j=NQ), -1.0, None, ALU.mult).then_inc(max_ready, 1)

            def augment(b):
                dve.wait_ge(max_ps, b + 1)
                if b >= 1:
                    dve.wait_ge(sT_ps, b)
                nc.vector.tensor_tensor(q_aug, qk[:, b % 2, 0:2, :], bank[7][:, 0:2 * P].rearrange("p (a t) -> p a t", a=2),
                                        ALU.add).then_inc(aug_ready, 1)

            def normalise_heads(b):
                dve.wait_ge(pv_ps, b + 1)
                s = b % 2
                o = bank[1][:, 0:HEADS * (HD + 1)].rearrange("p (h e) -> p h e", h=HEADS)
                link(nc.vector.reciprocal(small[:, s, 8:16], o[:, :, HD]))
                link(nc.vector.tensor_scalar(small[:, s, 16:24], small[:, s, 8:16], float(D // HEADS) ** -0.5, None, ALU.mult))
                if b >= 2:
                    dve.wait_ge(attT_ps, b - 1)
                nc.vector.tensor_tensor(att[:, s, :].rearrange("p (h e) -> p h e", h=HEADS), o[:, :, 0:HD],
                                        small[:, s, 16:24].unsqueeze(2).to_broadcast([P, HEADS, HD]), ALU.mult).then_inc(att_ready, 1)

            qkv_out(0)
            for t in range(NT + 1):
                if t < NT:
                    row_max(t)
                if t + 1 < NT:
                    qkv_out(t + 1)
                if t < NT:
                    augment(t)
                if t >= 1:
                    dve.wait_ge(o_ps, t)
                    if t == 1:
                        dve.wait_ge(in_xn, 16)
                    ln_head(t - 1, plus(7))
                if t < C_GU:
                    join(t, t % 2)
                if t >= 1:
                    ln_tail(t - 1)
                    add_attention(t - 1)
                if t < NT:
                    normalise_heads(t)

            for t in range(NT + 1):
                if t < NT:
                    s = t % 2
                    dve.wait_ge(sim_ps, t + 1)
                    link(nc.vector.tensor_reduce(small[:, s, 2:3], bank[2 + s][:, 0:P], AX.X, ALU.max))
                    nc.vector.tensor_scalar(small[:, s, 0:1], small[:, s, 2:3], -float(P) ** -0.5, None, ALU.mult).then_inc(sim_max, 1)
                if t >= 1:
                    dve.wait_ge(cx_ps, t)
                    ln_head(NT + t - 1, plus(4 + (t - 1) % 2))
                if t < NT:
                    dve.wait_ge(sim_exp, t + 1)
                    link(nc.vector.reciprocal(small[:, s, 3:4], small[:, s, 1:2]))
                    nc.vector.tensor_scalar(prob[:, s, :], prob[:, s, :], small[:, s, 3:4], None, ALU.mult).then_inc(sim_p, 1)
                if t >= 1:
                    ln_tail(NT + t - 1)

            def choose(b):
                s = b % 2
                ps = bank[s]
                g = gate_v[:, s, :]
                dve.wait_ge(ag_ps, b + 1)
                link(nc.vector.tensor_tensor(g[:, 0:4], ps[:, RMAX:RMAX + NR], g_b[:, :], ALU.add))
                nc.vector.tensor_tensor(g[:, 4:5], g[:, 0:1], g[:, 1:2], ALU.max)
                link(nc.vector.tensor_tensor(g[:, 5:6], g[:, 2:3], g[:, 3:4], ALU.max))
                nc.vector.tensor_tensor(g[:, 6:7], g[:, 1:2], g[:, 5:6], ALU.max)
                link(nc.vector.tensor_tensor(g[:, 7:8], g[:, 4:5], g[:, 2:3], ALU.max))
                nc.vector.tensor_tensor(g[:, 8:9], g[:, 6:7], g[:, 0:1], ALU.is_gt)
                nc.vector.tensor_tensor(g[:, 9:10], g[:, 5:6], g[:, 4:5], ALU.is_gt)
                link(nc.vector.tensor_tensor(g[:, 10:11], g[:, 3:4], g[:, 7:8], ALU.is_gt))
                if b >= 2:
                    dve.wait_ge(lm_ps, b - 1)
                nc.vector.tensor_copy(lm[:, s, 0:RANKS[0]], ps[:, 0:RANKS[0]])
                for n in range(1, NR):
                    last = nc.vector.tensor_scalar(lm[:, s, RANKS[n - 1]:RANKS[n]], ps[:, RANKS[n - 1]:RANKS[n]],
                                                   g[:, 7 + n:8 + n], None, ALU.mult)
                last.then_inc(lm_ready, 1)

            for t in range(NT + 1):
                if t < NT:
                    choose(t)
                if t >= 1:
                    dve.wait_ge(f0_ps, t)
                    ln_head(2 * NT + t - 1, plus(2 + (t - 1) % 2))
                    ln_tail(2 * NT + t - 1)

            for n in range(2 * KD):
                dve.wait_ge(af_ps, n + 1)
                if n == 0:
                    dve.wait_ge(scaled, C_GU)
                dst = wsum[:, n, :] if n < KD else woT[:, n - KD, :]
                nc.vector.tensor_tensor(dst, dst, bank[n % 2][:, :], ALU.add).then_inc(af_added, 1)
            join(C_GU, 0)
            for b in range(NT):
                s = b % 2
                dve.wait_ge(x1_ps, b + 1)
                dve.wait_ge(ln_done, 3 * NT)
                if b >= 2:
                    dve.wait_ge(xt_ps, 3 * NT + b - 1)
                nc.vector.tensor_tensor(rbuf[:, s, :], x[:, b, :], bank[s][:, :], ALU.add).then_inc(x1_ready, 1)
                dve.wait_ge(x1_ready, b + 1)
                nc.vector.tensor_tensor(x[:, b, :], x[:, b, :], rbuf[:, s, :], ALU.add).then_inc(summed, 1)

            def gu_add(c, s, j):
                dve.wait_ge(scaled, c + 1)
                dve.wait_ge(folded, j + 3)
                nc.vector.tensor_tensor(w[:, s, :], w[:, s, :], gu_fold, ALU.add).then_inc(w_ready, 1)

            def hidden(j):
                for tg in range(TG):
                    dve.wait_ge(sil_ready, 2 * j + tg + 1)
                    dve.wait_ge(up_ps, 2 * j + tg + 1)
                    nc.vector.tensor_tensor(hT[:, bass.ds(j, 1), tg * 512:(tg + 1) * 512].rearrange("p o t -> p (o t)"),
                                            sil[:, tg, :], bank[2 + tg][:, :], ALU.mult).then_inc(h_ready, 1)

            def slot_multiplied(j):
                dve.wait_ge(up_ps, 2 * j + 2)

            dve.wait_ge(x1_ps, NT)
            join(C_GU + 1, 1)
            gu_add(C_GU, 0, 0)
            with dve.Fori(0, NF // 2 - 1) as n:
                for s in range(2):
                    j = 2 * n + s
                    slot_multiplied(j)
                    join(C_GU + 2 + j, s)
                    gu_add(C_GU + 1 + j, 1 - s, j + 1)
                    hidden(j)
            slot_multiplied(NF - 2)
            join(C_DN, 0, D)
            gu_add(C_DN - 1, 1, NF - 1)
            hidden(NF - 2)
            slot_multiplied(NF - 1)
            join(C_DN + 1, 1, D)
            hidden(NF - 1)

            def dn_add(c, s, j):
                dve.wait_ge(scaled, c + 1)
                nc.vector.tensor_tensor(w[:, s, 0:D], w[:, s, 0:D], fold[:, bass.ds(j, 1), :].rearrange("p o c -> p (o c)"),
                                        ALU.add).then_inc(w_ready, 1)

            dve.wait_ge(fold_kept, NF)
            dn_add(C_DN, 0, 0)
            with dve.Fori(0, NF // 2 - 1) as n:
                for s in range(2):
                    j = 2 * n + s
                    dve.wait_ge(hu_used, j + 1)
                    join(C_DN + 2 + j, s, D)
                    dn_add(C_DN + 1 + j, 1 - s, j + 1)
            dn_add(C_END - 1, 1, NF - 1)
            dve.wait_ge(d_ps, 1)
            dve.wait_ge(summed, NT)
            for b in range(NT):
                ln_head(3 * NT + b, plus(b))
                if b >= 1:
                    ln_tail(3 * NT + b - 1)
            ln_tail(4 * NT - 1)

            for t in range(NT + 1):
                if t < NT:
                    s = t % 2
                    dve.wait_ge(x_ps, t + 1)
                    link(nc.vector.tensor_reduce(small[:, s, 2:3], bank[4 + s][:, 0:P], AX.X, ALU.max))
                    nc.vector.tensor_scalar(small[:, s, 0:1], small[:, s, 2:3], -float(D) ** -0.5, None, ALU.mult).then_inc(x_max, 1)
                if t >= 1:
                    s = (t - 1) % 2
                    dve.wait_ge(xo_ps, t)
                    dve.wait_ge(ln_done, 4 * NT)
                    link(nc.vector.reciprocal(small[:, s, 3:4], small[:, s, 1:2]))
                    ln_head(4 * NT + t - 1, lambda r, xb: nc.vector.scalar_tensor_tensor(
                        r, bank[s][:, :], small[:, s, 3:4], xb, ALU.mult, ALU.add).then_inc(ln_sum, 1))
                    ln_tail(4 * NT + t - 1)

            with dve.Fori(0, NF // 2) as n:
                for s in range(2):
                    j = 2 * n + s
                    for tg in range(TG):
                        dve.wait_ge(t_sil, 2 * j + tg + 1)
                        dve.wait_ge(t_up_ps, 2 * j + tg + 1)
                        nc.vector.scalar_tensor_tensor(hT[:, bass.ds(j, 1), tg * 512:(tg + 1) * 512].rearrange("p o t -> p (o t)"),
                                                       bank[2 + tg][:, :], ff_s[:, s, 1:2], sil[:, tg, :],
                                                       ALU.mult, ALU.mult).then_inc(t_h, 1)
            dve.wait_ge(t_d_ps, 1)
            dve.wait_ge(in_ds, 16)
            for b in range(NT):
                m = 5 * NT + b

                def scaled_sum(r, xb):
                    link(nc.vector.tensor_tensor(r, bank[b][:, :], ds[:, :], ALU.mult))
                    nc.vector.tensor_tensor(r, r, xb, ALU.add).then_inc(ln_sum, 1)

                if b == 0:
                    dve.wait_ge(ln_done, 5 * NT)
                ln_head(m, scaled_sum)
                if b >= 1:
                    ln_tail(m - 1)
            ln_tail(6 * NT - 1)


def layout(a):
    c = np.ascontiguousarray
    f = {k: np.asarray(v) for k, v in a.items()}

    def rows(m, n=P):
        return c(m.reshape(-1, n, m.shape[-1]).transpose(1, 0, 2))

    x2, ctx2 = f["x"].reshape(T, D), f["ctx_4096"].reshape(T, D)
    wqk = f["L0_attn_Wqk_w"].reshape(2, NQ, HD, 2, D)
    wqkT = np.zeros((D, 2, 2, NQ, QR), np.float32)
    wqkT[..., :HD] = wqk.transpose(4, 3, 0, 1, 2)
    qk_b = np.zeros((NQ, QR, 2, 2), np.float32)
    qk_b[:, :HD] = f["L0_attn_Wqk_b"].reshape(2, NQ, HD, 2).transpose(1, 2, 3, 0)
    qk_b[:, HD, 1, :] = 1.0
    ca, sa = f["L1_attn_codes_attn"], f["L1_attn_scales_attn"]

    def pairs(m):
        return c(m.reshape(2, 2, P, m.shape[-1]).transpose(0, 2, 1, 3).reshape(2, P, -1))

    def wide(g, u):
        m = np.stack([g, u]).reshape(2, NF, P, KD, P)
        return c(m.transpose(1, 4, 3, 0, 2).reshape(NF, P, KD * 2 * P))

    sgu = f["L1_attn_scales_gu"].reshape(2, NF, P, KD, 2)
    A, Bgu = f["L1_attn_lora_A_h"], f["L1_attn_lora_B_gu"]
    return {
        "x": rows(x2), "xT": rows(c(x2.T)), "ctx": rows(ctx2), "ctxT": rows(c(ctx2.T)),
        "wqkT": rows(wqkT.reshape(D, 4 * P)), "qk_b": c(qk_b.reshape(P, 4)),
        "wvT": rows(c(f["L0_attn_Wv_w"].T)), "v_b": f["L0_attn_Wv_b"][None],
        "wo0": np.concatenate([f["L0_attn_Wo_w"].T, f["L0_attn_Wo_b"][None]]),
        "w0T": rows(c(f["L0_ffn_W"].T)), "agT": rows(np.concatenate([f["L0_ffn_A"].T, f["L0_ffn_gate_w"].T], 1)),
        "bT0": np.concatenate([f["L0_ffn_B"].T, f["L0_ffn_b"][None]]), "g_b": f["L0_ffn_gate_b"][None],
        "c_qkv": np.concatenate([pairs(ca[m]) for m in range(3)]), "c_o": pairs(c(ca[3].T)),
        "s_qkv": c(sa[:3].reshape(3, KD, P, NB).transpose(2, 0, 1, 3).reshape(P, -1)),
        "s_o": c(sa[3].T.reshape(2, 2, 2, D).transpose(0, 2, 1, 3).reshape(2, 2, 2 * D)),
        "a_3": c(A[:3].reshape(3 * R1, D)), "bT_3": c(f["L1_attn_lora_B_attn"][:3].transpose(0, 2, 1).reshape(3 * R1, D)),
        "a_o": c(A[3]), "bT_o": c(f["L1_attn_lora_B_attn"][3].T), "a_g": c(A[4]), "a_u": c(A[5]),
        "bT_gu": c(Bgu.reshape(2, NF, P, R1).transpose(1, 3, 0, 2)), "a_d": c(f["L1_attn_lora_A_down"]), "bT_d": c(f["L1_attn_lora_B_down"].T),
        "c_gu": wide(f["L1_attn_codes_gu"][0], f["L1_attn_codes_gu"][1]),
        "s_gu": c(sgu.transpose(1, 4, 3, 0, 2).reshape(NF, 2, CH)),
        "c_dn": c(f["L1_attn_codes_down"].T.reshape(NF, P, D)), "s_dn": c(f["L1_attn_scales_down"].T.reshape(NF, 2, D)),
        "wqT1": rows(c(f["L1_xattn_Wq"].T)), "wkT1": rows(c(f["L1_xattn_Wk"].T)),
        "q_b": c(f["L1_xattn_bq"].reshape(KD, P).T), "k_b": c(f["L1_xattn_bk"].reshape(KD, P).T),
        "t_gu": wide(f["L1_ffn_gate_t"], f["L1_ffn_up_t"]),
        "ts_gu": c(np.stack([f["L1_ffn_gate_s"], f["L1_ffn_up_s"]], 1).reshape(NF, P, 2)),
        "t_dn": c(f["L1_ffn_down_t"].T.reshape(NF, P, D)), "ds": f["L1_ffn_down_s"][None],
    }


def kernel(**inputs):
    import concourse.bacc as bacc
    from concourse.bass_utils import run_bass_kernel_spmd

    nc = bacc.Bacc("TRN2", target_bir_lowering=False, num_devices=1)
    arrays, aps = {}, {}
    for name, a in layout(inputs).items():
        arrays[f"in_{name}"] = a
        aps[name] = nc.dram_tensor(f"in_{name}", a.shape, mybir.dt.from_np(a.dtype), kind="ExternalInput").ap()
    out = nc.dram_tensor("out", (NT, P, D), F32, kind="ExternalOutput").ap()
    decoder_kernel(nc, aps, out)
    r = run_bass_kernel_spmd(nc, [arrays], core_ids=[0])
    return r.results[0]["out"]
```

```python
from contextlib import ExitStack

import numpy as np
import concourse.bass as bass
from concourse import mybir

F32 = mybir.dt.float32
F32R = mybir.dt.float32r
I32 = mybir.dt.int32
ALU = mybir.AluOpType
ACT = mybir.ActivationFunctionType
AX = mybir.AxisListType

P = 128
NT = 8
T = NT * P
D = 512
KD = D // P
FF = 1792
NF = FF // P
HEADS, HD = 8, 8
NQ = 4
QR = P // NQ
RANKS = (8, 16, 32, 64)
RMAX = RANKS[-1]
NR = len(RANKS)
R1 = 16
RG = 2 * R1
O_ROW = 64
DT = -(-NF // 3)
DQ_ROWS = 2 * QR + R1
BLOCK = 64
NB = D // BLOCK
CH = 512
RING = 4
TG = T // 512
LN_EPS = 1e-5

NF4 = np.array([-1.0, -0.6961928009986877, -0.5250730514526367, -0.39491748809814453,
                -0.28444138169288635, -0.18477343022823334, -0.09105003625154495, 0.0,
                0.07958029955625534, 0.16093020141124725, 0.24611230194568634, 0.33791524171829224,
                0.44070982933044434, 0.5626170039176941, 0.7229568362236023, 1.0], np.float32)


def _lines():
    def near(v, n):
        out, up, down = [v], v, v
        for _ in range(n):
            up, down = np.nextafter(up, np.float32(np.inf)), np.nextafter(down, np.float32(-np.inf))
            out += [up, down]
        return out

    lines = []
    for pair in range(len(NF4) // 2):
        lo, hi = 2 * pair, 2 * pair + 1
        y = {lo: float(NF4[lo]), hi: float(NF4[hi])}
        slope = np.float32(y[hi] - y[lo])
        offset = np.float32(y[lo] - lo * float(slope))
        best = None
        for a in near(slope, 12):
            for b in near(offset, 6):
                worst = 0.0
                for c in (lo, hi):
                    fused = np.float32(float(a) * c + float(b))
                    twice = np.float32(np.float32(a * np.float32(c)) + b)
                    worst = max([worst] + [abs(float(v) - y[c]) / max(abs(y[c]), 0.05) for v in (fused, twice)])
                if best is None or worst < best[0]:
                    best = (worst, float(a), float(b))
        lines.append(best[1:])
    return lines


LINES = _lines()
ACT_LINES = ((1, 1), (5, 2), (2, 3), (3, 5), (0, 7), (4, 7))
POOL_LINES = ((6, 4), (7, 6))
DQ = 7

C_QKV, C_O = 0, 3 * KD
C_DN = C_O + KD
C_GU = C_DN + NF
C_END = C_GU + 2 * NF


def decoder_kernel(nc, i, out):
    ctx = ExitStack()
    with ctx:
        def sb(name, shape, dt=F32):
            return ctx.enter_context(nc.sbuf_tensor(name, shape, dt))

        def sem(name):
            return ctx.enter_context(nc.semaphore(name))
        x = sb("x", [P, NT, D])
        xh = sb("xh", [P, KD, T], F32R)
        xl = sb("xl", [P, KD, T], F32R)
        line = sb("line", [P, 8, CH])
        codes = sb("codes", [P, RING, CH], I32)
        scales = sb("scales", [P, RING, CH])
        wst = sb("wst", [P, CH])
        wh = sb("wh", [P, 2, 2 * CH], F32R)
        wl = sb("wl", [P, 2, 2 * CH], F32R)
        b_gu = sb("b_gu", [3 * RG, 2, 2 * P])
        b_st = sb("b_st", [3 * RG, 2, 2 * P], F32R)
        ah = sb("ah", [P, KD, 3 * RG], F32R)
        al = sb("al", [P, KD, 3 * RG], F32R)
        th = sb("th", [3 * RG, T], F32R)
        ff_s = sb("ff_s", [P, 2, 2])
        arena = sb("arena", [P, NF * T])
        fold = sb("fold", [P, NF, D])
        rbuf = sb("rbuf", [P, 2, D])
        ident = sb("ident", [P, P])
        st = sb("st", [P, 2, 6])
        mv = sb("mv", [P, 2, 2])
        rstd = sb("rstd", [P, 2, 2])
        minus_half = sb("minus_half", [P, 1])
        small = sb("small", [P, 2, 32])
        gate_v = sb("gate_v", [P, 2, 16])
        lm = sb("lm", [P, 2, RMAX])
        lmT = sb("lmT", [P, 2, P])
        probT = lmT
        prob = sb("prob", [P, 2, P])
        s_qkv = sb("s_qkv", [P, 3 * KD * NB])
        qk_b = sb("qk_b", [P, 4])
        v_b = sb("v_b", [P, HEADS * HD])
        g_b = sb("g_b", [P, NR])
        q_b = sb("q_b", [P, KD])
        k_b = sb("k_b", [P, KD])
        ds = sb("ds", [P, D])
        lora_r = ds[0:O_ROW + R1, :]

        hT = arena[:, :].rearrange("p (f t) -> p f t", f=NF)

        def carve(memory, start, n):
            return memory[:, start:start + n], start + n

        at = 0
        wsum, at = carve(arena, at, KD * D)
        woT, at = carve(arena, at, KD * D)
        shared, at = carve(arena, at, KD * D)
        xT_at = at
        xT, at = carve(arena, at, KD * T)
        wvT, at = carve(arena, at, KD * 64)
        wo0, at = carve(arena, at, D)
        agT, at = carve(arena, at, KD * (RMAX + NR))
        bT0, at = carve(arena, at, D)
        ctxT_r, at = carve(arena, at, 2 * D)
        bT_d, at = carve(arena, at, D)
        a_d, at = carve(arena, at, DT * P)
        assert at <= NF * T
        wsum, woT, shared, xT, wvT, agT = (m.rearrange("p (j c) -> p j c", j=KD) for m in (wsum, woT, shared, xT, wvT, agT))
        wqkT = w0T = mT = shared
        ctxT_r = ctxT_r.rearrange("p (s j c) -> p s j c", s=2, j=KD)
        lora_l = wo0[0:O_ROW + R1, :]
        CTXT_F, WQ_F, CTX_F = KD, KD + 2, NF
        ctxT1, at = carve(arena, 0, KD * T)
        wqT1, at = carve(arena, at, KD * D)
        assert at == xT_at and at <= WQ_F * T
        ctx1, at = carve(arena, xT_at + KD * T, NT * D)
        assert at <= NF * T
        ctxT1, wqT1 = (m.rearrange("p (j c) -> p j c", j=KD) for m in (ctxT1, wqT1))
        ctx1 = ctx1.rearrange("p (b c) -> p b c", b=NT)
        wkT1 = scales[:, :, :].rearrange("p s c -> p (s c)").rearrange("p (j c) -> p j c", j=KD)
        qT1 = line[:, :, :].rearrange("p l c -> p (l c)").rearrange("p (j t) -> p j t", j=KD)
        fold_flat = fold[:, :, :].rearrange("p f c -> p (f c)")
        kT1 = fold_flat[:, 0:KD * T].rearrange("p (j t) -> p j t", j=KD)
        at = 0
        qk, at = carve(fold_flat, at, 2 * 4 * P)
        q_aug, at = carve(fold_flat, at, 2 * P)
        mz, at = carve(fold_flat, at, 2 * P)
        pT, at = carve(fold_flat, at, 2 * HEADS * P)
        v1, at = carve(fold_flat, at, 2 * HEADS * (HD + 1))
        att, at = carve(fold_flat, at, 2 * 64)
        attT, at = carve(fold_flat, at, 2 * P)
        qk = qk.rearrange("p (s c t) -> p s c t", s=2, c=4)
        q_aug = q_aug.rearrange("p (a t) -> p a t", a=2)
        mz = mz.rearrange("p (a c) -> p a c", a=2)
        pT = pT.rearrange("p (s j a t) -> p s j a t", s=2, j=NQ, a=2)
        v1 = v1.rearrange("p (s h e) -> p s h e", s=2, h=HEADS)
        att = att.rearrange("p (s c) -> p s c", s=2)
        attT = attT.rearrange("p (s t) -> p s t", s=2)
        AGU_F, CTX_SLOT = NF - 3, NF - 2
        assert at <= AGU_F * D
        aT_gu = fold[:, AGU_F, 0:KD * 3 * RG].rearrange("p (j c) -> p j c", j=KD)
        ctx_r = fold[:, CTX_SLOT:NF, :]

        bank = [ctx.enter_context(nc.psum_tensor(f"bank{n}", [P, 512], F32)) for n in range(2)]
        heads_ps = ctx.enter_context(nc.psum_tensor("bank2345", [P, 4, 512], F32))
        bank += [heads_ps[:, n, :] for n in range(4)]
        bank += [ctx.enter_context(nc.psum_tensor(f"bank{n}", [P, 512], F32)) for n in (6, 7)]

        def gate_bank(s, tg):
            return bank[4 * s + tg][:, :]

        def up_bank(s, tg):
            return bank[4 * s + TG + tg][:, :]

        in_x = [sem(f"in_x{n}") for n in range(4)]
        in_qk, in_v, in_bias, in_xn, in_wo0 = sem("in_qk"), sem("in_v"), sem("in_bias"), sem("in_xn"), sem("in_wo0")
        in_ffn0, in_lora, in_agu = sem("in_ffn0"), sem("in_lora"), sem("in_agu")
        in_ctx = [sem(f"in_ctx{n}") for n in range(2)]
        in_codes = [sem(f"in_codes{n}") for n in range(RING)]
        in_gu = [sem(f"in_gu{n}") for n in range(2)]
        in_ctx1, in_ctxT1, in_wk, in_wq, in_ds = sem("in_xctx"), sem("in_xctxT"), sem("in_wk"), sem("in_wq"), sem("in_ds")
        in_tgu = [sem(f"in_tgu{n}") for n in range(2)]
        in_tdn = [sem(f"in_tdn{n}") for n in range(2)]
        consts = sem("consts")
        ident_ready = sem("ident_ready")
        dve_step = sem("dve_step")
        pool_step = sem("pool_step")
        act_lines, pool_lines, joined, scaled = sem("act_lines"), sem("pool_lines"), sem("joined"), sem("scaled")
        hi_ready, w_ready = sem("hi_ready"), sem("w_ready")
        b_hi, b_ready = sem("b_hi"), sem("b_ready")
        a_hi, a_ready, t_ps, t_hi, t_ready = sem("a_hi"), sem("a_ready"), sem("t_ps"), sem("t_hi"), sem("t_ready")
        fold_ready, fold_kept = sem("fold_ready"), sem("fold_kept")
        ln_stats, ln_rstd, ln_sum, ln_done = sem("ln_stats"), sem("ln_rstd"), sem("ln_sum"), sem("ln_done")
        xt_ps, xt_ready, xl_ready = sem("xt_ps"), sem("xt_ready"), sem("xl_ready")
        qkv_ps, qk_ready, v_ready = sem("qkv_ps"), sem("qk_ready"), sem("v_ready")
        s_ps, max_ready, max_ps, aug_ready, sT_ps, p_ready = (sem(n) for n in ("s_ps", "max_ready", "max_ps", "aug_ready", "sT_ps", "p_ready"))
        pv_ps, att_ready, attT_ps, attT_ready, o_ps = (sem(n) for n in ("pv_ps", "att_ready", "attT_ps", "attT_ready", "o_ps"))
        sim_ps, sim_max, sim_exp, sim_p, cx_ps = (sem(n) for n in ("sim_ps", "sim_max", "sim_exp", "sim_p", "cx_ps"))
        ag_ps, lm_ready, lm_ps, lmT_ready, f0_ps = (sem(n) for n in ("ag_ps", "lm_ready", "lm_ps", "lmT_ready", "f0_ps"))
        af_ps, af_added, m_ps, m_ready, x1_ps, x1_ready, x1_sum = (sem(n) for n in ("af_ps", "af_added", "m_ps", "m_ready", "x1_ps", "x1_ready", "x1_sum"))
        gate_ps, up_ps, sil_ready, h_ready = (sem(n) for n in ("gate_ps", "up_ps", "sil_ready", "h_ready"))
        dn_hi, dn_ready, hu_used, d_ps = sem("dn_hi"), sem("dn_ready"), sem("hu_used"), sem("d_ps")
        pj_ps, pj_ready = sem("pj_ps"), sem("pj_ready")
        x_ps, x_max, x_exp, xpT_ps, xpT_ready, xo_ps = (sem(n) for n in ("x_ps", "x_max", "x_exp", "xpT_ps", "xpT_ready", "xo_ps"))
        t_cast, t_gate_ps, t_up_ps, t_sil, t_h = (sem(n) for n in ("t_cast", "t_gate_ps", "t_up_ps", "t_sil", "t_h"))
        t_dcast, t_dhi, t_dlo, t_used, t_d_ps = (sem(n) for n in ("t_dcast", "t_dhi", "t_dlo", "t_used", "t_d_ps"))
        out_done = sem("out_done")
        pool_seen, sp_seen = sem("pool_seen"), sem("sp_seen")

        block = ctx.enter_context(nc.Block())

        def chunk_dmas(c):
            return 1 if c < C_O else 3

        def codes_landed(eng, c):
            eng.wait_ge(in_codes[c % RING], 16 * sum(chunk_dmas(n) for n in range(c % RING, c + 1, RING)))

        def gu_slot(s):
            return (C_GU + 2 * s) % RING

        @block.sync
        def _(sp):
            sp.dma_start(wqkT, i["wqkT"]).then_inc(in_qk, 16)
            for n in range(4):
                sp.dma_start(xT[:, :, 2 * n * P:2 * (n + 1) * P], i["xT"][:, :, 2 * n * P:2 * (n + 1) * P]).then_inc(in_x[n], 16)
                if n == 0:
                    sp.dma_start(wvT, i["wvT"]).then_inc(in_v, 16)
                    sp.dma_start(qk_b[:, :], i["qk_b"]).then_inc(in_bias, 16)
                    sp.dma_start(v_b[:, :], i["v_b"].partition_broadcast(P)).then_inc(in_bias, 16)
                    sp.dma_start(g_b[:, :], i["g_b"].partition_broadcast(P)).then_inc(in_bias, 16)
                    sp.dma_start(s_qkv[:, :], i["s_qkv"]).then_inc(in_bias, 16)
                    sp.dma_start(q_b[:, :], i["q_b"]).then_inc(in_bias, 16)
                    sp.dma_start(k_b[:, :], i["k_b"]).then_inc(in_bias, 16)
                    for c in range(RING):
                        sp.dma_start(codes[:, c, :], i["c_qkv"][c]).then_inc(in_codes[c], 16)
            sp.dma_start(x[:, :, :], i["x"]).then_inc(in_xn, 16)
            sp.dma_start(wo0[0:65, :], i["wo0"]).then_inc(in_wo0, 16)
            sp.dma_start(aT_gu, i["aT_gu"]).then_inc(in_agu, 16)
            for n in range(2):
                sp.dma_start(ctx_r[:, n, :], i["ctx"][:, n, :]).then_inc(in_ctx[n], 16)
                sp.dma_start(ctxT_r[:, n, :, :], i["ctxT"][:, :, n * P:(n + 1) * P]).then_inc(in_ctx[n], 16)
            sp.dma_start(agT, i["agT"]).then_inc(in_ffn0, 16)
            sp.dma_start(bT0[0:RMAX + 1, :], i["bT0"]).then_inc(in_ffn0, 16)
            for dst, name in ((a_d[0:DQ_ROWS, :], "a_d"), (bT_d[0:DQ_ROWS, :], "bT_d"), (lora_r, "lora_r")):
                sp.dma_start(dst, i[name]).then_inc(in_lora, 16)

            def slot_free(c):
                for done, n in ((act_lines, len(ACT_LINES)),
                                (pool_lines, len(POOL_LINES)),
                                (scaled, 1)):
                    sp.wait_ge(done, n * (c - RING + 1))
                    if not isinstance(c, int):
                        sp.sem_inc(sp_seen, 1)

            def scales_of(dst, src):
                for half in range(2):
                    yield dst[half * BLOCK:(half + 1) * BLOCK], src(half)

            def load_chunk(c):
                slot_free(c)
                done = in_codes[c % RING]
                if c < C_O:
                    sp.dma_start(codes[:, c % RING, :], i["c_qkv"][c]).then_inc(done, 16)
                else:
                    what, n = ("o", c - C_O) if c < C_DN else ("dn", c - C_DN)
                    sp.dma_start(codes[:, c % RING, :], i["c_" + what][n]).then_inc(done, 16)
                    for dst, s_src in scales_of(scales[:, c % RING, :], lambda half: i["s_" + what][n, half:half + 1, :]):
                        sp.dma_start(dst, s_src.partition_broadcast(BLOCK)).then_inc(done, 16)

            for c in range(RING, C_DN + 2):
                load_chunk(c)
            sp.wait_ge(qkv_ps, NT)
            sp.dma_start(w0T, i["w0T"]).then_inc(in_ffn0, 16)
            sp.wait_ge(o_ps, NT)
            sp.dma_start(lora_l, i["lora_l"]).then_inc(in_lora, 16)

            for b in range(2, NT):
                load_chunk(C_DN + b)
                sp.wait_ge(cx_ps, b - 1)
                sp.dma_start(ctx_r[:, b % 2, :], i["ctx"][:, b, :]).then_inc(in_ctx[b % 2], 16)
                sp.dma_start(ctxT_r[:, b % 2, :, :], i["ctxT"][:, :, b * P:(b + 1) * P]).then_inc(in_ctx[b % 2], 16)
            for c in range(C_DN + NT, C_GU):
                load_chunk(c)

            with sp.Fori(0, NF // 2) as n:
                for s in range(2):
                    j = 2 * n + s
                    slots = slice(gu_slot(s), gu_slot(s) + 2)
                    slot_free(C_GU + 1 + 2 * j)
                    sp.wait_ge(b_ready, j + 1)
                    sp.sem_inc(sp_seen, 1)
                    sp.dma_start(codes[:, slots, :].rearrange("p s c -> p (s c)"),
                                 i["c_gu"][bass.ds(j, 1), :, :].rearrange("o p c -> (o p) c")).then_inc(in_gu[s], 16)
                    for half in range(2):
                        sp.dma_start(scales[half * BLOCK:(half + 1) * BLOCK, slots, :].rearrange("p s c -> p (s c)"),
                                     i["s_gu"][bass.ds(j, 1), half, :].partition_broadcast(BLOCK).rearrange("p o c -> p (o c)")).then_inc(in_gu[s], 16)
                    sp.dma_start(b_gu[:, s, :], i["b_gu"][bass.ds(j, 1), :, :].rearrange("o r c -> (o r) c")).then_inc(in_gu[s], 16)

            sp.wait_ge(af_ps, 2 * KD)
            sp.dma_start(ds[:, :], i["ds"].partition_broadcast(P)).then_inc(in_ds, 16)
            sp.wait_ge(scaled, C_END)
            sp.dma_start(wkT1, i["wkT1"]).then_inc(in_wk, 16)
            for used, dst, name, done in ((CTXT_F, ctxT1, "ctxT", in_ctxT1), (WQ_F, wqT1, "wqT1", in_wq), (CTX_F, ctx1, "ctx", in_ctx1)):
                sp.wait_ge(dn_ready, used)
                sp.dma_start(dst, i[name]).then_inc(done, 16)

            sp.wait_ge(act_lines, len(ACT_LINES) * C_END)
            sp.wait_ge(pool_lines, len(POOL_LINES) * C_END)
            with sp.Fori(0, NF // 2) as n:
                for s in range(2):
                    j = 2 * n + s
                    sp.wait_ge(t_h, 2 * j + 2)
                    sp.sem_inc(sp_seen, 1)
                    sp.wait_ge(t_cast, j + 1)
                    sp.sem_inc(sp_seen, 1)
                    sp.dma_start(codes[:, 2 * s:2 * s + 2, :].rearrange("p s c -> p (s c)"),
                                 i["t_gu"][bass.ds(j, 1), :, :].rearrange("o p c -> (o p) c")).then_inc(in_tgu[s], 16)
                    sp.dma_start(ff_s[:, s, :], i["ts_gu"][bass.ds(j, 1), :, :].rearrange("o p c -> (o p) c")).then_inc(in_tgu[s], 16)
            sp.wait_ge(t_cast, NF + 2)
            with sp.Fori(0, NF // 2) as n:
                for s in range(2):
                    j = 2 * n + s
                    sp.wait_ge(t_dcast, j + 1)
                    sp.sem_inc(sp_seen, 1)
                    sp.dma_start(codes[:, s, :], i["t_dn"][bass.ds(j, 1), :, :].rearrange("o p c -> (o p) c")).then_inc(in_tdn[s], 16)

            for b in range(NT):
                sp.wait_ge(ln_done, 5 * NT + b + 1)
                sp.dma_start(out[b, :, :], x[:, b, :]).then_inc(out_done, 16)
            sp.wait_ge(out_done, 16 * NT)

        @block.tensor
        def _(pe):
            def transpose_tile(b, src, dst):
                for k in range(KD):
                    last = pe.transpose(dst[:, k * P:(k + 1) * P], src[:, k * P:(k + 1) * P], ident[:, :])
                last.then_inc(xt_ps, 1)

            def qkv(b):
                if b == 0:
                    pe.wait_ge(in_qk, 16)
                    pe.wait_ge(in_v, 16)
                if b % 2 == 0:
                    pe.wait_ge(in_x[b // 2], 16)
                if b >= 1:
                    pe.wait_ge(qk_ready, b)
                    pe.wait_ge(v_ready, b)
                if b >= 2:
                    pe.wait_ge(att_ready, b - 1)
                t = slice(b * P, (b + 1) * P)
                for c in range(4):
                    for k in range(KD):
                        pe.matmul(bank[0][:, c * P:(c + 1) * P], wqkT[:, k, c * P:(c + 1) * P], xT[:, k, t],
                                  start=(k == 0), stop=(k == KD - 1))
                for k in range(KD):
                    last = pe.matmul(bank[1][:, 0:64], xT[:, k, t], wvT[:, k, :], start=(k == 0), stop=(k == KD - 1))
                last.then_inc(qkv_ps, 1)

            def scores(b):
                pe.wait_ge(qk_ready, b + 1)
                if b >= 1:
                    pe.wait_ge(p_ready, b)
                for a in range(2):
                    for j in range(NQ):
                        q = slice(QR * j, QR * (j + 1))
                        last = pe.matmul(bank[2 + j][:, a * P:(a + 1) * P], qk[q, b % 2, a, :], qk[q, b % 2, 2 + a, :],
                                         start=True, stop=True)
                last.then_inc(s_ps, 1)

            def max_rows(b):
                pe.wait_ge(max_ready, b + 1)
                if b >= 2:
                    pe.wait_ge(ln_sum, b - 1)
                for a in range(2):
                    last = pe.transpose(bank[7][:, a * P:(a + 1) * P], mz[:, a, :], ident[:, :])
                last.then_inc(max_ps, 1)

            def scores_T(b):
                pe.wait_ge(aug_ready, b + 1)
                for a in range(2):
                    for j in range(NQ):
                        q = slice(QR * j, QR * (j + 1))
                        last = pe.matmul(bank[2 + j][:, a * P:(a + 1) * P], qk[q, b % 2, 2 + a, :], q_aug[q, a, :],
                                         start=True, stop=True)
                last.then_inc(sT_ps, 1)

            def heads_out(b):
                pe.wait_ge(p_ready, b + 1)
                pe.wait_ge(v_ready, min(b + 2, NT))
                for h in range(HEADS):
                    last = pe.matmul(bank[1][:, h * (HD + 1):(h + 1) * (HD + 1)], pT[:, b % 2, h % NQ, h // NQ, :],
                                     v1[:, b % 2, h, :], start=True, stop=True)
                last.then_inc(pv_ps, 1)

            def heads_T(b):
                pe.wait_ge(att_ready, b + 1)
                if b >= 1:
                    pe.wait_ge(xt_ready, b)
                pe.transpose(bank[6][0:64, 0:P], att[:, b % 2, :], ident[:, :]).then_inc(attT_ps, 1)

            def o_proj(b):
                pe.wait_ge(attT_ready, b + 1)
                if b == 0:
                    pe.wait_ge(in_wo0, 16)
                pe.matmul(bank[7][:, :], attT[0:65, b % 2, :], wo0[0:65, :], start=True, stop=True).then_inc(o_ps, 1)

            def x_T(layer, b):
                pe.wait_ge(ln_done, layer * NT + b + 1)
                if layer:
                    pe.wait_ge(xt_ready, layer * NT + b)
                transpose_tile(b, x[:, b, :], bank[6])

            pe.wait_ge(ident_ready, 1)
            qkv(0)
            for t in range(NT + 2):
                if t < NT:
                    scores(t)
                if t >= 2:
                    pe.wait_ge(attT_ready, t - 1)
                    x_T(0, t - 2)
                if t + 1 < NT:
                    qkv(t + 1)
                if t < NT:
                    max_rows(t)
                if 1 <= t <= NT:
                    heads_T(t - 1)
                if t < NT:
                    scores_T(t)
                if 1 <= t <= NT:
                    o_proj(t - 1)
                if t < NT:
                    heads_out(t)

            def sims(b):
                pe.wait_ge(xt_ready, b + 1)
                pe.wait_ge(in_ctx[b % 2], 32 * (b // 2 + 1))
                if b >= 2:
                    pe.wait_ge(sim_exp, b - 1)
                for k in range(KD):
                    last = pe.matmul(bank[2 + b % 2][:, 0:P], xT[:, k, b * P:(b + 1) * P], ctxT_r[:, b % 2, k, :],
                                     start=(k == 0), stop=(k == KD - 1))
                last.then_inc(sim_ps, 1)

            def context(b):
                pe.wait_ge(sim_p, b + 1)
                if b >= 2:
                    pe.wait_ge(ln_sum, NT + b - 1)
                pe.matmul(bank[4 + b % 2][:, :], prob[:, b % 2, :], ctx_r[:, b % 2, :], start=True, stop=True).then_inc(cx_ps, 1)

            for t in range(NT + 2):
                if t < NT:
                    sims(t)
                if t >= 2:
                    x_T(1, t - 2)
                if 1 <= t <= NT:
                    context(t - 1)

            def ranks(b):
                pe.wait_ge(xt_ready, NT + b + 1)
                if b == 0:
                    pe.wait_ge(in_ffn0, 48)
                if b >= 2:
                    pe.wait_ge(lm_ready, b - 1)
                for k in range(KD):
                    last = pe.matmul(bank[b % 2][:, 0:RMAX + NR], xT[:, k, b * P:(b + 1) * P], agT[:, k, :],
                                     start=(k == 0), stop=(k == KD - 1))
                last.then_inc(ag_ps, 1)
                if b >= 2:
                    pe.wait_ge(ln_sum, 2 * NT + b - 1)
                for k in range(KD):
                    pe.matmul(bank[2 + b % 2][:, :], xT[:, k, b * P:(b + 1) * P], w0T[:, k, :], start=(k == 0), stop=False)

            def lora_T(b):
                pe.wait_ge(lm_ready, b + 1)
                if b >= 1:
                    pe.wait_ge(lmT_ready, b)
                pe.transpose(bank[7][0:RMAX, 0:P], lm[:, b % 2, :], ident[:, :]).then_inc(lm_ps, 1)

            def lora_out(b):
                pe.wait_ge(lmT_ready, b + 1)
                pe.matmul(bank[2 + b % 2][:, :], lmT[0:RMAX + 1, b % 2, :], bT0[0:RMAX + 1, :], start=False, stop=True).then_inc(f0_ps, 1)

            for t in range(NT + 2):
                if t < NT:
                    ranks(t)
                if t >= 2:
                    x_T(2, t - 2)
                if 1 <= t <= NT:
                    lora_T(t - 1)
                    lora_out(t - 1)

            pe.wait_ge(in_lora, 16 * 4)
            for n in range(2 * KD):
                j = n % KD
                if n >= 2:
                    pe.wait_ge(af_added, n - 1)
                rows = slice(0, 3 * R1) if n < KD else slice(O_ROW, O_ROW + R1)
                pe.matmul(bank[n % 2][:, :], lora_l[rows, j * P:(j + 1) * P], lora_r[rows, :], start=True, stop=True).then_inc(af_ps, 1)
            pe.wait_ge(af_added, 2 * KD)
            pe.wait_ge(ln_sum, 3 * NT)
            for c in range(KD):
                for j in range(KD):
                    last = pe.matmul(bank[2 + c][:, :], wsum[:, j, c * P:(c + 1) * P], woT[:, j, :], start=(j == 0), stop=(j == KD - 1))
                last.then_inc(m_ps, 1)
            pe.wait_ge(m_ready, KD)

            def down_lora(j):
                if j >= 2:
                    pe.wait_ge(fold_kept, j - 1)
                rows = slice(QR * (j // DT), QR * (j // DT) + R1)
                pe.matmul(bank[4 + j % 2][:, :], a_d[rows, (j % DT) * P:(j % DT + 1) * P], bT_d[rows, :],
                          start=True, stop=True).then_inc(fold_ready, 1)

            for t in range(NT + 1):
                if t < NT:
                    pe.wait_ge(xt_ready, 2 * NT + t + 1)
                    if t >= 2:
                        pe.wait_ge(x1_ready, t - 1)
                    for k in range(KD):
                        last = pe.matmul(bank[t % 2][:, :], xT[:, k, t * P:(t + 1) * P], mT[:, k, :], start=(k == 0), stop=(k == KD - 1))
                    last.then_inc(x1_ps, 1)
                if t >= 1:
                    pe.wait_ge(x1_ready, t)
                    pe.wait_ge(xt_ready, 3 * NT)
                    if t >= 2:
                        pe.wait_ge(xl_ready, t - 1)
                    transpose_tile(t - 1, rbuf[:, (t - 1) % 2, :], bank[6])
                for j in range(2 * t, min(2 * t + 2, NF)):
                    down_lora(j)

            pe.wait_ge(a_ready, 1)
            pe.wait_ge(xl_ready, NT)
            for tg in range(TG):
                for k in range(KD):
                    for a, xs in ((ah, xh), (ah, xl), (al, xh)):
                        last = pe.matmul(bank[2 + tg][0:3 * RG, :], a[:, k, :], xs[:, k, tg * 512:(tg + 1) * 512],
                                         start=(k == 0 and a is ah and xs is xh), stop=(k == KD - 1 and a is al))
                last.then_inc(t_ps, 1)

            def gu_tile(s, j):
                pe.wait_ge(w_ready, 2 * j + 2)
                pe.wait_ge(b_ready, j + 3)
                for tg in range(TG):
                    cols = slice(tg * 512, (tg + 1) * 512)
                    pe.wait_ge(h_ready, 2 * j + tg + 1)
                    for g, dst, done in ((0, gate_bank(s, tg), gate_ps), (1, up_bank(s, tg), up_ps)):
                        for k in range(KD):
                            c = (2 * k + g) * P
                            pe.matmul(dst, wh[:, s, c:c + P], xh[:, k, cols], start=(k == 0), stop=False)
                            pe.matmul(dst, wh[:, s, c:c + P], xl[:, k, cols], start=False, stop=False)
                            pe.matmul(dst, wl[:, s, c:c + P], xh[:, k, cols], start=False, stop=False)
                        pe.matmul(dst, b_st[:, s, g * P:(g + 1) * P], th[:, cols], start=False, stop=True).then_inc(done, 1)

            pe.wait_ge(t_ready, TG)
            pe.wait_ge(fold_kept, NF)
            with pe.Fori(0, NF // 2) as n:
                for s in range(2):
                    gu_tile(s, 2 * n + s)

            def down_tile(s, w_sem, w_n, parts, first, last_one, done):
                pe.wait_ge(w_sem, w_n)
                for b in range(NT):
                    for p, (h, wp) in enumerate(parts):
                        last = pe.matmul(bank[b][:, :], h[:, s, b * P:(b + 1) * P], wp[:, s, 0:D],
                                         start=first and p == 0, stop=last_one and p == len(parts) - 1)
                last.then_inc(done, 1)

            def down(w_sem, parts, used, done):
                down_tile(0, w_sem, 1, parts, True, False, used)
                down_tile(1, w_sem, 2, parts, False, False, used)
                with pe.Fori(1, NF // 2 - 1) as n:
                    for s in range(2):
                        down_tile(s, w_sem, 2 * n + s + 1, parts, False, False, used)
                down_tile(0, w_sem, NF - 1, parts, False, False, used)
                down_tile(1, w_sem, NF, parts, False, True, done)

            pe.wait_ge(h_ready, 2 * NF + 4)
            down(dn_ready, ((xh, wh), (xh, wl), (xl, wh)), hu_used, d_ps)

            def project(wT, src, m):
                c, tg = (m % (KD * TG)) // TG, m % TG
                if m < 4:
                    pe.wait_ge(ln_sum, 3 * NT + m + 1)
                else:
                    pe.wait_ge(pj_ready, m - 3)
                for k in range(KD):
                    last = pe.matmul(bank[m % 4][:, :], wT[:, k, c * P:(c + 1) * P], src[:, k, tg * 512:(tg + 1) * 512],
                                     start=(k == 0), stop=(k == KD - 1))
                last.then_inc(pj_ps, 1)

            def x2_T(b):
                pe.wait_ge(ln_done, 3 * NT + b + 1)
                if b < 4:
                    pe.wait_ge(ln_sum, 3 * NT + 4 + b + 1)
                else:
                    pe.wait_ge(xt_ready, 4 * NT + b - 3)
                transpose_tile(b, x[:, b, :], bank[4 + b % 4])

            pe.wait_ge(in_ctxT1, 16)
            pe.wait_ge(in_wk, 16)
            for m in range(4):
                project(wkT1, ctxT1, m)
            for b in range(4):
                x2_T(b)
            for m in range(4, KD * TG):
                project(wkT1, ctxT1, m)
                x2_T(m)
            pe.wait_ge(xt_ready, 5 * NT)
            pe.wait_ge(in_wq, 16)
            for m in range(KD * TG, 2 * KD * TG):
                project(wqT1, xT, m)
            pe.wait_ge(pj_ready, 2 * KD * TG)

            def x_scores(b):
                if b >= 2:
                    pe.wait_ge(x_exp, b - 1)
                for k in range(KD):
                    last = pe.matmul(bank[4 + b % 2][:, 0:P], qT1[:, k, b * P:(b + 1) * P], kT1[:, k, b * P:(b + 1) * P],
                                     start=(k == 0), stop=(k == KD - 1))
                last.then_inc(x_ps, 1)

            def x_probT(b):
                pe.wait_ge(x_exp, b + 1)
                if b >= 2:
                    pe.wait_ge(xpT_ready, b - 1)
                pe.transpose(bank[2 + b % 2][:, 0:P], prob[:, b % 2, :], ident[:, :]).then_inc(xpT_ps, 1)

            def x_out(b):
                pe.wait_ge(xpT_ready, b + 1)
                if b == 0:
                    pe.wait_ge(in_ctx1, 16)
                if b >= 2:
                    pe.wait_ge(ln_sum, 4 * NT + b - 1)
                pe.matmul(bank[b % 2][:, :], probT[:, b % 2, :], ctx1[:, b, :], start=True, stop=True).then_inc(xo_ps, 1)

            for t in range(NT + 2):
                if t < NT:
                    x_scores(t)
                if t >= 2:
                    b = t - 2
                    pe.wait_ge(ln_done, 4 * NT + b + 1)
                    if b >= 1:
                        pe.wait_ge(xl_ready, NT + b)
                    transpose_tile(b, x[:, b, :], bank[6])
                if 1 <= t <= NT:
                    x_probT(t - 1)
                    x_out(t - 1)

            def t_gu_tile(s, j):
                pe.wait_ge(t_cast, j + 3)
                for tg in range(TG):
                    cols = slice(tg * 512, (tg + 1) * 512)
                    pe.wait_ge(t_h, 2 * j + tg + 1)
                    for g, dst, done in ((0, gate_bank(s, tg), t_gate_ps), (1, up_bank(s, tg), t_up_ps)):
                        for k in range(KD):
                            c = (2 * k + g) * P
                            pe.matmul(dst, wh[:, s, c:c + P], xh[:, k, cols], start=(k == 0), stop=False)
                            last = pe.matmul(dst, wh[:, s, c:c + P], xl[:, k, cols], start=False, stop=(k == KD - 1))
                        last.then_inc(done, 1)

            pe.wait_ge(ln_sum, 5 * NT)
            pe.wait_ge(xl_ready, 2 * NT)
            with pe.Fori(0, NF // 2) as n:
                for s in range(2):
                    t_gu_tile(s, 2 * n + s)
            pe.wait_ge(t_h, 2 * NF + 4)
            down(t_dlo, ((xh, wh), (xl, wh)), t_used, t_d_ps)

        @block.scalar
        def _(act):
            def lines(c, slot):
                for line_n, freed in ACT_LINES:
                    if not (isinstance(c, int) and c == 0):
                        act.wait_ge(joined, DQ * (c - 1) + freed)
                    a, b = LINES[line_n]
                    nc.scalar.activation(line[:, line_n, :], codes[:, slot, :], ACT.Copy, bias=b, scale=a).then_inc(act_lines, 1)

            def early_lines(c):
                codes_landed(act, c)
                lines(c, c % RING)

            def gu_lines(s, n, half):
                act.wait_ge(in_gu[s], 64 * (n + 1))
                lines(C_GU + 4 * n + 2 * s + half, gu_slot(s) + half)

            def x_T_out(m, n=6, dst=xT):
                act.wait_ge(xt_ps, m + 1)
                b = m % NT
                nc.scalar.activation(dst[:, :, b * P:(b + 1) * P], bank[n][:, :].rearrange("p (k t) -> p k t", k=KD),
                                     ACT.Copy).then_inc(xt_ready, 1)

            early_lines(0)
            for t in range(NT + 2):
                if t >= 2:
                    x_T_out(t - 2)
                if 1 <= t <= NT:
                    act.wait_ge(attT_ps, t)
                    if t == 1:
                        act.wait_ge(consts, 1)
                    if t >= 3:
                        act.wait_ge(o_ps, t - 2)
                    nc.scalar.activation(attT[0:64, (t - 1) % 2, :], bank[6][0:64, 0:P], ACT.Copy).then_inc(attT_ready, 1)
                if t < NT:
                    act.wait_ge(sT_ps, t + 1)
                    if t >= 2:
                        act.wait_ge(pv_ps, t - 1)
                    nc.scalar.activation(pT[:, t % 2, :, :, :].rearrange("p j a t -> p j (a t)"), heads_ps[:, :, 0:2 * P],
                                         ACT.Exp).then_inc(p_ready, 1)
                    early_lines(2 * t + 1)
                    early_lines(2 * t + 2)
                if t == 0:
                    act.wait_ge(in_agu, 16)
                    nc.scalar.activation(ah[:, :, :], aT_gu, ACT.Copy).then_inc(a_hi, 1)

            for t in range(NT + 2):
                if t < NT:
                    act.wait_ge(sim_max, t + 1)
                    nc.scalar.activation(prob[:, t % 2, :], bank[2 + t % 2][:, 0:P], ACT.Exp, bias=small[:, t % 2, 0:1],
                                         scale=float(P) ** -0.5, accum_out=small[:, t % 2, 1:2]).then_inc(sim_exp, 1)
                if t >= 2:
                    x_T_out(NT + t - 2)
                if t < NT:
                    early_lines(C_DN + t + 1)

            for t in range(NT + 2):
                if 1 <= t <= NT:
                    act.wait_ge(lm_ps, t)
                    if t >= 3:
                        act.wait_ge(f0_ps, t - 2)
                    nc.scalar.activation(lmT[0:RMAX, (t - 1) % 2, :], bank[7][0:RMAX, 0:P], ACT.Copy).then_inc(lmT_ready, 1)
                if t >= 2:
                    x_T_out(2 * NT + t - 2)
                if C_DN + NT + t + 1 < C_GU:
                    early_lines(C_DN + NT + t + 1)

            def gu_hi(s, chunk, half):
                act.wait_ge(scaled, chunk + 1)
                nc.scalar.activation(wh[:, s, half * CH:(half + 1) * CH], wst[:, :], ACT.Copy).then_inc(hi_ready, 1)

            def gu_lora_hi(s):
                nc.scalar.activation(b_st[:, s, :], b_gu[:, s, :], ACT.Copy).then_inc(b_hi, 1)

            gu_lines(0, 0, 0)
            gu_lines(0, 0, 1)
            gu_hi(0, C_GU, 0)
            for c in range(KD):
                act.wait_ge(m_ps, c + 1)
                nc.scalar.activation(mT[:, c, :], bank[2 + c][:, :], ACT.Copy, scale=1.0 / 3.0).then_inc(m_ready, 1)
            gu_lines(1, 0, 0)
            gu_hi(0, C_GU + 1, 1)
            gu_lora_hi(0)
            for b in range(NT):
                x_T_out(3 * NT + b, dst=xh)
            for tg in range(TG):
                act.wait_ge(t_ps, tg + 1)
                nc.scalar.activation(th[:, tg * 512:(tg + 1) * 512], bank[2 + tg][0:3 * RG, :], ACT.Copy).then_inc(t_hi, 1)

            def silu(s, j, tg):
                act.wait_ge(gate_ps, 2 * j + tg + 1)
                nc.scalar.activation(hT[:, bass.ds(j, 1), tg * 512:(tg + 1) * 512].rearrange("p o t -> p (o t)"),
                                     gate_bank(s, tg), ACT.Silu).then_inc(sil_ready, 1)

            def gu_step(s, j, n_next, n_after):
                gu_lines(1 - s, n_next, 1)
                silu(s, j, 0)
                act.wait_ge(up_ps, 2 * j + 2)
                gu_hi(1 - s, C_GU + 2 * j + 2, 0)
                if n_after is not None:
                    gu_lines(s, n_after, 0)
                silu(s, j, 1)
                gu_hi(1 - s, C_GU + 2 * j + 3, 1)
                gu_lora_hi(1 - s)

            with act.Fori(0, NF // 2 - 1) as n:
                gu_step(0, 2 * n, n, n + 1)
                gu_step(1, 2 * n + 1, n + 1, n + 1)
            gu_step(0, NF - 2, NF // 2 - 1, None)
            for tg in range(TG):
                silu(1, NF - 1, tg)

            def hidden_hi(s, j, done):
                nc.scalar.activation(xh[:, s, :], hT[:, bass.ds(j, 1), :].rearrange("p o t -> p (o t)"), ACT.Copy).then_inc(done, 1)

            def dn_hi_parts(s, j, used):
                if used is not None:
                    act.wait_ge(hu_used, used)
                hidden_hi(s, j, dn_hi)
                nc.scalar.activation(wh[:, s, 0:D], fold[:, bass.ds(j, 1), :].rearrange("p o c -> p (o c)"), ACT.Copy).then_inc(dn_hi, 1)

            act.wait_ge(up_ps, 2 * NF + 2)
            act.wait_ge(h_ready, 2 * NF + 4)
            dn_hi_parts(0, 0, None)
            dn_hi_parts(1, 1, None)
            with act.Fori(1, NF // 2) as n:
                for s in range(2):
                    dn_hi_parts(s, 2 * n + s, 2 * n + s - 1)

            def projected(m):
                act.wait_ge(pj_ps, m + 1)
                c, tg = (m % (KD * TG)) // TG, m % TG
                dst, bias = (kT1, k_b) if m < KD * TG else (qT1, q_b)
                nc.scalar.activation(dst[:, c, tg * 512:(tg + 1) * 512], bank[m % 4][:, :], ACT.Identity,
                                     bias=bias[:, c:c + 1]).then_inc(pj_ready, 1)

            for m in range(4):
                projected(m)
            for b in range(4):
                x_T_out(4 * NT + b, n=4 + b)
            for m in range(4, KD * TG):
                projected(m)
                x_T_out(4 * NT + m, n=4 + m % 4)
            for m in range(KD * TG, 2 * KD * TG):
                projected(m)
            for t in range(NT + 2):
                if t < NT:
                    act.wait_ge(x_max, t + 1)
                    if t >= 2:
                        act.wait_ge(xpT_ps, t - 1)
                    nc.scalar.activation(prob[:, t % 2, :], bank[4 + t % 2][:, 0:P], ACT.Exp, bias=small[:, t % 2, 0:1],
                                         scale=float(D) ** -0.5, accum_out=small[:, t % 2, 1:2]).then_inc(x_exp, 1)
                if t >= 2:
                    x_T_out(5 * NT + t - 2, dst=xh)
                if 1 <= t <= NT:
                    act.wait_ge(xpT_ps, t)
                    if t >= 3:
                        act.wait_ge(xo_ps, t - 2)
                    nc.scalar.activation(probT[:, (t - 1) % 2, :], bank[2 + (t - 1) % 2][:, 0:P], ACT.Copy).then_inc(xpT_ready, 1)

            def t_gu_cast(s, n, free):
                act.wait_ge(in_tgu[s], 32 * (n + 1))
                if free is not None:
                    act.wait_ge(t_up_ps, free)
                nc.scalar.activation(wh[:, s, :], codes[:, 2 * s:2 * s + 2, :].rearrange("p s c -> p (s c)"), ACT.Copy).then_inc(t_cast, 1)

            def t_silu(s, j):
                for tg in range(TG):
                    act.wait_ge(t_gate_ps, 2 * j + tg + 1)
                    nc.scalar.activation(hT[:, bass.ds(j, 1), tg * 512:(tg + 1) * 512].rearrange("p o t -> p (o t)"),
                                         gate_bank(s, tg), ACT.Silu, scale=ff_s[:, s, 0:1]).then_inc(t_sil, 1)

            t_gu_cast(0, 0, None)
            t_gu_cast(1, 0, None)
            with act.Fori(0, NF // 2 - 1) as n:
                t_silu(0, 2 * n)
                t_gu_cast(0, n + 1, 4 * n + 2)
                t_silu(1, 2 * n + 1)
                t_gu_cast(1, n + 1, 4 * n + 4)
            t_silu(0, NF - 2)
            t_silu(1, NF - 1)

            def t_dn(s, j, n, free):
                act.wait_ge(in_tdn[s], 16 * (n + 1))
                if free is not None:
                    act.wait_ge(t_used, free)
                nc.scalar.activation(wh[:, s, 0:D], codes[:, s, :], ACT.Copy).then_inc(t_dcast, 1)
                hidden_hi(s, j, t_dhi)

            act.wait_ge(t_up_ps, 2 * NF)
            act.wait_ge(t_h, 2 * NF + 4)
            t_dn(0, 0, 0, None)
            t_dn(1, 1, 0, None)
            with act.Fori(1, NF // 2) as n:
                for s in range(2):
                    t_dn(s, 2 * n + s, n, 2 * n + s - 1)

        @block.gpsimd
        def _(pool):
            steps = [0]

            def link(ins):
                steps[0] += 1
                ins.then_inc(pool_step, 1)
                pool.wait_ge(pool_step, steps[0])

            link(nc.gpsimd.memset(ident[:, :], 0.0))
            nc.gpsimd.affine_select(out=ident[:, :], in_=ident[:, :], compare_op=ALU.not_equal, fill=1.0, base=0,
                                    pattern=[[-1, P]], channel_multiplier=1).then_inc(ident_ready, 1)
            link(nc.gpsimd.memset(minus_half[:, :], -0.5))

            def lines(c, slot):
                for line_n, freed in POOL_LINES:
                    if not (isinstance(c, int) and c == 0):
                        pool.wait_ge(joined, DQ * (c - 1) + freed)
                    if not isinstance(c, int):
                        pool.sem_inc(pool_seen, 1)
                    a, b = LINES[line_n]
                    nc.gpsimd.tensor_scalar(line[:, line_n, :], codes[:, slot, :], a, b, ALU.mult, ALU.add).then_inc(pool_lines, 1)

            def early_lines(c):
                codes_landed(pool, c)
                lines(c, c % RING)

            def rstd_of(m):
                pool.wait_ge(ln_stats, m + 1)
                link(nc.gpsimd.tensor_scalar(rstd[:, m % 2, 0:1], mv[:, m % 2, 1:2], LN_EPS, None, ALU.add))
                nc.gpsimd.tensor_tensor(rstd[:, m % 2, 1:2], rstd[:, m % 2, 0:1], minus_half[:, :], ALU.pow).then_inc(ln_rstd, 1)

            early_lines(0)
            for t in range(NT + 1):
                if t >= 1:
                    rstd_of(t - 1)
                if t < NT:
                    early_lines(2 * t + 1)
                    early_lines(2 * t + 2)
            for t in range(2 * NT):
                if C_DN + t + 1 < C_GU:
                    early_lines(C_DN + t + 1)
                rstd_of(NT + t)
            with pool.Fori(0, NF // 2) as n:
                for s in range(2):
                    pool.wait_ge(in_gu[s], 64 * (n + 1))
                    for half in range(2):
                        lines(C_GU + 4 * n + 2 * s + half, gu_slot(s) + half)
            for m in range(3 * NT, 6 * NT):
                rstd_of(m)

        @block.vector
        def _(dve):
            steps = [0]

            def link(ins):
                steps[0] += 1
                ins.then_inc(dve_step, 1)
                dve.wait_ge(dve_step, steps[0])

            def f32(m):
                return m.bitcast(F32)

            def join(c, before_last=None):
                def L(n):
                    return line[:, n, :]

                base = DQ * c
                na, npl = len(ACT_LINES) * c, len(POOL_LINES) * c
                dve.wait_ge(act_lines, na + 5)
                nc.vector.tensor_tensor(L(0), L(0), L(1), ALU.min).then_inc(joined, 1)
                dve.wait_ge(act_lines, na + 6)
                nc.vector.tensor_tensor(L(4), L(4), L(5), ALU.max).then_inc(joined, 1)
                dve.wait_ge(joined, base + 1)
                nc.vector.tensor_tensor(L(0), L(0), L(2), ALU.min).then_inc(joined, 1)
                dve.wait_ge(pool_lines, npl + 1)
                dve.wait_ge(joined, base + 2)
                nc.vector.tensor_tensor(L(4), L(4), L(6), ALU.max).then_inc(joined, 1)
                dve.wait_ge(joined, base + 3)
                nc.vector.scalar_tensor_tensor(L(0), L(0), 0.0, L(3), ALU.min, ALU.min).then_inc(joined, 1)
                dve.wait_ge(pool_lines, npl + 2)
                dve.wait_ge(joined, base + 4)
                nc.vector.tensor_tensor(L(4), L(4), L(7), ALU.max).then_inc(joined, 1)
                if before_last is not None:
                    before_last()
                dve.wait_ge(joined, base + 6)
                nc.vector.scalar_tensor_tensor(wst[:, :], L(4), 0.0, L(0), ALU.max, ALU.add).then_inc(joined, 1)
                dve.wait_ge(joined, base + 7)

            def attention_chunk(c):
                join(c)
                if c >= C_O:
                    nc.vector.tensor_tensor(woT[:, c - C_O, :], wst[:, :], scales[:, c % RING, :], ALU.mult).then_inc(scaled, 1)
                    return
                dst = wsum[:, c % KD, :]
                put = dst if c < KD else wst[:, :]
                nc.vector.tensor_tensor(put.rearrange("p (b c) -> p b c", b=NB), wst[:, :].rearrange("p (b c) -> p b c", b=NB),
                                        s_qkv[:, c * NB:(c + 1) * NB].unsqueeze(2).to_broadcast([P, NB, BLOCK]), ALU.mult).then_inc(scaled, 1)
                if c >= KD:
                    dve.wait_ge(scaled, c + 1)
                    link(nc.vector.tensor_tensor(dst, dst, wst[:, :], ALU.add))

            def down_chunk(c):
                join(c)
                nc.vector.tensor_tensor(fold[:, c - C_DN, :], wst[:, :], scales[:, c % RING, :], ALU.mult).then_inc(scaled, 1)

            def ln_head(m, add):
                b, s = m % NT, m % 2
                if m >= 2:
                    dve.wait_ge(ln_done, m - 1)
                add(rbuf[:, s, :], x[:, b, :])
                dve.wait_ge(ln_sum, m + 1)
                link(nc.vector.bn_stats(st[:, s, :], rbuf[:, s, :]))
                nc.vector.bn_aggr(mv[:, s, :], st[:, s, :]).then_inc(ln_stats, 1)

            def ln_tail(m):
                b, s = m % NT, m % 2
                dve.wait_ge(ln_rstd, m + 1)
                nc.vector.tensor_scalar(x[:, b, :], rbuf[:, s, :], mv[:, s, 0:1], rstd[:, s, 1:2],
                                        ALU.subtract, ALU.mult).then_inc(ln_done, 1)

            def plus(n):
                return lambda r, xb: nc.vector.tensor_tensor(r, xb, bank[n][:, :], ALU.add).then_inc(ln_sum, 1)

            def x_low(m):
                dve.wait_ge(xt_ready, m + 1)
                cols = slice(m % NT * P, (m % NT + 1) * P)
                nc.vector.tensor_tensor(xl[:, :, cols], bank[6][:, :].rearrange("p (k t) -> p k t", k=KD),
                                        f32(xh[:, :, cols]), ALU.subtract).then_inc(xl_ready, 1)

            nc.vector.memset(attT[64:65, :, :], 1.0)
            nc.vector.memset(lmT[64:65, :, :], 1.0)
            nc.vector.memset(mz[:, :, :], 0.0)
            nc.vector.memset(v1[:, :, :, HD:HD + 1], 1.0).then_inc(consts, 1)
            nc.vector.sem_inc(h_ready, 4)
            nc.vector.sem_inc(up_ps, 2)
            nc.vector.sem_inc(b_ready, 2)
            nc.vector.sem_inc(t_h, 4)
            nc.vector.sem_inc(t_cast, 2)
            nc.vector.sem_inc(t_dcast, 2)
            dve.wait_ge(consts, 1)

            def qkv_out(b):
                dve.wait_ge(qkv_ps, b + 1)
                if b >= 2:
                    dve.wait_ge(sT_ps, b - 1)
                    dve.wait_ge(pv_ps, b - 1)
                if b == 0:
                    dve.wait_ge(in_bias, 16 * 6)
                nc.vector.tensor_tensor(qk[:, b % 2, :, :], bank[0][:, :].rearrange("p (c t) -> p c t", c=4),
                                        qk_b[:, :].unsqueeze(2).to_broadcast([P, 4, P]), ALU.add).then_inc(qk_ready, 1)
                nc.vector.tensor_tensor(v1[:, b % 2, :, 0:HD], bank[1][:, 0:64].rearrange("p (h e) -> p h e", h=HEADS),
                                        v_b[:, :].rearrange("p (h e) -> p h e", h=HEADS), ALU.add).then_inc(v_ready, 1)

            def row_max(b):
                dve.wait_ge(s_ps, b + 1)
                s = b % 2
                link(nc.vector.tensor_reduce(small[:, s, 0:8].rearrange("p (j a) -> p j a", j=NQ),
                                             heads_ps[:, :, 0:2 * P].rearrange("p j (a k) -> p j a k", a=2), AX.X, ALU.max))
                if b >= 1:
                    dve.wait_ge(max_ps, b)
                nc.vector.tensor_scalar(mz[:, :, :].rearrange("p a (j r) -> p a j r", j=NQ)[:, :, :, HD],
                                        small[:, s, 0:8].rearrange("p (j a) -> p a j", j=NQ), -1.0, None, ALU.mult).then_inc(max_ready, 1)

            def augment(b):
                dve.wait_ge(max_ps, b + 1)
                if b >= 1:
                    dve.wait_ge(sT_ps, b)
                nc.vector.tensor_tensor(q_aug, qk[:, b % 2, 0:2, :], bank[7][:, 0:2 * P].rearrange("p (a t) -> p a t", a=2),
                                        ALU.add).then_inc(aug_ready, 1)

            def normalise_heads(b):
                dve.wait_ge(pv_ps, b + 1)
                s = b % 2
                o = bank[1][:, 0:HEADS * (HD + 1)].rearrange("p (h e) -> p h e", h=HEADS)
                link(nc.vector.reciprocal(small[:, s, 8:16], o[:, :, HD]))
                link(nc.vector.tensor_scalar(small[:, s, 16:24], small[:, s, 8:16], float(D // HEADS) ** -0.5, None, ALU.mult))
                if b >= 2:
                    dve.wait_ge(attT_ps, b - 1)
                nc.vector.tensor_tensor(att[:, s, :].rearrange("p (h e) -> p h e", h=HEADS), o[:, :, 0:HD],
                                        small[:, s, 16:24].unsqueeze(2).to_broadcast([P, HEADS, HD]), ALU.mult).then_inc(att_ready, 1)

            qkv_out(0)
            for t in range(NT + 1):
                if t < NT:
                    row_max(t)
                if t + 1 < NT:
                    qkv_out(t + 1)
                if t < NT:
                    augment(t)
                if t >= 1:
                    dve.wait_ge(o_ps, t)
                    if t == 1:
                        dve.wait_ge(in_xn, 16)
                    ln_head(t - 1, plus(7))
                if t < NT:
                    attention_chunk(2 * t)
                if t >= 1:
                    ln_tail(t - 1)
                if t < NT:
                    normalise_heads(t)
                    attention_chunk(2 * t + 1)
                if t == 0:
                    dve.wait_ge(a_hi, 1)
                    nc.vector.tensor_tensor(al[:, :, :], aT_gu, f32(ah[:, :, :]), ALU.subtract).then_inc(a_ready, 1)

            for t in range(NT + 1):
                if t < NT:
                    s = t % 2
                    dve.wait_ge(sim_ps, t + 1)
                    link(nc.vector.tensor_reduce(small[:, s, 2:3], bank[2 + s][:, 0:P], AX.X, ALU.max))
                    nc.vector.tensor_scalar(small[:, s, 0:1], small[:, s, 2:3], -float(P) ** -0.5, None, ALU.mult).then_inc(sim_max, 1)
                if t >= 1:
                    dve.wait_ge(cx_ps, t)
                    ln_head(NT + t - 1, plus(4 + (t - 1) % 2))
                if t < NT:
                    dve.wait_ge(sim_exp, t + 1)
                    link(nc.vector.reciprocal(small[:, s, 3:4], small[:, s, 1:2]))
                    nc.vector.tensor_scalar(prob[:, s, :], prob[:, s, :], small[:, s, 3:4], None, ALU.mult).then_inc(sim_p, 1)
                if t >= 1:
                    ln_tail(NT + t - 1)
                if t < NT:
                    down_chunk(C_DN + t)

            def choose(b):
                s = b % 2
                ps = bank[s]
                g = gate_v[:, s, :]
                dve.wait_ge(ag_ps, b + 1)
                link(nc.vector.tensor_tensor(g[:, 0:4], ps[:, RMAX:RMAX + NR], g_b[:, :], ALU.add))
                nc.vector.tensor_tensor(g[:, 4:5], g[:, 0:1], g[:, 1:2], ALU.max)
                link(nc.vector.tensor_tensor(g[:, 5:6], g[:, 2:3], g[:, 3:4], ALU.max))
                nc.vector.tensor_tensor(g[:, 6:7], g[:, 1:2], g[:, 5:6], ALU.max)
                link(nc.vector.tensor_tensor(g[:, 7:8], g[:, 4:5], g[:, 2:3], ALU.max))
                nc.vector.tensor_tensor(g[:, 8:9], g[:, 6:7], g[:, 0:1], ALU.is_gt)
                nc.vector.tensor_tensor(g[:, 9:10], g[:, 5:6], g[:, 4:5], ALU.is_gt)
                link(nc.vector.tensor_tensor(g[:, 10:11], g[:, 3:4], g[:, 7:8], ALU.is_gt))
                if b >= 2:
                    dve.wait_ge(lm_ps, b - 1)
                nc.vector.tensor_copy(lm[:, s, 0:RANKS[0]], ps[:, 0:RANKS[0]])
                for n in range(1, NR):
                    last = nc.vector.tensor_scalar(lm[:, s, RANKS[n - 1]:RANKS[n]], ps[:, RANKS[n - 1]:RANKS[n]],
                                                   g[:, 7 + n:8 + n], None, ALU.mult)
                last.then_inc(lm_ready, 1)

            for t in range(NT + 1):
                if t < NT:
                    choose(t)
                if t >= 1:
                    dve.wait_ge(f0_ps, t)
                    ln_head(2 * NT + t - 1, plus(2 + (t - 1) % 2))
                    ln_tail(2 * NT + t - 1)
                if C_DN + NT + t < C_GU:
                    down_chunk(C_DN + NT + t)

            for n in range(2 * KD):
                dve.wait_ge(af_ps, n + 1)
                if n == 0:
                    dve.wait_ge(scaled, C_GU)
                dst = wsum[:, n, :] if n < KD else woT[:, n - KD, :]
                nc.vector.tensor_tensor(dst, dst, bank[n % 2][:, :], ALU.add).then_inc(af_added, 1)

            def gu_chunk(c, slot, before_last):
                join(c, before_last)
                nc.vector.tensor_tensor(wst[:, :], wst[:, :], scales[:, slot, :], ALU.mult).then_inc(scaled, 1)

            def gu_low(s, n, half):
                dve.wait_ge(hi_ready, n + 1)
                cols = slice(half * CH, (half + 1) * CH)
                nc.vector.tensor_tensor(wl[:, s, cols], wst[:, :], f32(wh[:, s, cols]), ALU.subtract).then_inc(w_ready, 1)

            def gu_lora_low(s, j):
                dve.wait_ge(b_hi, j + 1)
                lo = slice(2 * RG, 3 * RG)
                nc.vector.tensor_tensor(b_st[lo, s, :], b_gu[lo, s, :], f32(b_st[lo, s, :]), ALU.subtract).then_inc(b_ready, 1)

            def gu_weights(s, j):
                c = C_GU + 2 * j

                def first_half_out():
                    gu_low(s, 2 * j, 0)
                    dve.wait_ge(w_ready, 2 * j + 1)

                gu_chunk(c, gu_slot(s), None)
                gu_chunk(c + 1, gu_slot(s) + 1, first_half_out)

            def gu_weights_end(s, j):
                gu_low(s, 2 * j + 1, 1)
                gu_lora_low(s, j)

            gu_weights(0, 0)
            for b in range(NT + 1):
                if b < NT:
                    s = b % 2
                    dve.wait_ge(x1_ps, b + 1)
                    dve.wait_ge(ln_done, 3 * NT)
                    if b >= 2:
                        dve.wait_ge(xt_ps, 3 * NT + b - 1)
                    nc.vector.tensor_tensor(rbuf[:, s, :], x[:, b, :], bank[s][:, :], ALU.add).then_inc(x1_ready, 1)
                if b == 0:
                    gu_weights_end(0, 0)
                if b >= 1:
                    x_low(3 * NT + b - 1)
                if b < NT:
                    dve.wait_ge(x1_ready, b + 1)
                    nc.vector.tensor_tensor(x[:, b, :], x[:, b, :], rbuf[:, s, :], ALU.add).then_inc(x1_sum, 1)
                for j in range(2 * b, min(2 * b + 2, NF)):
                    dve.wait_ge(fold_ready, j + 1)
                    nc.vector.tensor_tensor(fold[:, j, :], fold[:, j, :], bank[4 + j % 2][:, :], ALU.add).then_inc(fold_kept, 1)
            mid = slice(RG, 2 * RG)
            for tg in range(TG):
                cols = slice(tg * 512, (tg + 1) * 512)
                dve.wait_ge(t_hi, tg + 1)
                nc.vector.tensor_tensor(th[mid, cols], bank[2 + tg][mid, :], f32(th[mid, cols]), ALU.subtract).then_inc(t_ready, 1)

            def hidden(s, j):
                for tg in range(TG):
                    dve.wait_ge(sil_ready, 2 * j + tg + 1)
                    dve.wait_ge(up_ps, 2 * j + tg + 3)
                    h = hT[:, bass.ds(j, 1), tg * 512:(tg + 1) * 512].rearrange("p o t -> p (o t)")
                    nc.vector.tensor_tensor(h, h, up_bank(s, tg), ALU.mult).then_inc(h_ready, 1)

            def gu_step(s, j):
                gu_weights(1 - s, j + 1)
                hidden(s, j)
                gu_weights_end(1 - s, j + 1)

            with dve.Fori(0, NF // 2 - 1) as n:
                for s in range(2):
                    gu_step(s, 2 * n + s)
            gu_step(0, NF - 2)
            hidden(1, NF - 1)

            def hidden_low(s, j, done):
                return nc.vector.tensor_tensor(xl[:, s, :], hT[:, bass.ds(j, 1), :].rearrange("p o t -> p (o t)"),
                                               f32(xh[:, s, :]), ALU.subtract)

            with dve.Fori(0, NF // 2) as n:
                for s in range(2):
                    j = 2 * n + s
                    dve.wait_ge(dn_hi, 2 * j + 1)
                    hidden_low(s, j, None)
                    dve.wait_ge(dn_hi, 2 * j + 2)
                    nc.vector.tensor_tensor(wl[:, s, 0:D], fold[:, bass.ds(j, 1), :].rearrange("p o c -> p (o c)"),
                                            f32(wh[:, s, 0:D]), ALU.subtract).then_inc(dn_ready, 1)
            dve.wait_ge(d_ps, 1)
            dve.wait_ge(x1_sum, NT)
            for b in range(NT):
                ln_head(3 * NT + b, plus(b))
                if b >= 1:
                    ln_tail(3 * NT + b - 1)
            ln_tail(4 * NT - 1)

            for t in range(NT + 2):
                if t < NT:
                    s = t % 2
                    dve.wait_ge(x_ps, t + 1)
                    link(nc.vector.tensor_reduce(small[:, s, 2:3], bank[4 + s][:, 0:P], AX.X, ALU.max))
                    nc.vector.tensor_scalar(small[:, s, 0:1], small[:, s, 2:3], -float(D) ** -0.5, None, ALU.mult).then_inc(x_max, 1)
                if 1 <= t <= NT:
                    s = (t - 1) % 2
                    dve.wait_ge(xo_ps, t)
                    dve.wait_ge(ln_done, 4 * NT)
                    link(nc.vector.reciprocal(small[:, s, 3:4], small[:, s, 1:2]))
                    ln_head(4 * NT + t - 1, lambda r, xb: nc.vector.scalar_tensor_tensor(
                        r, bank[s][:, :], small[:, s, 3:4], xb, ALU.mult, ALU.add).then_inc(ln_sum, 1))
                    ln_tail(4 * NT + t - 1)
                if t >= 2:
                    x_low(5 * NT + t - 2)

            with dve.Fori(0, NF // 2) as n:
                for s in range(2):
                    j = 2 * n + s
                    for tg in range(TG):
                        dve.wait_ge(t_sil, 2 * j + tg + 1)
                        dve.wait_ge(t_up_ps, 2 * j + tg + 1)
                        h = hT[:, bass.ds(j, 1), tg * 512:(tg + 1) * 512].rearrange("p o t -> p (o t)")
                        nc.vector.scalar_tensor_tensor(h, up_bank(s, tg), ff_s[:, s, 1:2], h, ALU.mult, ALU.mult).then_inc(t_h, 1)
            with dve.Fori(0, NF // 2) as n:
                for s in range(2):
                    j = 2 * n + s
                    dve.wait_ge(t_dhi, j + 1)
                    hidden_low(s, j, None).then_inc(t_dlo, 1)
            dve.wait_ge(t_d_ps, 1)
            dve.wait_ge(in_ds, 16)
            for b in range(NT):
                m = 5 * NT + b

                def scaled_sum(r, xb):
                    link(nc.vector.tensor_tensor(r, bank[b][:, :], ds[:, :], ALU.mult))
                    nc.vector.tensor_tensor(r, r, xb, ALU.add).then_inc(ln_sum, 1)

                if b == 0:
                    dve.wait_ge(ln_done, 5 * NT)
                ln_head(m, scaled_sum)
                if b >= 1:
                    ln_tail(m - 1)
            ln_tail(6 * NT - 1)


def layout(a):
    c = np.ascontiguousarray
    f = {k: np.asarray(v) for k, v in a.items()}

    def rows(m, n=P):
        return c(m.reshape(-1, n, m.shape[-1]).transpose(1, 0, 2))

    x2, ctx2 = f["x"].reshape(T, D), f["ctx_4096"].reshape(T, D)
    wqk = f["L0_attn_Wqk_w"].reshape(2, NQ, HD, 2, D)
    wqkT = np.zeros((D, 2, 2, NQ, QR), np.float32)
    wqkT[..., :HD] = wqk.transpose(4, 3, 0, 1, 2)
    qk_b = np.zeros((NQ, QR, 2, 2), np.float32)
    qk_b[:, :HD] = f["L0_attn_Wqk_b"].reshape(2, NQ, HD, 2).transpose(1, 2, 3, 0)
    qk_b[:, HD, 1, :] = 1.0
    ca, sa = f["L1_attn_codes_attn"], f["L1_attn_scales_attn"]

    def wide(g, u):
        m = np.stack([g, u]).reshape(2, NF, P, KD, P)
        return c(m.transpose(1, 4, 3, 0, 2).reshape(NF, P, KD * 2 * P))

    sgu = f["L1_attn_scales_gu"].reshape(2, NF, P, KD, 2)
    A, Ba, Bgu = f["L1_attn_lora_A_h"], f["L1_attn_lora_B_attn"], f["L1_attn_lora_B_gu"]
    lora_l, lora_r = np.zeros((O_ROW + R1, D), np.float32), np.zeros((O_ROW + R1, D), np.float32)
    lora_l[:3 * R1], lora_r[:3 * R1] = Ba[:3].transpose(0, 2, 1).reshape(3 * R1, D), A[:3].reshape(3 * R1, D)
    lora_l[O_ROW:], lora_r[O_ROW:] = A[3], Ba[3].T
    b_gu = np.zeros((NF, 3, 2, R1, 2, P), np.float32)
    for g in range(2):
        b_gu[:, :, g, :, g, :] = Bgu[g].reshape(NF, 1, P, R1).transpose(0, 1, 3, 2)
    b_gu = b_gu.reshape(NF, 3 * RG, 2 * P)
    a_d, bT_d = np.zeros((DQ_ROWS, DT * P), np.float32), np.zeros((DQ_ROWS, D), np.float32)
    for n in range(3):
        part = f["L1_attn_lora_A_down"][:, n * DT * P:(n + 1) * DT * P]
        a_d[n * QR:n * QR + R1, :part.shape[1]] = part
        bT_d[n * QR:n * QR + R1] = f["L1_attn_lora_B_down"].T
    return {
        "x": rows(x2), "xT": rows(c(x2.T)), "ctx": rows(ctx2), "ctxT": rows(c(ctx2.T)),
        "wqkT": rows(wqkT.reshape(D, 4 * P)), "qk_b": c(qk_b.reshape(P, 4)),
        "wvT": rows(c(f["L0_attn_Wv_w"].T)), "v_b": f["L0_attn_Wv_b"][None],
        "wo0": np.concatenate([f["L0_attn_Wo_w"].T, f["L0_attn_Wo_b"][None]]),
        "w0T": rows(c(f["L0_ffn_W"].T)), "agT": rows(np.concatenate([f["L0_ffn_A"].T, f["L0_ffn_gate_w"].T], 1)),
        "bT0": np.concatenate([f["L0_ffn_B"].T, f["L0_ffn_b"][None]]), "g_b": f["L0_ffn_gate_b"][None],
        "c_qkv": c(ca[:3].reshape(3 * KD, P, D)), "c_o": c(ca[3].T.reshape(KD, P, D)),
        "s_qkv": c(sa[:3].reshape(3, KD, P, NB).transpose(2, 0, 1, 3).reshape(P, -1)),
        "s_o": c(sa[3].T.reshape(KD, 2, D)), "lora_l": lora_l, "lora_r": lora_r,
        "aT_gu": rows(np.tile(A[4:6].reshape(RG, D).T, 3)), "b_gu": b_gu, "a_d": a_d, "bT_d": bT_d,
        "c_gu": wide(f["L1_attn_codes_gu"][0], f["L1_attn_codes_gu"][1]),
        "s_gu": c(sgu.transpose(1, 4, 3, 0, 2).reshape(NF, 2, 2 * CH)),
        "c_dn": c(f["L1_attn_codes_down"].T.reshape(NF, P, D)), "s_dn": c(f["L1_attn_scales_down"].T.reshape(NF, 2, D)),
        "wqT1": rows(c(f["L1_xattn_Wq"].T)), "wkT1": rows(c(f["L1_xattn_Wk"].T)),
        "q_b": c(f["L1_xattn_bq"].reshape(KD, P).T), "k_b": c(f["L1_xattn_bk"].reshape(KD, P).T),
        "t_gu": wide(f["L1_ffn_gate_t"], f["L1_ffn_up_t"]),
        "ts_gu": c(np.stack([f["L1_ffn_gate_s"], f["L1_ffn_up_s"]], 1).reshape(NF, P, 2)),
        "t_dn": c(f["L1_ffn_down_t"].T.reshape(NF, P, D)), "ds": f["L1_ffn_down_s"][None],
    }


def kernel(**inputs):
    import concourse.bacc as bacc
    from concourse.bass_utils import run_bass_kernel_spmd

    nc = bacc.Bacc("TRN2", target_bir_lowering=False, num_devices=1)
    arrays, aps = {}, {}
    for name, a in layout(inputs).items():
        arrays[f"in_{name}"] = a
        aps[name] = nc.dram_tensor(f"in_{name}", a.shape, mybir.dt.from_np(a.dtype), kind="ExternalInput").ap()
    out = nc.dram_tensor("out", (NT, P, D), F32, kind="ExternalOutput").ap()
    decoder_kernel(nc, aps, out)
    r = run_bass_kernel_spmd(nc, [arrays], core_ids=[0])
    return r.results[0]["out"]
```

```python
from contextlib import ExitStack

import numpy as np
import concourse.bass as bass
from concourse import mybir

F32 = mybir.dt.float32
F32R = mybir.dt.float32r
I32 = mybir.dt.int32
ALU = mybir.AluOpType
ACT = mybir.ActivationFunctionType
AX = mybir.AxisListType

P = 128
NT = 8
T = NT * P
D = 512
KD = D // P
FF = 1792
NF = FF // P
HEADS, HD = 8, 8
HA = HEADS * HD
HR = HA + HEADS
QR = 32
RANKS = (8, 16, 32, 64)
RMAX = RANKS[-1]
NR = len(RANKS)
R1 = 16
RG = 2 * R1
O_ROW = 64
DT = -(-NF // 3)
DQ_ROWS = 2 * QR + R1
BLOCK = 64
NB = D // BLOCK
CH = 512
RING = 4
TG = T // 512
LN_EPS = 1e-5

NF4 = np.array([-1.0, -0.6961928009986877, -0.5250730514526367, -0.39491748809814453,
                -0.28444138169288635, -0.18477343022823334, -0.09105003625154495, 0.0,
                0.07958029955625534, 0.16093020141124725, 0.24611230194568634, 0.33791524171829224,
                0.44070982933044434, 0.5626170039176941, 0.7229568362236023, 1.0], np.float32)


def _lines():
    def near(v, n):
        out, up, down = [v], v, v
        for _ in range(n):
            up, down = np.nextafter(up, np.float32(np.inf)), np.nextafter(down, np.float32(-np.inf))
            out += [up, down]
        return out

    lines = []
    for pair in range(len(NF4) // 2):
        lo, hi = 2 * pair, 2 * pair + 1
        y = {lo: float(NF4[lo]), hi: float(NF4[hi])}
        slope = np.float32(y[hi] - y[lo])
        offset = np.float32(y[lo] - lo * float(slope))
        best = None
        for a in near(slope, 12):
            for b in near(offset, 6):
                worst = 0.0
                for c in (lo, hi):
                    fused = np.float32(float(a) * c + float(b))
                    twice = np.float32(np.float32(a * np.float32(c)) + b)
                    worst = max([worst] + [abs(float(v) - y[c]) / max(abs(y[c]), 0.05) for v in (fused, twice)])
                if best is None or worst < best[0]:
                    best = (worst, float(a), float(b))
        lines.append(best[1:])
    return lines


LINES = _lines()
DRAWN = ((0, 1), (4, 2), (1, 3), (5, 4), (2, 5), (6, 6), (3, 7), (7, 7))
DQ = 7

C_QKV, C_O = 0, 3 * KD
C_DN = C_O + KD
C_GU = C_DN + NF
C_END = C_GU + 2 * NF

PLAN = ([1] * NT, [3], [1] * NT, [1] * 7, [1] * 4)
PLAN_END = [sum(map(sum, PLAN[:n + 1])) for n in range(len(PLAN))]
assert PLAN_END[1] < C_DN and PLAN_END[2] <= C_DN + NF - 6 and PLAN_END[-1] == C_GU


def plan(phase, t):
    if t >= len(PLAN[phase]):
        return []
    first = PLAN_END[phase] - sum(PLAN[phase][t:])
    return list(range(first, first + PLAN[phase][t]))


L1_FIRST = 2
GU1_STEP = NT - 2
TAIL = 6 * NT - NT // 2
FF_BANK = (2, 3, 7)
X3_BANK = (7, 4)
AF0 = 2


def decoder_kernel(nc, i, out):
    kq_dram = nc.dram_tensor("kq", (P, KD, T), F32, kind="Internal").ap()
    beta_dram = nc.dram_tensor("beta", (1, T), F32, kind="Internal").ap()
    ctx = ExitStack()
    with ctx:
        def sb(name, shape, dt=F32):
            return ctx.enter_context(nc.sbuf_tensor(name, shape, dt))

        def sem(name):
            return ctx.enter_context(nc.semaphore(name))
        x = sb("x", [P, NT, D])
        xh = sb("xh", [P, KD, T], F32R)
        xl = sb("xl", [P, KD, T], F32R)
        line = sb("line", [P, 8, CH])
        codes = sb("codes", [P, RING, CH], I32)
        scales = sb("scales", [P, RING, CH])
        wst = sb("wst", [P, CH])
        wh = sb("wh", [P, 2, 2 * CH], F32R)
        wl = sb("wl", [P, 2, 2 * CH], F32R)
        b_gu = sb("b_gu", [3 * RG, 2, 2 * P])
        b_st = sb("b_st", [3 * RG, 2, 2 * P], F32R)
        ah = sb("ah", [P, KD, 3 * RG], F32R)
        al = sb("al", [P, KD, 3 * RG], F32R)
        th = sb("th", [3 * RG, T], F32R)
        ff_s = sb("ff_s", [P, 2, 2])
        arena = sb("arena", [P, NF * T])
        fold = sb("fold", [P, NF, D])
        rbuf = sb("rbuf", [P, 2, D])
        ident = sb("ident", [P, P])
        st = sb("st", [P, 2, 6])
        mv = sb("mv", [P, 2, 2])
        rstd = sb("rstd", [P, 2, 3])
        minus_half = sb("minus_half", [P, 1])
        small = sb("small", [P, 2, 32])
        gate_v = sb("gate_v", [P, 2, 16])
        lm = sb("lm", [P, 2, RMAX])
        lmT = sb("lmT", [P, 2, P])
        probT = lmT
        prob = sb("prob", [P, 2, P])
        s_qkv = sb("s_qkv", [P, 3 * KD * NB])
        qk_b = sb("qk_b", [HA, 2])
        k_bm = sb("k_bm", [HA, HEADS])
        head_m = sb("head_m", [HR, HEADS])
        inverse = sb("inverse", [P, 2, HA])
        v_b = sb("v_b", [P, HEADS * HD])
        g_b = sb("g_b", [P, NR])
        q_b = sb("q_b", [P, KD])
        k_b = sb("k_b", [P, KD])
        wb = sb("wb", [P, 2 * KD + 1])
        ones = sb("ones", [1, P])
        ds = sb("ds", [P, D])
        lora_r = ds[0:O_ROW + R1, :]
        kq_s = ds[:, :].rearrange("p (e t) -> p e t", e=KD)
        beta_s = b_gu[0:1, 0, 0:P]

        hT = arena[:, :].rearrange("p (f t) -> p f t", f=NF)

        def carve(memory, start, n):
            return memory[:, start:start + n], start + n

        at = 0
        wsum, at = carve(arena, at, KD * D)
        woT, at = carve(arena, at, KD * D)
        shared, at = carve(arena, at, KD * D)
        xT_at = at
        xT, at = carve(arena, at, KD * T)
        wo0, at = carve(arena, at, D)
        agT, at = carve(arena, at, KD * (RMAX + NR))
        bT0, at = carve(arena, at, D)
        ctxT_r, at = carve(arena, at, 2 * D)
        bT_d, at = carve(arena, at, D)
        a_d, at = carve(arena, at, DT * P)
        q_a, at = carve(arena, at, 2 * P)
        p_sum, at = carve(arena, at, 2 * P)
        assert at <= NF * T
        qkvT = shared[:, 0:KD * 3 * HA].rearrange("p (j c) -> p j c", j=KD)
        wsum, woT, shared, xT, agT = (m.rearrange("p (j c) -> p j c", j=KD) for m in (wsum, woT, shared, xT, agT))
        w0T = mT = wq1 = shared
        q_a, p_sum = (m.rearrange("p (s t) -> p s t", s=2) for m in (q_a, p_sum))
        wk1 = [m[:, 0:D] for m in (bT0, bT_d, a_d, ds)]
        ctxT_r = ctxT_r.rearrange("p (s j c) -> p s j c", s=2, j=KD)
        lora_l = wo0[0:O_ROW + R1, :]
        KQ_F, BETA_F, CTX_F = KD, KD + 1, NF
        kqT, at = carve(arena, 0, KD * T)
        beta, at = carve(arena, at, T)
        assert at <= xT_at
        ctx1, at = carve(arena, xT_at + KD * T, NT * D)
        assert at <= NF * T
        kqT = kqT.rearrange("p (j t) -> p j t", j=KD)
        ctx1 = ctx1.rearrange("p (b c) -> p b c", b=NT)
        fold_flat = fold[:, :, :].rearrange("p f c -> p (f c)")
        t_dn = fold_flat.bitcast(I32).rearrange("p (f c) -> p f c", f=NF)
        at = 0
        attT, at = carve(fold_flat, at, 2 * P)
        mz, at = carve(fold_flat, at, P)
        kx, at = carve(fold_flat, at, 2 * HEADS * P)
        pT, at = carve(fold_flat, at, 2 * HEADS * P)
        vx, at = carve(fold_flat, at, 2 * HEADS * (HR + HD))
        attT, kx, pT, vx = (attT.rearrange("p (s t) -> p s t", s=2), kx.rearrange("p (s h t) -> p s h t", s=2, h=HEADS),
                            pT.rearrange("p (s h t) -> p s h t", s=2, h=HEADS), vx.rearrange("p (s c) -> p s c", s=2))
        v_own = vx.rearrange("p s (h c) -> p s h c", h=HEADS)[:, :, :, 0:HD]
        v_ones = vx[:, :, 0:HEADS * (HR + 1)].rearrange("p s (h c) -> p s h c", h=HEADS)[:, :, :, HA]
        KQ_F0, CTX_SLOT = NF - 6, NF - 2
        assert at <= CTX_SLOT * D
        kq_w = fold[:, KQ_F0:KQ_F0 + KD, :]
        ctx_r = fold[:, CTX_SLOT:NF, :]
        aT_gu = rbuf[:, 1, 0:KD * 3 * RG].rearrange("p (j c) -> p j c", j=KD)

        bank = [ctx.enter_context(nc.psum_tensor(f"bank{n}", [P, 512], F32)) for n in range(2)]
        heads_ps = ctx.enter_context(nc.psum_tensor("bank2345", [P, 4, 512], F32))
        bank += [heads_ps[:, n, :] for n in range(4)]
        bank += [ctx.enter_context(nc.psum_tensor(f"bank{n}", [P, 512], F32)) for n in (6, 7)]

        def gate_bank(s, tg):
            return bank[4 * s + tg][:, :]

        def up_bank(s, tg):
            return bank[4 * s + TG + tg][:, :]

        def x_small(b, n):
            return small[:, b % 2, 4 * (b // 2 % 2) + n:4 * (b // 2 % 2) + n + 1]

        in_x = [sem(f"in_x{n}") for n in range(4)]
        in_qk, in_bias, in_xn, in_wo0 = sem("in_qk"), sem("in_bias"), sem("in_xn"), sem("in_wo0")
        in_ffn0, in_lora, in_agu = sem("in_ffn0"), sem("in_lora"), sem("in_agu")
        in_ctx = [sem(f"in_ctx{n}") for n in range(2)]
        in_codes = [sem(f"in_codes{n}") for n in range(RING)]
        in_gu = [sem(f"in_gu{n}") for n in range(2)]
        in_ctx1, in_kq, in_wk, in_wq, in_ds = sem("in_context1"), sem("in_kq"), sem("in_wk"), sem("in_wq"), sem("in_ds")
        in_tgu = [sem(f"in_tgu{n}") for n in range(2)]
        in_ts = [sem(f"in_ts{n}") for n in range(2)]
        in_tdn = sem("in_tdn")
        consts = sem("consts")
        ident_ready = sem("ident_ready")
        dve_step = sem("dve_step")
        pool_step = sem("pool_step")
        lines_drawn, joined, scaled = sem("lines_drawn"), sem("joined"), sem("scaled")
        hi_ready, w_ready = sem("hi_ready"), sem("w_ready")
        b_hi, b_ready = sem("b_hi"), sem("b_ready")
        a_hi, a_ready, t_ps, t_hi, t_ready = sem("a_hi"), sem("a_ready"), sem("t_ps"), sem("t_hi"), sem("t_ready")
        fold_ready, fold_kept = sem("fold_ready"), sem("fold_kept")
        ln_stats, ln_rstd, ln_sum, ln_done = sem("ln_stats"), sem("ln_rstd"), sem("ln_sum"), sem("ln_done")
        xt_ps, xt_ready, xl_ready, x2_ps, x2_ready = (sem(n) for n in ("xt_ps", "xt_ready", "xl_ready", "x2_ps", "x2_ready"))
        qkv_ps, qk_ready, v_ready = sem("qkv_ps"), sem("qk_ready"), sem("v_ready")
        s_ps, max_ready, max_ps, aug_ready, sT_ps, p_ready = (sem(n) for n in ("s_ps", "max_ready", "max_ps", "aug_ready", "sT_ps", "p_ready"))
        pv_ps, sums_ready, sum_ps, inv_ready, rb_ps, att_ready, o_ps = (sem(n) for n in ("pv_ps", "sums_ready", "sum_ps", "inv_ready", "rb_ps", "att_ready", "o_ps"))
        sim_ps, sim_max, sim_exp, sim_p, cx_ps = (sem(n) for n in ("sim_ps", "sim_max", "sim_exp", "sim_p", "cx_ps"))
        ag_ps, lm_ready, lm_ps, lmT_ready, f0_ps = (sem(n) for n in ("ag_ps", "lm_ready", "lm_ps", "lmT_ready", "f0_ps"))
        af_ps, af_added, m_ps, m_ready, x1_ps, x1_ready, x1_sum = (sem(n) for n in ("af_ps", "af_added", "m_ps", "m_ready", "x1_ps", "x1_ready", "x1_sum"))
        gate_ps, up_ps, sil_ready, h_ready = (sem(n) for n in ("gate_ps", "up_ps", "sil_ready", "h_ready"))
        dn_hi, dn_ready, hu_used, d_ps = sem("dn_hi"), sem("dn_ready"), sem("hu_used"), sem("d_ps")
        kw_ps, kw_ready, kq_ps, kq_ready, kq_out = (sem(n) for n in ("kw_ps", "kw_ready", "kq_ps", "kq_ready", "kq_out"))
        x_ps, x_max, x_exp, xpT_ps, xpT_ready, xo_ps = (sem(n) for n in ("x_ps", "x_max", "x_exp", "xpT_ps", "xpT_ready", "xo_ps"))
        t_cast, t_gate_ps, t_up_ps, t_sil, t_h = (sem(n) for n in ("t_cast", "t_gate_ps", "t_up_ps", "t_sil", "t_h"))
        t_dhi, t_dw, t_dlo, t_used, t_d_ps = (sem(n) for n in ("t_dhi", "t_dw", "t_dlo", "t_used", "t_d_ps"))
        out_done = sem("out_done")
        sp_seen = sem("sp_seen")

        block = ctx.enter_context(nc.Block())

        def chunk_dmas(c):
            return 1 if c < C_O else 3

        def codes_landed(eng, c):
            eng.wait_ge(in_codes[c % RING], 16 * sum(chunk_dmas(n) for n in range(c % RING, c + 1, RING)))

        def gu_slot(s):
            return (C_GU + 2 * s) % RING

        @block.sync
        def _(sp):
            sp.dma_start(qkvT, i["qkvT"]).then_inc(in_qk, 16)
            for n in range(4):
                sp.dma_start(xT[:, :, 2 * n * P:2 * (n + 1) * P], i["xT"][:, :, 2 * n * P:2 * (n + 1) * P]).then_inc(in_x[n], 16)
                if n == 0:
                    sp.dma_start(qk_b[:, :], i["qk_b"]).then_inc(in_bias, 16)
                    sp.dma_start(head_m[:, :], i["head_m"]).then_inc(in_bias, 16)
                    sp.dma_start(v_b[:, :], i["v_b"].partition_broadcast(P)).then_inc(in_bias, 16)
                    sp.dma_start(g_b[:, :], i["g_b"].partition_broadcast(P)).then_inc(in_bias, 16)
                    sp.dma_start(s_qkv[:, :], i["s_qkv"]).then_inc(in_bias, 16)
                    sp.dma_start(q_b[:, :], i["q_b"]).then_inc(in_bias, 16)
                    sp.dma_start(k_b[:, :], i["k_b"]).then_inc(in_bias, 16)
                    for c in range(RING):
                        sp.dma_start(codes[:, c, :], i["c_qkv"][c]).then_inc(in_codes[c], 16)
            sp.dma_start(x[:, :, :], i["x"]).then_inc(in_xn, 16)
            sp.dma_start(wo0[0:65, :], i["wo0"]).then_inc(in_wo0, 16)
            sp.dma_start(aT_gu, i["aT_gu"]).then_inc(in_agu, 16)
            for n in range(2):
                sp.dma_start(ctx_r[:, n, :], i["ctx"][:, n, :]).then_inc(in_ctx[n], 16)
                sp.dma_start(ctxT_r[:, n, :, :], i["ctxT"][:, :, n * P:(n + 1) * P]).then_inc(in_ctx[n], 16)
            sp.dma_start(agT, i["agT"]).then_inc(in_ffn0, 16)
            for d in range(KD):
                sp.dma_start(wk1[d], i["wk1"][d]).then_inc(in_wk, 16)

            def slot_free(c):
                for done, n in ((lines_drawn, len(DRAWN)),
                                (scaled, 1)):
                    sp.wait_ge(done, n * (c - RING + 1))
                    if not isinstance(c, int):
                        sp.sem_inc(sp_seen, 1)

            def scales_of(dst, src):
                for half in range(2):
                    yield dst[half * BLOCK:(half + 1) * BLOCK], src(half)

            def load_chunk(c):
                slot_free(c)
                done = in_codes[c % RING]
                if c < C_O:
                    sp.dma_start(codes[:, c % RING, :], i["c_qkv"][c]).then_inc(done, 16)
                else:
                    what, n = ("o", c - C_O) if c < C_DN else ("dn", c - C_DN)
                    sp.dma_start(codes[:, c % RING, :], i["c_" + what][n]).then_inc(done, 16)
                    for dst, s_src in scales_of(scales[:, c % RING, :], lambda half: i["s_" + what][n, half:half + 1, :]):
                        sp.dma_start(dst, s_src.partition_broadcast(BLOCK)).then_inc(done, 16)

            for c in range(RING, PLAN_END[0] + RING):
                load_chunk(c)
                if c == PLAN_END[0] + 1:
                    sp.wait_ge(qkv_ps, NT)
                    sp.dma_start(wq1, i["wq1"]).then_inc(in_wq, 16)
            def keys_out(b):
                sp.wait_ge(kq_ready, b + 1)
                sp.dma_start(kq_dram[:, :, b * P:(b + 1) * P], kq_s).then_inc(kq_out, 16)
                sp.dma_start(beta_dram[:, b * P:(b + 1) * P], beta_s).then_inc(kq_out, 16)

            sp.wait_ge(o_ps, NT)
            sp.dma_start(lora_l, i["lora_l"]).then_inc(in_lora, 16)
            for c in range(PLAN_END[0] + RING, PLAN_END[1] + RING):
                load_chunk(c)
            sp.wait_ge(kw_ps, KD)
            sp.dma_start(w0T, i["w0T"]).then_inc(in_ffn0, 16)
            sp.dma_start(bT0[0:RMAX + 1, :], i["bT0"]).then_inc(in_ffn0, 16)
            sp.dma_start(a_d[0:DQ_ROWS, :], i["a_d"]).then_inc(in_lora, 16)
            sp.dma_start(bT_d[0:DQ_ROWS, :], i["bT_d"]).then_inc(in_lora, 16)

            for b in range(2, NT):
                sp.wait_ge(kq_ps, b - 1)
                sp.dma_start(ctxT_r[:, b % 2, :, :], i["ctxT"][:, :, b * P:(b + 1) * P]).then_inc(in_ctx[b % 2], 16)
                sp.wait_ge(cx_ps, b - 1)
                sp.dma_start(ctx_r[:, b % 2, :], i["ctx"][:, b, :]).then_inc(in_ctx[b % 2], 16)
                load_chunk(PLAN_END[1] + RING + b - 2)
                keys_out(b - 2)
            for b in range(NT - 2, NT):
                load_chunk(PLAN_END[1] + RING + b)
                keys_out(b)
            sp.wait_ge(kq_out, 32 * NT)
            sp.dma_start(lora_r, i["lora_r"]).then_inc(in_lora, 16)
            for c in range(PLAN_END[2] + RING, C_GU):
                load_chunk(c)

            with sp.Fori(0, NF // 2) as n:
                for s in range(2):
                    j = 2 * n + s
                    slots = slice(gu_slot(s), gu_slot(s) + 2)
                    slot_free(C_GU + 1 + 2 * j)
                    sp.wait_ge(b_ready, j + 1)
                    sp.sem_inc(sp_seen, 1)
                    sp.dma_start(codes[:, slots, :].rearrange("p s c -> p (s c)"),
                                 i["c_gu"][bass.ds(j, 1), :, :].rearrange("o p c -> (o p) c")).then_inc(in_gu[s], 16)
                    for half in range(2):
                        sp.dma_start(scales[half * BLOCK:(half + 1) * BLOCK, slots, :].rearrange("p s c -> p (s c)"),
                                     i["s_gu"][bass.ds(j, 1), half, :].partition_broadcast(BLOCK).rearrange("p o c -> p (o c)")).then_inc(in_gu[s], 16)
                    sp.dma_start(b_gu[:, s, :], i["b_gu"][bass.ds(j, 1), :, :].rearrange("o r c -> (o r) c")).then_inc(in_gu[s], 16)

            sp.wait_ge(af_ps, 2 * KD)
            sp.dma_start(ds[:, :], i["ds"].partition_broadcast(P)).then_inc(in_ds, 16)
            for used, dst, src, done in ((KQ_F, kqT, kq_dram, in_kq), (BETA_F, beta[0:1, :], beta_dram, in_kq), (CTX_F, ctx1, i["ctx"], in_ctx1)):
                sp.wait_ge(dn_ready, NF + used)
                sp.dma_start(dst, src).then_inc(done, 16)

            sp.wait_ge(d_ps, NT)
            sp.dma_start(t_dn, i["t_dn"]).then_inc(in_tdn, 16)
            sp.wait_ge(lines_drawn, len(DRAWN) * C_END)
            with sp.Fori(0, NF // 2) as n:
                for s in range(2):
                    j = 2 * n + s
                    sp.wait_ge(t_cast, j + 1)
                    sp.sem_inc(sp_seen, 1)
                    sp.dma_start(codes[:, 2 * s:2 * s + 2, :].rearrange("p s c -> p (s c)"),
                                 i["t_gu"][bass.ds(j, 1), :, :].rearrange("o p c -> (o p) c")).then_inc(in_tgu[s], 16)
                    sp.wait_ge(t_h, 2 * j + 2)
                    sp.sem_inc(sp_seen, 1)
                    sp.dma_start(ff_s[:, s, :], i["ts_gu"][bass.ds(j, 1), :, :].rearrange("o p c -> (o p) c")).then_inc(in_ts[s], 16)
            for b in range(NT):
                sp.wait_ge(ln_done, 5 * NT + b + 1)
                sp.dma_start(out[b, :, :], x[:, b, :]).then_inc(out_done, 16)
            sp.wait_ge(out_done, 16 * NT)

        @block.tensor
        def _(pe):
            def transpose_tile(b, src, dst, done=xt_ps):
                for k in range(KD):
                    last = pe.transpose(dst[:, k * P:(k + 1) * P], src[:, k * P:(k + 1) * P], ident[:, :])
                last.then_inc(done, 1)

            def qkv(b):
                if b == 0:
                    pe.wait_ge(in_qk, 16)
                if b % 2 == 0:
                    pe.wait_ge(in_x[b // 2], 16)
                if b >= 1:
                    pe.wait_ge(qk_ready, b)
                    pe.wait_ge(v_ready, b)
                t = slice(b * P, (b + 1) * P)
                for n in range(2):
                    for k in range(KD):
                        pe.matmul(bank[0][0:HA, n * P:(n + 1) * P], qkvT[:, k, n * HA:(n + 1) * HA], xT[:, k, t],
                                  start=(k == 0), stop=(k == KD - 1))
                for k in range(KD):
                    last = pe.matmul(bank[0][:, 2 * P:2 * P + HA], xT[:, k, t], qkvT[:, k, 2 * HA:3 * HA], start=(k == 0), stop=(k == KD - 1))
                last.then_inc(qkv_ps, 1)

            def scores(b):
                pe.wait_ge(qk_ready, b + 1)
                if b >= 2:
                    pe.wait_ge(p_ready, b - 1)
                for n in range(2):
                    last = pe.matmul(bank[2 + 2 * (b % 2) + n][:, :], q_a[0:HA, b % 2, :],
                                     kx[0:HA, b % 2, 4 * n:4 * n + 4, :].rearrange("p h t -> p (h t)"), start=True, stop=True)
                last.then_inc(s_ps, 1)

            def max_rows(b):
                pe.wait_ge(max_ready, b + 1)
                if b >= 2:
                    pe.wait_ge(ln_sum, b - 1)
                pe.transpose(bank[7][0:HR, 0:P], mz[:, 0:HR], ident[:, :]).then_inc(max_ps, 1)

            def scores_T(b):
                pe.wait_ge(aug_ready, b + 1)
                for h in range(HEADS):
                    last = pe.matmul(bank[2 + 2 * (b % 2) + h // 4][:, h % 4 * P:(h % 4 + 1) * P], kx[0:HR, b % 2, h, :], q_a[0:HR, b % 2, :],
                                     start=True, stop=True)
                last.then_inc(sT_ps, 1)

            def heads_out(b):
                pe.wait_ge(p_ready, b + 1)
                pe.wait_ge(v_ready, b + 1)
                if b >= 1:
                    pe.wait_ge(att_ready, b)
                for h in range(HEADS):
                    last = pe.matmul(bank[1][0:HR, 0:P], vx[:, b % 2, h * HR:(h + 1) * HR], pT[:, b % 2, h, :],
                                     start=(h == 0), stop=(h == HEADS - 1))
                last.then_inc(pv_ps, 1)

            def sums_T(b):
                pe.wait_ge(sums_ready, b + 1)
                pe.transpose(bank[1][:, 3 * P:3 * P + HEADS], p_sum[HA:HR, b % 2, :], ident[HA:HR, HA:HR]).then_inc(sum_ps, 1)

            def spread_inverse(b):
                pe.wait_ge(inv_ready, b + 1)
                pe.matmul(bank[1][0:HA, P:2 * P], inverse[:, b % 2, :], ident[:, :],
                          start=True, stop=True).then_inc(rb_ps, 1)

            def o_proj(b):
                pe.wait_ge(att_ready, b + 1)
                if b == 0:
                    pe.wait_ge(in_wo0, 16)
                pe.matmul(bank[7][:, :], attT[0:HA + 1, b % 2, :], wo0[0:HA + 1, :], start=True, stop=True).then_inc(o_ps, 1)

            def x_T(layer, b):
                pe.wait_ge(ln_done, layer * NT + b + 1)
                if layer or b:
                    pe.wait_ge(xt_ready, layer * NT + b)
                transpose_tile(b, x[:, b, :], bank[6])

            def key_weights(c):
                if c == 0:
                    pe.wait_ge(p_ready, NT)
                    pe.wait_ge(qk_ready, NT)
                    pe.wait_ge(v_ready, NT)
                    pe.wait_ge(in_wk, 16 * KD)
                    pe.wait_ge(in_wq, 16)
                e = slice(c * P, (c + 1) * P)
                columns = [(bank[0][:, c:c + 1], lambda d: wq1[:, d, e], k_b), (bank[0][:, KD + c:KD + c + 1], lambda d: wk1[d][:, e], q_b)]
                if c == KD - 1:
                    columns.append((bank[0][0:1, 2 * KD:2 * KD + 1], lambda d: q_b[:, d:d + 1], k_b))
                for d in range(KD):
                    for dst, lhs, rhs in columns[d:d + 1]:
                        for n in range(KD):
                            pe.matmul(dst, lhs(n), rhs[:, n:n + 1], start=(n == 0), stop=(n == KD - 1))
                    last = pe.matmul(bank[2 + c][:, :], wk1[d][:, e], wq1[:, d, :], start=(d == 0), stop=(d == KD - 1))
                last.then_inc(kw_ps, 1)

            pe.wait_ge(ident_ready, 1)
            for t in range(-2, NT + 2):
                if 0 <= t < NT:
                    scores_T(t)
                if 1 <= t <= NT:
                    sums_T(t - 1)
                if t == NT:
                    key_weights(0)
                if 0 <= t + 1 < NT:
                    scores(t + 1)
                if t >= 2:
                    x_T(0, t - 2)
                if 1 <= t <= NT:
                    spread_inverse(t - 1)
                if t + 2 < NT:
                    qkv(t + 2)
                if 1 <= t <= NT:
                    o_proj(t - 1)
                if t == NT:
                    for c in range(1, KD):
                        key_weights(c)
                if 0 <= t < NT:
                    heads_out(t)
                if 0 <= t + 1 < NT:
                    max_rows(t + 1)

            def sims(b):
                pe.wait_ge(xt_ready, b + 1)
                pe.wait_ge(in_ctx[b % 2], 32 * (b // 2 + 1))
                if b >= 2:
                    pe.wait_ge(sim_exp, b - 1)
                for k in range(KD):
                    last = pe.matmul(bank[2 + b % 2][:, 0:P], xT[:, k, b * P:(b + 1) * P], ctxT_r[:, b % 2, k, :],
                                     start=(k == 0), stop=(k == KD - 1))
                last.then_inc(sim_ps, 1)

            def context(b):
                pe.wait_ge(sim_p, b + 1)
                if b >= 2:
                    pe.wait_ge(ln_sum, NT + b - 1)
                pe.matmul(bank[4 + b % 2][:, :], prob[:, b % 2, :], ctx_r[:, b % 2, :], start=True, stop=True).then_inc(cx_ps, 1)

            def keys(b):
                if b == 0:
                    pe.wait_ge(kw_ready, KD + 1)
                elif b >= 2:
                    pe.wait_ge(kq_ready, b - 1)
                for e in range(KD):
                    for c in range(KD):
                        pe.matmul(bank[b % 2][:, e * P:(e + 1) * P], kq_w[:, c, e * P:(e + 1) * P], ctxT_r[:, b % 2, c, :],
                                  start=(c == 0), stop=(c == KD - 1))

            def key_bias(b):
                if b >= 1:
                    pe.wait_ge(kq_ready, b)
                for c in range(KD):
                    last = pe.matmul(bank[7][0:1, 0:P], wb[:, KD + c:KD + c + 1], ctxT_r[:, b % 2, c, :], start=(c == 0), stop=(c == KD - 1))
                last.then_inc(kq_ps, 1)

            pe.wait_ge(kw_ready, KD)
            sims(0)
            for t in range(NT + 2):
                if 1 <= t <= NT:
                    context(t - 1)
                if t < NT:
                    keys(t)
                if t + 1 < NT:
                    sims(t + 1)
                if t >= 2:
                    x_T(1, t - 2)
                if t < NT:
                    key_bias(t)

            def ranks(b):
                pe.wait_ge(xt_ready, NT + b + 1)
                if b == 0:
                    pe.wait_ge(in_ffn0, 48)
                    pe.wait_ge(kq_ready, NT)
                if b >= 2:
                    pe.wait_ge(lmT_ready, b - 1)
                for k in range(KD):
                    last = pe.matmul(bank[b % 2][:, 0:RMAX + NR], xT[:, k, b * P:(b + 1) * P], agT[:, k, :],
                                     start=(k == 0), stop=(k == KD - 1))
                last.then_inc(ag_ps, 1)

            def ffn_W(b):
                if b >= 3:
                    pe.wait_ge(ln_sum, 2 * NT + b - 2)
                for k in range(KD):
                    pe.matmul(bank[FF_BANK[b % 3]][:, :], xT[:, k, b * P:(b + 1) * P], w0T[:, k, :], start=(k == 0), stop=False)

            def lora_T(b):
                pe.wait_ge(lm_ready, b + 1)
                pe.transpose(bank[b % 2][0:RMAX, P:2 * P], lm[:, b % 2, :], ident[:, :]).then_inc(lm_ps, 1)

            def lora_out(b):
                pe.wait_ge(lmT_ready, b + 1)
                pe.matmul(bank[FF_BANK[b % 3]][:, :], lmT[0:RMAX + 1, b % 2, :], bT0[0:RMAX + 1, :], start=False, stop=True).then_inc(f0_ps, 1)

            def attention_lora(n):
                if n == 0:
                    pe.wait_ge(in_lora, 16 * 4)
                    pe.wait_ge(ln_sum, 2 * NT)
                if n >= 2:
                    pe.wait_ge(af_added, n - 1)
                j = n % KD
                rows = slice(0, 3 * R1) if n < KD else slice(O_ROW, O_ROW + R1)
                pe.matmul(bank[4 + n % 2][:, :], lora_l[rows, j * P:(j + 1) * P], lora_r[rows, :], start=True, stop=True).then_inc(af_ps, 1)

            def attention_product(c):
                if c == 0:
                    pe.wait_ge(af_added, 2 * KD)
                if c >= 2:
                    pe.wait_ge(m_ready, c - 1)
                for j in range(KD):
                    last = pe.matmul(bank[4 + c % 2][:, :], wsum[:, j, c * P:(c + 1) * P], woT[:, j, :], start=(j == 0), stop=(j == KD - 1))
                last.then_inc(m_ps, 1)

            for t in range(NT + 2):
                if t < NT:
                    ranks(t)
                if 1 <= t <= NT:
                    lora_T(t - 1)
                if t < NT:
                    ffn_W(t)
                if t >= NT:
                    attention_product(2 * (t - NT))
                if t >= 2:
                    x_T(2, t - 2)
                if 1 <= t <= NT:
                    lora_out(t - 1)
                if t >= NT:
                    attention_product(2 * (t - NT) + 1)
                for n in range(AF0 * max(t - 1, 0), min(AF0 * t, 2 * KD)):
                    attention_lora(n)

            pe.wait_ge(m_ready, KD)

            def down_lora(j):
                if j >= 2:
                    pe.wait_ge(fold_kept, j - 1)
                rows = slice(QR * (j // DT), QR * (j // DT) + R1)
                pe.matmul(bank[4 + j % 2][:, :], a_d[rows, (j % DT) * P:(j % DT + 1) * P], bT_d[rows, :],
                          start=True, stop=True).then_inc(fold_ready, 1)

            def gu_lora(tg):
                pe.wait_ge(a_ready, 1)
                pe.wait_ge(xl_ready, NT // 2 * (tg + 1))
                for k in range(KD):
                    for a, xs in ((ah, xh), (ah, xl), (al, xh)):
                        last = pe.matmul(bank[2 + tg][0:3 * RG, :], a[:, k, :], xs[:, k, tg * 512:(tg + 1) * 512],
                                         start=(k == 0 and a is ah and xs is xh), stop=(k == KD - 1 and a is al))
                last.then_inc(t_ps, 1)

            for t in range(NT + 1):
                if t < NT:
                    pe.wait_ge(xt_ready, 2 * NT + t + 1)
                    if t >= 2:
                        pe.wait_ge(x1_ready, t - 1)
                    for k in range(KD):
                        last = pe.matmul(bank[t % 2][:, :], xT[:, k, t * P:(t + 1) * P], mT[:, k, :], start=(k == 0), stop=(k == KD - 1))
                    last.then_inc(x1_ps, 1)
                if t >= 1:
                    pe.wait_ge(x1_ready, t)
                    pe.wait_ge(xt_ready, 3 * NT)
                    if t >= 2:
                        pe.wait_ge(xl_ready, t - 1)
                    transpose_tile(t - 1, rbuf[:, (t - 1) % 2, :], bank[6])
                for j in range(2 * t, min(2 * t + 2, NF)):
                    down_lora(j)
                if t == NT - 1:
                    gu_lora(0)
            gu_lora(1)

            def gu_tile(s, j):
                pe.wait_ge(w_ready, 2 * j + 2)
                pe.wait_ge(b_ready, j + 3)
                for tg in range(TG):
                    cols = slice(tg * 512, (tg + 1) * 512)
                    pe.wait_ge(h_ready, 2 * j + tg + 1)
                    for g, dst, done in ((0, gate_bank(s, tg), gate_ps), (1, up_bank(s, tg), up_ps)):
                        for k in range(KD):
                            c = (2 * k + g) * P
                            pe.matmul(dst, wh[:, s, c:c + P], xh[:, k, cols], start=(k == 0), stop=False)
                            pe.matmul(dst, wh[:, s, c:c + P], xl[:, k, cols], start=False, stop=False)
                            pe.matmul(dst, wl[:, s, c:c + P], xh[:, k, cols], start=False, stop=False)
                        pe.matmul(dst, b_st[:, s, g * P:(g + 1) * P], th[:, cols], start=False, stop=True).then_inc(done, 1)

            pe.wait_ge(t_ready, TG)
            pe.wait_ge(fold_kept, NF)
            with pe.Fori(0, NF // 2) as n:
                for s in range(2):
                    gu_tile(s, 2 * n + s)

            def down_tile(half, s, ready, n, parts, first, last_one, done):
                for operand in ready:
                    pe.wait_ge(operand, n)
                for b in range(half * NT // 2, (half + 1) * NT // 2):
                    for p, (h, wp) in enumerate(parts):
                        last = pe.matmul(bank[b][:, :], h[:, s, b * P:(b + 1) * P], wp[:, s, 0:D],
                                         start=first and p == 0, stop=last_one and p == len(parts) - 1)
                    if last_one:
                        last.then_inc(done, 1)
                if not last_one:
                    last.then_inc(done, 1)

            def down(ready, parts, used, done, left):
                for half in range(2):
                    n0 = half * NF
                    pe.wait_ge(left, 2 * NF + 2 + 2 * half)
                    for s in range(2):
                        down_tile(half, s, ready, n0 + s + 1, parts, s == 0, False, used)
                    with pe.Fori(1, NF // 2 - 1) as n:
                        for s in range(2):
                            down_tile(half, s, ready, n0 + 2 * n + s + 1, parts, False, False, used)
                    down_tile(half, 0, ready, n0 + NF - 1, parts, False, False, used)
                    down_tile(half, 1, ready, n0 + NF, parts, False, True, done)

            down((dn_ready,), ((xh, wh), (xh, wl), (xl, wh)), hu_used, d_ps, h_ready)

            def x2_T(b):
                pe.wait_ge(ln_done, 3 * NT + b + 1)
                if b >= 2:
                    pe.wait_ge(x2_ready, b - 1)
                transpose_tile(b, x[:, b, :], bank[b % 2], x2_ps)

            def x_scores(b):
                pe.wait_ge(x2_ready, b + 1)
                if b == 0:
                    pe.wait_ge(in_kq, 32)
                if b >= 2:
                    pe.wait_ge(xpT_ready, b - 1)
                else:
                    pe.wait_ge(ln_sum, 3 * NT + 4)
                t = slice(b * P, (b + 1) * P)
                for k in range(KD):
                    pe.matmul(bank[2 + b % 2][:, 0:P], xT[:, k, t], kqT[:, k, t], start=(k == 0), stop=False)
                pe.matmul(bank[2 + b % 2][:, 0:P], ones[:, :], beta[0:1, t], start=False, stop=True).then_inc(x_ps, 1)

            def x_probT(b):
                pe.wait_ge(x_exp, b + 1)
                pe.transpose(bank[2 + b % 2][:, P:2 * P], prob[:, b % 2, :], ident[:, :]).then_inc(xpT_ps, 1)

            def x_out(b):
                pe.wait_ge(xpT_ready, b + 1)
                if b == 0:
                    pe.wait_ge(in_ctx1, 16)
                    pe.wait_ge(ln_sum, 4 * NT)
                if b >= 2:
                    pe.wait_ge(ln_sum, 4 * NT + b - 1)
                pe.matmul(bank[5 + b % 2][:, :], probT[:, b % 2, :], ctx1[:, b, :], start=True, stop=True).then_inc(xo_ps, 1)

            def x3_T(b):
                pe.wait_ge(ln_done, 4 * NT + b + 1)
                if b >= 2:
                    pe.wait_ge(xl_ready, NT + b - 1)
                transpose_tile(b, x[:, b, :], bank[X3_BANK[b % 2]])

            def t_gu_product(s, tg, g):
                cols = slice(tg * 512, (tg + 1) * 512)
                dst, done = ((gate_bank(s, tg), t_gate_ps), (up_bank(s, tg), t_up_ps))[g]
                for k in range(KD):
                    c = (2 * k + g) * P
                    pe.matmul(dst, wh[:, s, c:c + P], xh[:, k, cols], start=(k == 0), stop=False)
                    last = pe.matmul(dst, wh[:, s, c:c + P], xl[:, k, cols], start=False, stop=(k == KD - 1))
                last.then_inc(done, 1)

            def t_gu_tile(s, j, groups=range(TG)):
                pe.wait_ge(t_cast, j + 3)
                for tg in groups:
                    pe.wait_ge(t_h, 2 * j + tg + 1)
                    for g in range(2):
                        t_gu_product(s, tg, g)

            for t in range(NT + 4):
                if t < NT:
                    x2_T(t)
                if 1 <= t <= NT:
                    x_probT(t - 1)
                if t >= 4:
                    x3_T(t - 4)
                if t < NT:
                    x_scores(t)
                if 1 <= t <= NT:
                    x_out(t - 1)
                if t == NT + 1:
                    pe.wait_ge(t_cast, 3)
                    pe.wait_ge(xl_ready, NT + NT // 2)
                    t_gu_product(0, 0, 0)
                elif t == NT + 2:
                    t_gu_product(0, 0, 1)
            pe.wait_ge(ln_sum, 5 * NT)
            pe.wait_ge(xl_ready, 2 * NT)
            t_gu_tile(0, 0, (1,))
            t_gu_tile(1, 1)
            with pe.Fori(1, NF // 2) as n:
                for s in range(2):
                    t_gu_tile(s, 2 * n + s)
            down((t_dlo, t_dw), ((xh, wh), (xl, wh)), t_used, t_d_ps, t_h)

        @block.scalar
        def _(act):
            def lines(c, slot):
                for line_n, freed in DRAWN:
                    if not (isinstance(c, int) and c == 0):
                        act.wait_ge(joined, DQ * (c - 1) + freed)
                    a, b = LINES[line_n]
                    nc.scalar.activation(line[:, line_n, :], codes[:, slot, :], ACT.Copy, bias=b, scale=a).then_inc(lines_drawn, 1)

            def early_lines(c):
                codes_landed(act, c)
                lines(c, c % RING)

            def gu_lines(s, n, half):
                act.wait_ge(in_gu[s], 64 * (n + 1))
                lines(C_GU + 4 * n + 2 * s + half, gu_slot(s) + half)

            def x_T_out(m, n=6, dst=xT, there=xt_ps, done=xt_ready):
                act.wait_ge(there, m + 1)
                b = m % NT
                nc.scalar.activation(dst[:, :, b * P:(b + 1) * P], bank[n][:, :].rearrange("p (k t) -> p k t", k=KD),
                                     ACT.Copy).then_inc(done, 1)

            def norm_tail(m):
                act.wait_ge(ln_rstd, m + 1)
                src = rbuf[:, m % 2, :] if m < TAIL else x[:, m % NT, :]
                nc.scalar.activation(x[:, m % NT, :], src, ACT.Identity, bias=rstd[:, m % 2, 2:3],
                                     scale=rstd[:, m % 2, 1:2]).then_inc(ln_done, 1)

            def key_weights_out(c):
                act.wait_ge(kw_ps, c + 1)
                nc.scalar.activation(kq_w[:, c, :], bank[2 + c][:, :], ACT.Copy).then_inc(kw_ready, 1)

            def qk_out(b):
                act.wait_ge(qkv_ps, b + 1)
                if b == 0:
                    act.wait_ge(consts, 1)
                if b >= 2:
                    act.wait_ge(sT_ps, b - 1)
                nc.scalar.activation(q_a[0:HA, b % 2, :], bank[0][0:HA, 0:P], ACT.Identity, bias=qk_b[:, 0:1])
                for h in range(HEADS):
                    last = nc.scalar.activation(kx[0:HA, b % 2, h, :], bank[0][0:HA, P:2 * P], ACT.Identity,
                                                bias=k_bm[:, h:h + 1], scale=head_m[0:HA, h:h + 1])
                last.then_inc(qk_ready, 1)

            def heads_exp(b):
                act.wait_ge(sT_ps, b + 1)
                if b >= 2:
                    act.wait_ge(pv_ps, b - 1)
                nc.scalar.activation(pT[:, b % 2, :, :].rearrange("p h t -> p (h t)"),
                                     heads_ps[:, 2 * (b % 2):2 * (b % 2) + 2, :].rearrange("p n c -> p (n c)"), ACT.Exp).then_inc(p_ready, 1)

            def sums_out(b):
                act.wait_ge(pv_ps, b + 1)
                if b >= 2:
                    act.wait_ge(o_ps, b - 1)
                nc.scalar.activation(attT[0:HA, b % 2, :], bank[1][0:HA, 0:P], ACT.Copy)
                nc.scalar.activation(p_sum[HA:HR, b % 2, :], bank[1][HA:HR, 0:P], ACT.Copy, scale=float(HA) ** 0.5).then_inc(sums_ready, 1)

            qk_out(0)
            early_lines(0)
            qk_out(1)
            for t in range(NT + 2):
                for c in plan(0, t)[:1]:
                    early_lines(c + 1)
                if t < NT:
                    heads_exp(t)
                if t >= 2:
                    x_T_out(t - 2)
                if t + 2 < NT:
                    qk_out(t + 2)
                if t < NT:
                    sums_out(t)
                    if t >= 1:
                        norm_tail(t - 1)
                for c in plan(0, t)[1:]:
                    early_lines(c + 1)
                if t == NT:
                    for c, after in enumerate(plan(1, 0)):
                        key_weights_out(c)
                        if c == KD - 2:
                            key_weights_out(KD - 1)
                            nc.scalar.activation(wb[:, 0:2 * KD], bank[0][:, 0:2 * KD], ACT.Copy)
                            nc.scalar.activation(wb[0:1, 2 * KD:2 * KD + 1], bank[0][0:1, 2 * KD:2 * KD + 1], ACT.Copy).then_inc(kw_ready, 1)
                        early_lines(after + 1)
                        if c == 0:
                            norm_tail(NT - 1)
                if t == 0:
                    act.wait_ge(in_agu, 16)
                    nc.scalar.activation(ah[:, :, :], aT_gu, ACT.Copy).then_inc(a_hi, 1)

            def sims_exp(b):
                act.wait_ge(sim_max, b + 1)
                if b >= 2:
                    act.wait_ge(cx_ps, b - 1)
                nc.scalar.activation(prob[:, b % 2, :], bank[2 + b % 2][:, 0:P], ACT.Exp, bias=small[:, b % 2, 0:1],
                                     scale=float(P) ** -0.5, accum_out=small[:, b % 2, 1:2]).then_inc(sim_exp, 1)

            sims_exp(0)
            for t in range(NT + 2):
                for c in plan(2, t):
                    early_lines(c + 1)
                if 1 <= t <= NT:
                    norm_tail(NT + t - 1)
                if t >= 2:
                    x_T_out(NT + t - 2)
                if t + 1 < NT:
                    sims_exp(t + 1)
                if t < NT:
                    act.wait_ge(kq_ps, t + 1)
                    if t >= 1:
                        act.wait_ge(kq_out, 32 * t)
                    for e in range(KD):
                        nc.scalar.activation(kq_s[:, e, :], bank[t % 2][:, e * P:(e + 1) * P], ACT.Identity, bias=wb[:, e:e + 1])
                    nc.scalar.activation(beta_s, bank[7][0:1, 0:P], ACT.Identity, bias=wb[0:1, 2 * KD:2 * KD + 1]).then_inc(kq_ready, 1)

            for t in range(NT + 2):
                if 1 <= t <= NT:
                    act.wait_ge(lm_ps, t)
                    if t >= 3:
                        act.wait_ge(f0_ps, t - 2)
                    nc.scalar.activation(lmT[0:RMAX, (t - 1) % 2, :], bank[(t - 1) % 2][0:RMAX, P:2 * P], ACT.Copy).then_inc(lmT_ready, 1)
                if t >= 2:
                    norm_tail(2 * NT + t - 2)
                for c in plan(3, t):
                    early_lines(c + 1)
                if t >= 2:
                    x_T_out(2 * NT + t - 2)
                if t == NT + 1:
                    early_lines(PLAN_END[3] + 1)
                for c in range(2 * (t - NT), 2 * (t - NT) + 2) if t >= NT else ():
                    act.wait_ge(m_ps, c + 1)
                    nc.scalar.activation(mT[:, c, :], bank[4 + c % 2][:, :], ACT.Copy, scale=1.0 / 3.0).then_inc(m_ready, 1)

            def gu_hi(s, chunk, half):
                act.wait_ge(scaled, chunk + 1)
                nc.scalar.activation(wh[:, s, half * CH:(half + 1) * CH], wst[:, :], ACT.Copy).then_inc(hi_ready, 1)

            def gu_lora_hi(s):
                nc.scalar.activation(b_st[:, s, :], b_gu[:, s, :], ACT.Copy).then_inc(b_hi, 1)

            for n in range(1, L1_FIRST):
                early_lines(PLAN_END[3] + n + 1)
            for b in range(NT):
                c = PLAN_END[3] + L1_FIRST + b
                if c + 1 < C_GU:
                    early_lines(c + 1)
                elif c + 1 == C_GU:
                    gu_lines(0, 0, 0)
                elif c == C_GU:
                    gu_lines(0, 0, 1)
                    gu_hi(0, C_GU, 0)
                elif c == C_GU + 1:
                    gu_lines(1, 0, 0)
                    gu_hi(0, C_GU + 1, 1)
                    gu_lora_hi(0)
                elif b == GU1_STEP:
                    gu_lines(1, 0, 1)
                    gu_hi(1, C_GU + 2, 0)
                x_T_out(3 * NT + b, dst=xh)
            for tg in range(TG):
                act.wait_ge(t_ps, tg + 1)
                nc.scalar.activation(th[:, tg * 512:(tg + 1) * 512], bank[2 + tg][0:3 * RG, :], ACT.Copy).then_inc(t_hi, 1)
            gu_lines(0, 1, 0)
            gu_hi(1, C_GU + 3, 1)
            gu_lora_hi(1)

            def silu_table():
                nc.scalar.activation(small[0:1, 1, 31:32], minus_half[0:1, :], ACT.Silu)

            def silu(s, j, tg):
                act.wait_ge(gate_ps, 2 * j + tg + 1)
                nc.scalar.activation(hT[:, bass.ds(j, 1), tg * 512:(tg + 1) * 512].rearrange("p o t -> p (o t)"),
                                     gate_bank(s, tg), ACT.Silu).then_inc(sil_ready, 1)

            def gu_step(s, j, n_next, n_after):
                gu_lines(1 - s, n_next, 1)
                for tg in range(TG):
                    silu(1 - s, j - 1, tg)
                act.wait_ge(up_ps, 2 * j + 2)
                gu_hi(1 - s, C_GU + 2 * j + 2, 0)
                gu_lora_hi(1 - s)
                if n_after is not None:
                    gu_lines(s, n_after, 0)
                gu_hi(1 - s, C_GU + 2 * j + 3, 1)

            silu_table()
            with act.Fori(0, NF // 2 - 2) as n:
                gu_step(1, 2 * n + 1, n + 1, n + 1)
                gu_step(0, 2 * n + 2, n + 1, n + 2)
            gu_step(1, NF - 3, NF // 2 - 1, NF // 2 - 1)
            gu_step(0, NF - 2, NF // 2 - 1, None)
            def hidden_hi(half, s, j, done):
                cols = slice(half * 512, (half + 1) * 512)
                nc.scalar.activation(xh[:, s, cols], hT[:, bass.ds(j, 1), cols].rearrange("p o t -> p (o t)"), ACT.Copy).then_inc(done, 1)

            def down_parts(used_sem, done_sem, parts):
                for half in range(2):
                    n0 = half * (NF - 1)
                    for s in range(2):
                        if half and s == 0:
                            act.wait_ge(used_sem, n0)
                        elif half:
                            act.wait_ge(done_sem, NT // 2)
                        if half or s:
                            parts(half, s, s)
                    with act.Fori(1, NF // 2) as n:
                        for s in range(2):
                            act.wait_ge(used_sem, n0 + 2 * n + s - 1)
                            parts(half, s, 2 * n + s)

            def dn_hi_parts(half, s, j):
                hidden_hi(half, s, j, dn_hi)
                nc.scalar.activation(wh[:, s, 0:D], fold[:, bass.ds(j, 1), :].rearrange("p o c -> p (o c)"), ACT.Copy).then_inc(dn_hi, 1)

            for tg in range(TG):
                silu(0, NF - 2, tg)
            silu(1, NF - 1, 0)
            act.wait_ge(up_ps, 2 * NF + 1)
            dn_hi_parts(0, 0, 0)
            silu(1, NF - 1, 1)
            act.wait_ge(up_ps, 2 * NF + 2)
            act.wait_ge(h_ready, 2 * NF + 4)
            down_parts(hu_used, d_ps, dn_hi_parts)

            def t_gu_cast(s, n, free):
                act.wait_ge(in_tgu[s], 16 * (n + 1))
                if free is not None:
                    act.wait_ge(t_up_ps, free)
                nc.scalar.activation(wh[:, s, :], codes[:, 2 * s:2 * s + 2, :].rearrange("p s c -> p (s c)"), ACT.Copy).then_inc(t_cast, 1)

            for t in range(NT + 4):
                if t < NT:
                    x_T_out(t, t % 2, xT, x2_ps, x2_ready)
                if 1 <= t <= NT:
                    act.wait_ge(xpT_ps, t)
                    if t >= 3:
                        act.wait_ge(xo_ps, t - 2)
                    nc.scalar.activation(probT[:, (t - 1) % 2, :], bank[2 + (t - 1) % 2][:, P:2 * P], ACT.Copy).then_inc(xpT_ready, 1)
                if t >= 4:
                    x_T_out(4 * NT + t - 4, X3_BANK[t % 2], xh)
                if t < NT:
                    act.wait_ge(x_max, t + 1)
                    if t >= 2:
                        act.wait_ge(xpT_ps, t - 1)
                    nc.scalar.activation(prob[:, t % 2, :], bank[2 + t % 2][:, 0:P], ACT.Exp, bias=x_small(t, 0),
                                         scale=float(D) ** -0.5, accum_out=x_small(t, 1)).then_inc(x_exp, 1)
                if NT <= t < NT + 2:
                    t_gu_cast(t - NT, 0, None)
            silu_table()

            def t_silu(s, n, groups=range(TG)):
                j = 2 * n + s
                act.wait_ge(in_ts[s], 16 * (n + 1))
                for tg in groups:
                    act.wait_ge(t_gate_ps, 2 * j + tg + 1)
                    nc.scalar.activation(hT[:, bass.ds(j, 1), tg * 512:(tg + 1) * 512].rearrange("p o t -> p (o t)"),
                                         gate_bank(s, tg), ACT.Silu, scale=ff_s[:, s, 0:1]).then_inc(t_sil, 1)

            with act.Fori(0, NF // 2 - 1) as n:
                t_silu(0, n)
                t_gu_cast(0, n + 1, 4 * n + 2)
                t_silu(1, n)
                t_gu_cast(1, n + 1, 4 * n + 4)
            def t_dn_parts(half, s, j):
                hidden_hi(half, s, j, t_dhi)
                nc.scalar.activation(wh[:, s, 0:D], t_dn[:, bass.ds(j, 1), :].rearrange("p o c -> p (o c)"), ACT.Copy).then_inc(t_dw, 1)

            t_silu(0, NF // 2 - 1)
            t_silu(1, NF // 2 - 1, (0,))
            act.wait_ge(in_tdn, 16)
            act.wait_ge(t_up_ps, 2 * NF - 1)
            t_dn_parts(0, 0, 0)
            t_silu(1, NF // 2 - 1, (1,))
            act.wait_ge(t_up_ps, 2 * NF)
            act.wait_ge(t_h, 2 * NF + 4)
            down_parts(t_used, t_d_ps, t_dn_parts)
            for m in range(TAIL, 6 * NT):
                norm_tail(m)

        @block.gpsimd
        def _(pool):
            steps = [0]

            def link(ins):
                steps[0] += 1
                ins.then_inc(pool_step, 1)
                pool.wait_ge(pool_step, steps[0])

            link(nc.gpsimd.memset(ident[:, :], 0.0))
            nc.gpsimd.affine_select(out=ident[:, :], in_=ident[:, :], compare_op=ALU.not_equal, fill=1.0, base=0,
                                    pattern=[[-1, P]], channel_multiplier=1).then_inc(ident_ready, 1)
            link(nc.gpsimd.memset(minus_half[:, :], -0.5))

            def rstd_of(m):
                pool.wait_ge(ln_stats, m + 1)
                link(nc.gpsimd.tensor_scalar(rstd[:, m % 2, 0:1], mv[:, m % 2, 1:2], LN_EPS, None, ALU.add))
                last = nc.gpsimd.tensor_tensor(rstd[:, m % 2, 1:2], rstd[:, m % 2, 0:1], minus_half[:, :], ALU.pow)
                if m < 3 * NT or m >= TAIL:
                    link(last)
                    last = nc.gpsimd.tensor_scalar(rstd[:, m % 2, 2:3], mv[:, m % 2, 0:1], rstd[:, m % 2, 1:2], -1.0, ALU.mult, ALU.mult)
                last.then_inc(ln_rstd, 1)

            for m in range(6 * NT):
                rstd_of(m)

        @block.vector
        def _(dve):
            steps = [0]

            def link(ins):
                steps[0] += 1
                ins.then_inc(dve_step, 1)
                dve.wait_ge(dve_step, steps[0])

            def f32(m):
                return m.bitcast(F32)

            def join(c, before_last=None, after_first=None, settle=True):
                def L(n):
                    return line[:, n, :]

                drawn, base = len(DRAWN) * c, DQ * c
                dve.wait_ge(lines_drawn, drawn + 3)
                nc.vector.tensor_tensor(L(1), L(0), L(1), ALU.min).then_inc(joined, 1)
                if after_first is not None:
                    after_first()
                dve.wait_ge(lines_drawn, drawn + 4)
                nc.vector.tensor_tensor(L(5), L(4), L(5), ALU.max).then_inc(joined, 1)
                dve.wait_ge(lines_drawn, drawn + 5)
                dve.wait_ge(joined, base + 1)
                nc.vector.tensor_tensor(L(2), L(1), L(2), ALU.min).then_inc(joined, 1)
                dve.wait_ge(lines_drawn, drawn + 6)
                dve.wait_ge(joined, base + 2)
                nc.vector.tensor_tensor(L(6), L(5), L(6), ALU.max).then_inc(joined, 1)
                dve.wait_ge(lines_drawn, drawn + 7)
                dve.wait_ge(joined, base + 3)
                nc.vector.scalar_tensor_tensor(L(3), L(2), 0.0, L(3), ALU.min, ALU.min).then_inc(joined, 1)
                dve.wait_ge(lines_drawn, drawn + 8)
                dve.wait_ge(joined, base + 4)
                nc.vector.tensor_tensor(L(7), L(6), L(7), ALU.max).then_inc(joined, 1)
                if before_last is not None:
                    before_last()
                dve.wait_ge(joined, base + 6)
                nc.vector.scalar_tensor_tensor(wst[:, :], L(7), 0.0, L(3), ALU.max, ALU.add).then_inc(joined, 1)
                if settle:
                    dve.wait_ge(joined, base + 7)

            def attention_chunk(c, between=None):
                join(c, between)
                if c >= C_O:
                    nc.vector.tensor_tensor(woT[:, c - C_O, :], wst[:, :], scales[:, c % RING, :], ALU.mult).then_inc(scaled, 1)
                    return
                dst = wsum[:, c % KD, :]
                put = dst if c < KD else wst[:, :]
                nc.vector.tensor_tensor(put.rearrange("p (b c) -> p b c", b=NB), wst[:, :].rearrange("p (b c) -> p b c", b=NB),
                                        s_qkv[:, c * NB:(c + 1) * NB].unsqueeze(2).to_broadcast([P, NB, BLOCK]), ALU.mult).then_inc(scaled, 1)
                if c >= KD:
                    dve.wait_ge(scaled, c + 1)
                    link(nc.vector.tensor_tensor(dst, dst, wst[:, :], ALU.add))

            def down_chunk(c):
                join(c)
                nc.vector.tensor_tensor(fold[:, c - C_DN, :], wst[:, :], scales[:, c % RING, :], ALU.mult).then_inc(scaled, 1)

            def chunk(c, between=None):
                if c < C_DN:
                    attention_chunk(c, between)
                else:
                    down_chunk(c)

            def ln_head(m, add):
                b, s = m % NT, m % 2
                if m >= 2:
                    dve.wait_ge(ln_done, m - 1)
                add(rbuf[:, s, :], x[:, b, :])
                dve.wait_ge(ln_sum, m + 1)
                link(nc.vector.bn_stats(st[:, s, :], rbuf[:, s, :]))
                nc.vector.bn_aggr(mv[:, s, :], st[:, s, :]).then_inc(ln_stats, 1)

            def plus(n):
                return lambda r, xb: nc.vector.tensor_tensor(r, xb, bank[n][:, :], ALU.add).then_inc(ln_sum, 1)

            def x_low(m, n=6):
                dve.wait_ge(xt_ready, m + 1)
                cols = slice(m % NT * P, (m % NT + 1) * P)
                nc.vector.tensor_tensor(xl[:, :, cols], bank[n][:, :].rearrange("p (k t) -> p k t", k=KD),
                                        f32(xh[:, :, cols]), ALU.subtract).then_inc(xl_ready, 1)

            nc.vector.memset(attT[HA:HA + 1, :, :], 1.0)
            nc.vector.memset(lmT[RMAX:RMAX + 1, :, :], 1.0)
            nc.vector.memset(mz[:, :], 0.0)
            nc.vector.memset(ones[:, :], 1.0)
            link(nc.vector.memset(vx[:, :, :], 0.0))
            nc.vector.memset(v_ones, 1.0)
            dve.wait_ge(in_bias, 16 * 7)
            nc.vector.tensor_scalar(k_bm[:, :], head_m[0:HA, :], qk_b[:, 1:2], None, ALU.mult).then_inc(consts, 1)
            for n in range(2):
                nc.vector.tensor_copy(kx[HA:HR, n, :, :], head_m[HA:HR, :].unsqueeze(2).to_broadcast([HEADS, HEADS, P]))
            nc.vector.sem_inc(h_ready, 4)
            nc.vector.sem_inc(up_ps, 2)
            nc.vector.sem_inc(b_ready, 2)
            nc.vector.sem_inc(t_h, 4)
            nc.vector.sem_inc(t_cast, 2)

            def v_out(b):
                dve.wait_ge(qk_ready, b + 1)
                if b >= 2:
                    dve.wait_ge(pv_ps, b - 1)
                nc.vector.tensor_tensor(v_own[:, b % 2, :, :], bank[0][:, 2 * P:2 * P + HA].rearrange("p (h e) -> p h e", h=HEADS),
                                        v_b[:, :].rearrange("p (h e) -> p h e", h=HEADS), ALU.add).then_inc(v_ready, 1)

            def row_max(b):
                dve.wait_ge(s_ps, b + 1)
                s = b % 2
                link(nc.vector.tensor_reduce(small[:, s, 0:HEADS].rearrange("p (n h) -> p n h", n=2),
                                             heads_ps[:, 2 * s:2 * s + 2, :].rearrange("p n (h k) -> p n h k", h=4), AX.X, ALU.max))
                if b >= 1:
                    dve.wait_ge(max_ps, b)
                nc.vector.tensor_scalar(mz[:, HA:HR], small[:, s, 0:HEADS], -1.0, None, ALU.mult).then_inc(max_ready, 1)

            def augment(b):
                dve.wait_ge(max_ps, b + 1)
                if b >= 2:
                    dve.wait_ge(sT_ps, b - 1)
                nc.vector.tensor_copy(q_a[HA:HR, b % 2, :], bank[7][HA:HR, 0:P]).then_inc(aug_ready, 1)

            def invert_sums(b):
                dve.wait_ge(sum_ps, b + 1)
                if b >= 2:
                    dve.wait_ge(rb_ps, b - 1)
                one = small[:, b % 2, 16:16 + HEADS]
                link(nc.vector.reciprocal(one, bank[1][:, 3 * P:3 * P + HEADS]))
                nc.vector.tensor_copy(inverse[:, b % 2, :].rearrange("p (h e) -> p h e", h=HEADS),
                                      one.unsqueeze(2).to_broadcast([P, HEADS, HD])).then_inc(inv_ready, 1)

            def normalise_heads(b):
                dve.wait_ge(rb_ps, b + 1)
                dve.wait_ge(sums_ready, b + 1)
                nc.vector.tensor_tensor(attT[0:HA, b % 2, :], attT[0:HA, b % 2, :], bank[1][0:HA, P:2 * P], ALU.mult).then_inc(att_ready, 1)

            for t in range(-2, NT + 1):
                chunks = plan(1, 0) if t == NT else plan(0, t) if t >= 0 else []
                for c in chunks[:1]:
                    chunk(c, (lambda: invert_sums(t - 1)) if t >= 1 else None)
                if t >= 1:
                    normalise_heads(t - 1)
                if 0 <= t + 1 < NT:
                    row_max(t + 1)
                if t >= 1:
                    dve.wait_ge(o_ps, t)
                    if t == 1:
                        dve.wait_ge(in_xn, 16)
                    ln_head(t - 1, plus(7))
                if 0 <= t + 1 < NT:
                    augment(t + 1)
                if t + 2 < NT:
                    v_out(t + 2)
                for c in chunks[1:]:
                    chunk(c)
                if t == 0:
                    dve.wait_ge(a_hi, 1)
                    nc.vector.tensor_tensor(al[:, :, :], aT_gu, f32(ah[:, :, :]), ALU.subtract).then_inc(a_ready, 1)

            for t in range(NT + 1):
                if t < NT:
                    s = t % 2
                    dve.wait_ge(sim_ps, t + 1)
                    link(nc.vector.tensor_reduce(small[:, s, 2:3], bank[2 + s][:, 0:P], AX.X, ALU.max))
                    nc.vector.tensor_scalar(small[:, s, 0:1], small[:, s, 2:3], -float(P) ** -0.5, None, ALU.mult).then_inc(sim_max, 1)
                if t >= 1:
                    dve.wait_ge(cx_ps, t)
                    ln_head(NT + t - 1, plus(4 + (t - 1) % 2))
                if t < NT:
                    dve.wait_ge(sim_exp, t + 1)
                    link(nc.vector.reciprocal(small[:, s, 3:4], small[:, s, 1:2]))
                    nc.vector.tensor_scalar(prob[:, s, :], prob[:, s, :], small[:, s, 3:4], None, ALU.mult).then_inc(sim_p, 1)
                for c in plan(2, t):
                    chunk(c)

            def choose(b):
                s = b % 2
                ps = bank[s]
                g = gate_v[:, s, :]
                dve.wait_ge(ag_ps, b + 1)
                link(nc.vector.tensor_tensor(g[:, 0:4], ps[:, RMAX:RMAX + NR], g_b[:, :], ALU.add))
                nc.vector.tensor_tensor(g[:, 4:5], g[:, 0:1], g[:, 1:2], ALU.max)
                link(nc.vector.tensor_tensor(g[:, 5:6], g[:, 2:3], g[:, 3:4], ALU.max))
                nc.vector.tensor_tensor(g[:, 6:7], g[:, 1:2], g[:, 5:6], ALU.max)
                link(nc.vector.tensor_tensor(g[:, 7:8], g[:, 4:5], g[:, 2:3], ALU.max))
                nc.vector.tensor_tensor(g[:, 8:9], g[:, 6:7], g[:, 0:1], ALU.is_gt)
                nc.vector.tensor_tensor(g[:, 9:10], g[:, 5:6], g[:, 4:5], ALU.is_gt)
                link(nc.vector.tensor_tensor(g[:, 10:11], g[:, 3:4], g[:, 7:8], ALU.is_gt))
                if b >= 2:
                    dve.wait_ge(lm_ps, b - 1)
                nc.vector.tensor_copy(lm[:, s, 0:RANKS[0]], ps[:, 0:RANKS[0]])
                for n in range(1, NR):
                    last = nc.vector.tensor_scalar(lm[:, s, RANKS[n - 1]:RANKS[n]], ps[:, RANKS[n - 1]:RANKS[n]],
                                                   g[:, 7 + n:8 + n], None, ALU.mult)
                last.then_inc(lm_ready, 1)

            def add_lora(n):
                dve.wait_ge(af_ps, n + 1)
                if n == 0:
                    dve.wait_ge(scaled, C_DN)
                dst = wsum[:, n, :] if n < KD else woT[:, n - KD, :]
                nc.vector.tensor_tensor(dst, dst, bank[4 + n % 2][:, :], ALU.add).then_inc(af_added, 1)

            for t in range(NT + 2):
                if t >= 2:
                    dve.wait_ge(f0_ps, t - 1)
                    ln_head(2 * NT + t - 2, plus(FF_BANK[(t - 2) % 3]))
                if t < NT:
                    choose(t)
                if t == 0:
                    dve.wait_ge(kq_ps, NT)
                for c in plan(3, t):
                    chunk(c)
                for n in range(AF0 * max(t - 1, 0), min(AF0 * t, 2 * KD)):
                    add_lora(n)

            def hidden(s, j, groups=range(TG)):
                for tg in groups:
                    dve.wait_ge(sil_ready, 2 * j + tg + 1)
                    dve.wait_ge(up_ps, 2 * j + tg + 3)
                    h = hT[:, bass.ds(j, 1), tg * 512:(tg + 1) * 512].rearrange("p o t -> p (o t)")
                    nc.vector.tensor_tensor(h, h, up_bank(s, tg), ALU.mult).then_inc(h_ready, 1)

            def gu_scale(slot):
                nc.vector.tensor_tensor(wst[:, :], wst[:, :], scales[:, slot, :], ALU.mult).then_inc(scaled, 1)

            def gu_low(s, n, half):
                dve.wait_ge(hi_ready, n + 1)
                cols = slice(half * CH, (half + 1) * CH)
                nc.vector.tensor_tensor(wl[:, s, cols], wst[:, :], f32(wh[:, s, cols]), ALU.subtract).then_inc(w_ready, 1)

            def gu_lora_low(s, j):
                dve.wait_ge(b_hi, j + 1)
                lo = slice(2 * RG, 3 * RG)
                nc.vector.tensor_tensor(b_st[lo, s, :], b_gu[lo, s, :], f32(b_st[lo, s, :]), ALU.subtract).then_inc(b_ready, 1)

            def first_half_out(s, j):
                gu_low(s, 2 * j, 0)
                dve.wait_ge(w_ready, 2 * j + 1)

            def gu_first_half(s, j):
                join(C_GU + 2 * j)
                gu_scale(gu_slot(s))

            def gu_second_half(s, j, also=None):
                def between():
                    first_half_out(s, j)
                    if also is not None:
                        also()

                join(C_GU + 2 * j + 1, between)
                gu_scale(gu_slot(s) + 1)

            def gu_weights(s, j):
                c = C_GU + 2 * j

                def scale_first():
                    dve.wait_ge(joined, DQ * (c + 1))
                    gu_scale(gu_slot(s))

                def between():
                    hidden(s, j - 2, (0,))
                    first_half_out(s, j)

                join(c, settle=False)
                join(c + 1, between, scale_first, settle=False)
                gu_lora_low(s, j)
                dve.wait_ge(joined, DQ * (c + 2))
                gu_scale(gu_slot(s) + 1)

            def gu_lora_mid():
                mid = slice(RG, 2 * RG)
                for tg in range(TG):
                    cols = slice(tg * 512, (tg + 1) * 512)
                    dve.wait_ge(t_hi, tg + 1)
                    nc.vector.tensor_tensor(th[mid, cols], bank[2 + tg][mid, :], f32(th[mid, cols]), ALU.subtract).then_inc(t_ready, 1)

            for n in range(L1_FIRST):
                down_chunk(PLAN_END[3] + n)
            for b in range(NT + 1):
                if b < NT:
                    s = b % 2
                    dve.wait_ge(x1_ps, b + 1)
                    dve.wait_ge(ln_done, 3 * NT)
                    if b >= 2:
                        dve.wait_ge(xt_ps, 3 * NT + b - 1)
                    nc.vector.tensor_tensor(rbuf[:, s, :], x[:, b, :], bank[s][:, :], ALU.add).then_inc(x1_ready, 1)
                if b >= 1:
                    x_low(3 * NT + b - 1)
                c = PLAN_END[3] + L1_FIRST + b
                if c < C_GU:
                    down_chunk(c)
                elif c == C_GU:
                    gu_first_half(0, 0)
                elif c == C_GU + 1:
                    gu_second_half(0, 0)
                elif c == C_GU + 2:
                    gu_low(0, 1, 1)
                    gu_lora_low(0, 0)
                if b == GU1_STEP:
                    dve.wait_ge(w_ready, 2)
                    gu_first_half(1, 1)
                elif b == NT:
                    gu_second_half(1, 1, gu_lora_mid)
                if b < NT:
                    dve.wait_ge(x1_ready, b + 1)
                    nc.vector.tensor_tensor(x[:, b, :], x[:, b, :], rbuf[:, s, :], ALU.add).then_inc(x1_sum, 1)
                for j in range(2 * b, min(2 * b + 2, NF)):
                    dve.wait_ge(fold_ready, j + 1)
                    dve.wait_ge(scaled, C_DN + j + 1)
                    nc.vector.tensor_tensor(fold[:, j, :], fold[:, j, :], bank[4 + j % 2][:, :], ALU.add).then_inc(fold_kept, 1)

            gu_low(1, 3, 1)
            gu_lora_low(1, 1)
            with dve.Fori(1, NF // 2) as n:
                for s in range(2):
                    j = 2 * n + s
                    gu_weights(s, j)
                    hidden(s, j - 2, (1,))
                    gu_low(s, 2 * j + 1, 1)
            hidden(0, NF - 2)
            hidden(1, NF - 1, (0,))

            def hidden_low(half, s, j):
                cols = slice(half * 512, (half + 1) * 512)
                return nc.vector.tensor_tensor(xl[:, s, cols], hT[:, bass.ds(j, 1), cols].rearrange("p o t -> p (o t)"),
                                               f32(xh[:, s, cols]), ALU.subtract)

            def x2_sum(b):
                dve.wait_ge(d_ps, b + 1)
                nc.vector.tensor_tensor(x[:, b, :], x[:, b, :], bank[b][:, :], ALU.add).then_inc(ln_sum, 1)

            def stats_of(m):
                b, s = m % NT, m % 2
                dve.wait_ge(ln_sum, m + 1)
                dve.wait_ge(ln_done, m - 1)
                link(nc.vector.bn_stats(st[:, s, :], x[:, b, :]))
                nc.vector.bn_aggr(mv[:, s, :], st[:, s, :]).then_inc(ln_stats, 1)

            def norm_of(m):
                b, s = m % NT, m % 2
                dve.wait_ge(ln_rstd, m + 1)
                nc.vector.tensor_scalar(x[:, b, :], x[:, b, :], mv[:, s, 0:1], rstd[:, s, 1:2],
                                        ALU.subtract, ALU.mult).then_inc(ln_done, 1)

            def x2_stats(b):
                stats_of(3 * NT + b)

            def x2_norm(b):
                norm_of(3 * NT + b)

            def dn_low_parts(half, s, j):
                dve.wait_ge(dn_hi, 2 * NF * half + 2 * j + 1)
                hidden_low(half, s, j)
                dve.wait_ge(dn_hi, 2 * NF * half + 2 * j + 2)
                nc.vector.tensor_tensor(wl[:, s, 0:D], fold[:, bass.ds(j, 1), :].rearrange("p o c -> p (o c)"),
                                        f32(wh[:, s, 0:D]), ALU.subtract).then_inc(dn_ready, 1)

            def down_low(parts, first, second):
                parts(0, 1, 1)
                with dve.Fori(1, NF // 2) as n:
                    for s in range(2):
                        parts(0, s, 2 * n + s)
                for n in range(NF // 2):
                    parts(1, 0, 2 * n)
                    pair, step = divmod(n, 3)
                    if step and pair < NT // 4:
                        first(2 * pair + step - 1)
                    elif pair and not step:
                        second(2 * pair - 2)
                    parts(1, 1, 2 * n + 1)
                    if pair and not step:
                        second(2 * pair - 1)

            def x2_first(b):
                if b == 0:
                    dve.wait_ge(x1_sum, NT)
                x2_sum(b)
                x2_stats(b)

            dn_low_parts(0, 0, 0)
            hidden(1, NF - 1, (1,))
            down_low(dn_low_parts, x2_first, x2_norm)

            def x_max_of(b):
                s = b % 2
                dve.wait_ge(x_ps, b + 1)
                link(nc.vector.tensor_reduce(x_small(b, 2), bank[2 + s][:, 0:P], AX.X, ALU.max))
                nc.vector.tensor_scalar(x_small(b, 0), x_small(b, 2), -float(D) ** -0.5, None, ALU.mult).then_inc(x_max, 1)

            for b in range(NT // 2, NT):
                x2_sum(b)
            for t in range(2):
                x_max_of(t)
                pair = (NT // 2 + 2 * t, NT // 2 + 2 * t + 1)
                for b in pair:
                    x2_stats(b)
                for b in pair:
                    x2_norm(b)
            for t in range(2, NT + 4):
                if t < NT:
                    x_max_of(t)
                if t - 2 < NT:
                    b = t - 2
                    dve.wait_ge(xo_ps, b + 1)
                    link(nc.vector.reciprocal(x_small(b, 3), x_small(b, 1)))
                    nc.vector.scalar_tensor_tensor(x[:, b, :], bank[5 + b % 2][:, :], x_small(b, 3), x[:, b, :],
                                                   ALU.mult, ALU.add).then_inc(ln_sum, 1)
                if 3 <= t < NT + 3:
                    norm_of(4 * NT + t - 3)
                if t >= 4:
                    x_low(4 * NT + t - 4, X3_BANK[t % 2])
                if t - 2 < NT:
                    stats_of(4 * NT + t - 2)

            def t_hidden(s, j, groups=range(TG)):
                for tg in groups:
                    dve.wait_ge(t_sil, 2 * j + tg + 1)
                    dve.wait_ge(t_up_ps, 2 * j + tg + 1)
                    h = hT[:, bass.ds(j, 1), tg * 512:(tg + 1) * 512].rearrange("p o t -> p (o t)")
                    nc.vector.scalar_tensor_tensor(h, up_bank(s, tg), ff_s[:, s, 1:2], h, ALU.mult, ALU.mult).then_inc(t_h, 1)

            with dve.Fori(0, NF // 2 - 1) as n:
                for s in range(2):
                    t_hidden(s, 2 * n + s)
            t_hidden(0, NF - 2)
            t_hidden(1, NF - 1, (0,))

            def t_low_part(half, s, j):
                dve.wait_ge(t_dhi, NF * half + j + 1)
                hidden_low(half, s, j).then_inc(t_dlo, 1)

            def last_first(b):
                m = 5 * NT + b
                if b == 0:
                    dve.wait_ge(in_ds, 16)
                dve.wait_ge(t_d_ps, b + 1)
                link(nc.vector.tensor_tensor(rbuf[:, b % 2, :], bank[b][:, :], ds[:, :], ALU.mult))
                nc.vector.tensor_tensor(x[:, b, :], x[:, b, :], rbuf[:, b % 2, :], ALU.add).then_inc(ln_sum, 1)
                stats_of(m)

            def last_norm(b):
                norm_of(5 * NT + b)

            t_low_part(0, 0, 0)
            t_hidden(1, NF - 1, (1,))
            down_low(t_low_part, last_first, last_norm)
            for b in range(NT // 2, NT):
                last_first(b)


def layout(a):
    c = np.ascontiguousarray
    f = {k: np.asarray(v) for k, v in a.items()}

    def rows(m, n=P):
        return c(m.reshape(-1, n, m.shape[-1]).transpose(1, 0, 2))

    x2, ctx2 = f["x"].reshape(T, D), f["ctx_4096"].reshape(T, D)
    wqk = f["L0_attn_Wqk_w"].reshape(HA, 2, D)
    qkv = np.concatenate([wqk[:, 0], wqk[:, 1], f["L0_attn_Wv_w"]])
    heads = np.arange(HEADS)
    head_m = np.concatenate([np.repeat(heads, HD), heads])[:, None] == heads
    ca, sa = f["L1_attn_codes_attn"], f["L1_attn_scales_attn"]

    def wide(g, u):
        m = np.stack([g, u]).reshape(2, NF, P, KD, P)
        return c(m.transpose(1, 4, 3, 0, 2).reshape(NF, P, KD * 2 * P))

    sgu = f["L1_attn_scales_gu"].reshape(2, NF, P, KD, 2)
    A, Ba, Bgu = f["L1_attn_lora_A_h"], f["L1_attn_lora_B_attn"], f["L1_attn_lora_B_gu"]
    lora_l, lora_r = np.zeros((O_ROW + R1, D), np.float32), np.zeros((O_ROW + R1, D), np.float32)
    lora_l[:3 * R1], lora_r[:3 * R1] = Ba[:3].transpose(0, 2, 1).reshape(3 * R1, D), A[:3].reshape(3 * R1, D)
    lora_l[O_ROW:], lora_r[O_ROW:] = A[3], Ba[3].T
    b_gu = np.zeros((NF, 3, 2, R1, 2, P), np.float32)
    for g in range(2):
        b_gu[:, :, g, :, g, :] = Bgu[g].reshape(NF, 1, P, R1).transpose(0, 1, 3, 2)
    b_gu = b_gu.reshape(NF, 3 * RG, 2 * P)
    a_d, bT_d = np.zeros((DQ_ROWS, DT * P), np.float32), np.zeros((DQ_ROWS, D), np.float32)
    for n in range(3):
        part = f["L1_attn_lora_A_down"][:, n * DT * P:(n + 1) * DT * P]
        a_d[n * QR:n * QR + R1, :part.shape[1]] = part
        bT_d[n * QR:n * QR + R1] = f["L1_attn_lora_B_down"].T
    return {
        "x": rows(x2), "xT": rows(c(x2.T)), "ctx": rows(ctx2), "ctxT": rows(c(ctx2.T)),
        "qkvT": rows(c(qkv.T)), "qk_b": f["L0_attn_Wqk_b"].reshape(HA, 2), "v_b": f["L0_attn_Wv_b"][None],
        "head_m": head_m.astype(np.float32),
        "wo0": np.concatenate([f["L0_attn_Wo_w"].T, f["L0_attn_Wo_b"][None]]),
        "w0T": rows(c(f["L0_ffn_W"].T)), "agT": rows(np.concatenate([f["L0_ffn_A"].T, f["L0_ffn_gate_w"].T], 1)),
        "bT0": np.concatenate([f["L0_ffn_B"].T, f["L0_ffn_b"][None]]), "g_b": f["L0_ffn_gate_b"][None],
        "c_qkv": c(ca[:3].reshape(3 * KD, P, D)), "c_o": c(ca[3].T.reshape(KD, P, D)),
        "s_qkv": c(sa[:3].reshape(3, KD, P, NB).transpose(2, 0, 1, 3).reshape(P, -1)),
        "s_o": c(sa[3].T.reshape(KD, 2, D)), "lora_l": lora_l, "lora_r": lora_r,
        "aT_gu": rows(np.tile(A[4:6].reshape(RG, D).T, 3)), "b_gu": b_gu, "a_d": a_d, "bT_d": bT_d,
        "c_gu": wide(f["L1_attn_codes_gu"][0], f["L1_attn_codes_gu"][1]),
        "s_gu": c(sgu.transpose(1, 4, 3, 0, 2).reshape(NF, 2, 2 * CH)),
        "c_dn": c(f["L1_attn_codes_down"].T.reshape(NF, P, D)), "s_dn": c(f["L1_attn_scales_down"].T.reshape(NF, 2, D)),
        "wk1": f["L1_xattn_Wk"].reshape(KD, P, D), "wq1": rows(f["L1_xattn_Wq"]),
        "q_b": c(f["L1_xattn_bq"].reshape(KD, P).T), "k_b": c(f["L1_xattn_bk"].reshape(KD, P).T),
        "t_gu": wide(f["L1_ffn_gate_t"], f["L1_ffn_up_t"]),
        "ts_gu": c(np.stack([f["L1_ffn_gate_s"], f["L1_ffn_up_s"]], 1).reshape(NF, P, 2)),
        "t_dn": rows(c(f["L1_ffn_down_t"].T)), "ds": f["L1_ffn_down_s"][None],
    }


def kernel(**inputs):
    import concourse.bacc as bacc
    from concourse.bass_utils import run_bass_kernel_spmd

    nc = bacc.Bacc("TRN2", target_bir_lowering=False, num_devices=1)
    arrays, aps = {}, {}
    for name, a in layout(inputs).items():
        arrays[f"in_{name}"] = a
        aps[name] = nc.dram_tensor(f"in_{name}", a.shape, mybir.dt.from_np(a.dtype), kind="ExternalInput").ap()
    out = nc.dram_tensor("out", (NT, P, D), F32, kind="ExternalOutput").ap()
    decoder_kernel(nc, aps, out)
    r = run_bass_kernel_spmd(nc, [arrays], core_ids=[0])
    return r.results[0]["out"]
```
